# Optimizing a Trainium2 kernel written in Bass

```python
import numpy as np
import jax
import jax.numpy as jnp

def _softmax(x, axis=-1):
    return jax.nn.softmax(x, axis=axis)

def _gelu(x):
    return jax.nn.gelu(x, approximate=True)

def _silu(x):
    return jax.nn.silu(x)

def _sigmoid(x):
    return jax.nn.sigmoid(x)

def _layernorm(x, axis=-1, eps=1e-05):
    m = jnp.mean(x, axis=axis, keepdims=True)
    v = jnp.var(x, axis=axis, keepdims=True)
    return (x - m) / jnp.sqrt(v + eps)

def _scatter_add(tgt, idx, src, axis=0):
    return tgt.at[idx].add(src)

def _segment_sum(src, seg, n):
    return jax.ops.segment_sum(src, seg, n)
kernel_name = 'mk_gnn_preln_d2_gnn_r8_43699c'

def setup_inputs(seed: int=0):
    np.random.seed(seed)
    _w = jnp.asarray

    def _rec_inputs():
        import jax
        import jax.numpy as jnp
        _gk = jax.random.key(seed)
        x = -0.000202 + 1 * jax.random.normal(jax.random.fold_in(_gk, 1), (6250, 128), jnp.float32)
        _s = jax.random.randint(jax.random.fold_in(_gk, 2), (100000,), 0, 6250, jnp.int32)
        _d = jax.random.randint(jax.random.fold_in(_gk, 3), (100000,), 0, 6250, jnp.int32)
        _loop = jnp.arange(6250, dtype=jnp.int32)
        src = jnp.concatenate([_s, _d, _loop])
        dst = jnp.concatenate([_d, _s, _loop])
        _o = jnp.argsort(dst, stable=True)
        src = src[_o]
        dst = dst[_o]
        edge_attr_70 = 0.000111316 + 1.00009 * jax.random.normal(jax.random.fold_in(_gk, 11), (206250, 70), jnp.float32)
        return (x, src, dst, edge_attr_70)
    x, src, dst, edge_attr_70 = _rec_inputs()

    def _L0_gnn_setup():
        import jax, jax.numpy as jnp
        import numpy as np
        N_NODES = 6250
        IN_C = 128
        OUT_C = 128
        EDGE_F = 65
        N_EDGES = 100000
        EDGE_ATTR_COLS = 70
        key = jax.random.key(seed)
        ks = jax.random.split(key, 10)
        fcat = 3 * IN_C + EDGE_F
        sc = lambda d: 1.0 / np.sqrt(d)
        return {'x': jax.random.normal(ks[0], (N_NODES, IN_C), dtype=jnp.float32), 'edge_index': jax.random.randint(ks[1], (2, N_EDGES), 0, N_NODES, dtype=jnp.int32), 'edge_attr': jax.random.normal(ks[2], (N_EDGES, EDGE_ATTR_COLS), dtype=jnp.float32), 'Wf': jax.random.normal(ks[3], (fcat, IN_C), dtype=jnp.float32) * sc(fcat), 'bf': jnp.zeros((IN_C,), dtype=jnp.float32), 'Wq': jax.random.normal(ks[4], (IN_C, IN_C), dtype=jnp.float32) * sc(IN_C), 'Wk': jax.random.normal(ks[5], (IN_C, IN_C), dtype=jnp.float32) * sc(IN_C), 'Wa': jax.random.normal(ks[6], (IN_C, 1), dtype=jnp.float32) * sc(IN_C), 'Wu': jax.random.normal(ks[7], (IN_C, OUT_C), dtype=jnp.float32) * sc(IN_C), 'bu': jnp.zeros((OUT_C,), dtype=jnp.float32)}
    _L0_gnn_all = _L0_gnn_setup()
    _L0_gnn_in = {k: v for k, v in _L0_gnn_all.items() if k in ('Wf', 'bf', 'Wq', 'Wk', 'Wa', 'Wu', 'bu')}
    del _L0_gnn_all

    def _L1_gnn_setup():
        import jax, jax.numpy as jnp
        import numpy as np
        N_NODES = 6250
        N_EDGES = 100000
        IN_CH = 128
        OUT_CH = 128
        MLP_HID = 64
        key = jax.random.key(seed)
        ks = jax.random.split(key, 8)
        x = jax.random.normal(ks[0], (N_NODES, IN_CH), dtype=jnp.float32)
        edge_index = jax.random.randint(ks[1], (2, N_EDGES), 0, N_NODES, dtype=jnp.int64)
        s1 = 1.0 / np.sqrt(2 * IN_CH)
        mlp_w1 = jax.random.uniform(ks[2], (2 * IN_CH, MLP_HID), jnp.float32, -s1, s1)
        mlp_b1 = jax.random.uniform(ks[3], (MLP_HID,), jnp.float32, -s1, s1)
        s2 = 1.0 / np.sqrt(MLP_HID)
        mlp_w2 = jax.random.uniform(ks[4], (MLP_HID, 1), jnp.float32, -s2, s2)
        mlp_b2 = jax.random.uniform(ks[5], (1,), jnp.float32, -s2, s2)
        s3 = 1.0 / np.sqrt(IN_CH)
        conv_w = jax.random.uniform(ks[6], (IN_CH, OUT_CH), jnp.float32, -s3, s3)
        conv_b = jnp.zeros((OUT_CH,), jnp.float32)
        return {'x': x, 'edge_index': edge_index, 'mlp_w1': mlp_w1, 'mlp_b1': mlp_b1, 'mlp_w2': mlp_w2, 'mlp_b2': mlp_b2, 'conv_w': conv_w, 'conv_b': conv_b}
    _L1_gnn_all = _L1_gnn_setup()
    _L1_gnn_in = {k: v for k, v in _L1_gnn_all.items() if k in ('mlp_w1', 'mlp_b1', 'mlp_w2', 'mlp_b2', 'conv_w', 'conv_b')}
    del _L1_gnn_all
    return {'x': x, 'src': src, 'dst': dst, 'edge_attr_70': edge_attr_70, 'L0_gnn_Wf': _L0_gnn_in['Wf'], 'L0_gnn_bf': _L0_gnn_in['bf'], 'L0_gnn_Wq': _L0_gnn_in['Wq'], 'L0_gnn_Wk': _L0_gnn_in['Wk'], 'L0_gnn_Wa': _L0_gnn_in['Wa'], 'L0_gnn_Wu': _L0_gnn_in['Wu'], 'L0_gnn_bu': _L0_gnn_in['bu'], 'L1_gnn_mlp_w1': _L1_gnn_in['mlp_w1'], 'L1_gnn_mlp_b1': _L1_gnn_in['mlp_b1'], 'L1_gnn_mlp_w2': _L1_gnn_in['mlp_w2'], 'L1_gnn_mlp_b2': _L1_gnn_in['mlp_b2'], 'L1_gnn_conv_w': _L1_gnn_in['conv_w'], 'L1_gnn_conv_b': _L1_gnn_in['conv_b']}

def reference(x, src, dst, edge_attr_70, L0_gnn_Wf, L0_gnn_bf, L0_gnn_Wq, L0_gnn_Wk, L0_gnn_Wa, L0_gnn_Wu, L0_gnn_bu, L1_gnn_mlp_w1, L1_gnn_mlp_b1, L1_gnn_mlp_w2, L1_gnn_mlp_b2, L1_gnn_conv_w, L1_gnn_conv_b):
    import jax
    import jax.numpy as jnp

    def _L0_gnn_ref(x, edge_index, edge_attr, Wf, bf, Wq, Wk, Wa, Wu, bu):
        import jax, jax.numpy as jnp
        import numpy as np
        N_NODES = 6250
        IN_C = 128
        OUT_C = 128
        EDGE_F = 65
        N_EDGES = 100000
        EDGE_ATTR_COLS = 70
        src = edge_index[0]
        tgt = edge_index[1]
        ni = x[src]
        nj = x[tgt]
        mask = (edge_attr[:, 0:1] < 8).astype(x.dtype)
        fcat = jnp.concatenate([ni, nj, ni - nj, edge_attr[:, :EDGE_F]], axis=1)
        f = jax.nn.elu(fcat @ Wf + bf) * mask
        scale = IN_C ** (-0.5)
        q = ni @ Wq
        k = f @ Wk
        a = jnp.tanh(q * k * scale @ Wa)
        numerator = jnp.exp(a)
        a_sum = jax.ops.segment_sum(a, src, num_segments=N_NODES)
        denominator = jnp.exp(a_sum)[src]
        s = numerator / denominator
        z = s * f
        aggr = jax.ops.segment_sum(z, src, num_segments=N_NODES)
        return (x + aggr) @ Wu + bu

    def _L1_gnn_ref(x, edge_index, mlp_w1, mlp_b1, mlp_w2, mlp_b2, conv_w, conv_b):
        import jax, jax.numpy as jnp
        import numpy as np
        N_NODES = 6250
        N_EDGES = 100000
        IN_CH = 128
        OUT_CH = 128
        MLP_HID = 64
        n = x.shape[0]
        row, col = (edge_index[0], edge_index[1])
        edge_feat = jnp.concatenate([x[row], x[col]], axis=-1)
        h = jax.nn.gelu(edge_feat @ mlp_w1 + mlp_b1, approximate=False)
        edge_weight = jax.nn.sigmoid(h @ mlp_w2 + mlp_b2)[:, 0]
        loop = jnp.arange(n, dtype=row.dtype)
        row_f = jnp.concatenate([row, loop])
        col_f = jnp.concatenate([col, loop])
        ew_f = jnp.concatenate([edge_weight, jnp.ones((n,), x.dtype)])
        deg = jax.ops.segment_sum(ew_f, col_f, num_segments=n)
        dinv = jnp.where(deg > 0, jax.lax.rsqrt(deg), 0.0)
        norm = dinv[row_f] * ew_f * dinv[col_f]
        xt = x @ conv_w
        msg = xt[row_f] * norm[:, None]
        out = jax.ops.segment_sum(msg, col_f, num_segments=n)
        return out + conv_b
    edge_index = jnp.stack([src, dst])
    h = jnp.maximum(_layernorm(x, axis=-1), 0.0)
    x = x + _L0_gnn_ref(h, edge_index, edge_attr_70, L0_gnn_Wf, L0_gnn_bf, L0_gnn_Wq, L0_gnn_Wk, L0_gnn_Wa, L0_gnn_Wu, L0_gnn_bu)
    h = jnp.maximum(_layernorm(x, axis=-1), 0.0)
    x = x + _L1_gnn_ref(h, edge_index, L1_gnn_mlp_w1, L1_gnn_mlp_b1, L1_gnn_mlp_w2, L1_gnn_mlp_b2, L1_gnn_conv_w, L1_gnn_conv_b)
    return x

_drawn_inputs = setup_inputs


def setup_inputs(seed=0):
    import zlib

    import numpy as np

    out = dict(_drawn_inputs(seed))
    spreads = {'L0_gnn_bf': (0.0, 0.1), 'L0_gnn_bu': (0.0, 2.0), 'L1_gnn_conv_b': (0.0, 2.0)}
    factors = {'L1_gnn_mlp_w1': 23.315,
     'L1_gnn_mlp_b1': 200.0,
     'L1_gnn_mlp_w2': 67.12,
     'L1_gnn_conv_w': 8.0}
    for name, (base, spread) in spreads.items():
        noise = np.random.default_rng([zlib.crc32(name.encode()), seed]).standard_normal(out[name].shape)
        drawn = base * np.exp(spread * noise) if base else spread * noise
        out[name] = jnp.asarray(drawn.astype(out[name].dtype))
    for name, factor in factors.items():
        out[name] = (out[name] * factor).astype(out[name].dtype)
    return out
```

```python
import numpy as np
from contextlib import ExitStack

import concourse.bass as bass
from concourse import mybir

f32 = mybir.dt.float32
bf16 = mybir.dt.bfloat16
i32 = mybir.dt.int32
ALU = mybir.AluOpType
ACT = mybir.ActivationFunctionType
AX = mybir.AxisListType

P = 128
G = 4
U = 2
AHEAD = 3
UB = 4
FAR = 1 << 20
EPS = 1e-5

SRC_LO, DST_LO, DST_HI, DST, DROW = 65, 66, 67, 68, 69
META = 5


class Plan:

    def __init__(self, n_nodes, n_edges, d, attr, attr_used, hid):
        self.n, self.e, self.d, self.attr, self.ef, self.hid = n_nodes, n_edges, d, attr, attr_used, hid
        self.nb = -(-n_nodes // P)
        self.tail = n_nodes - (self.nb - 1) * P
        self.full = n_edges // P
        self.rest = n_edges - self.full * P
        self.prep_loops = self.full // (G * U)
        self.peeled = self.full - self.prep_loops * G * U
        assert self.rest and self.peeled < G
        self.cols = self.prep_loops * G * U + G
        tiles = (n_edges + self.nb * (P - 1)) // P
        self.tiles = -(-tiles // P) * P
        self.loops = self.tiles // (G * UB)
        self.groups = self.loops * UB
        self.rows = self.tiles * P


def gnn(nc, x, src, dst, edge_attr, Wf, bf, Wq, Wk, Wa, Wu, bu, w1, b1, w2, b2, conv_w, conv_b, out):
    n_nodes, d = x.shape
    n_edges, attr = edge_attr.shape
    pl = Plan(n_nodes, n_edges, d, attr, Wf.shape[0] - 3 * d, w1.shape[1])
    nb, hid, ef = pl.nb, pl.hid, pl.ef
    assert d == P and ef == SRC_LO and attr == ef + META

    c = Shared()
    c.nc, c.pl, c.nb, c.d, c.hid, c.ef, c.attr = nc, pl, nb, d, hid, ef, attr
    c.x, c.src, c.dst, c.edge_attr, c.out = x, src, dst, edge_attr, out
    c.Wf, c.bf, c.Wq, c.Wk, c.Wa, c.Wu, c.bu = Wf, bf, Wq, Wk, Wa, Wu, bu
    c.w1, c.b1, c.w2, c.b2, c.conv_w, c.conv_b = w1, b1, w2, b2, conv_w, conv_b
    c.LAST = nb - 1
    c.AGW = AGW = 2 * d
    c.X_AT = nb * 3 * hid
    c.ZW = ZW = d + 1

    c.rows_s = nc.dram_tensor("rows_by_source", [pl.rows + AHEAD * G * P, attr], f32).ap()
    c.rows_d = nc.dram_tensor("messages_by_target", [pl.rows, ZW], f32).ap()
    c.tab_b = nc.dram_tensor("table_b", [nb * P, d], f32).ap()
    c.tab_q = nc.dram_tensor("table_q", [nb * P, hid], f32).ap()
    c.blk_dram = nc.dram_tensor("block_of_tile", [2, pl.tiles], i32).ap()

    ctx = ExitStack()
    with ctx:
        def sb(name, shape, dt=f32):
            return ctx.enter_context(nc.sbuf_tensor(name, shape, dt))

        c.iota_i = sb("iota_i", [P, P], i32)
        c.part_i = sb("part_i", [P, 1], i32)
        c.tile_i = sb("tile_i", [P, pl.tiles // P], i32)
        c.iota = sb("iota", [P, P])
        c.iota_b = sb("iota_b", [P, P], bf16)
        c.part = sb("part", [P, 1])
        c.ident = sb("ident", [P, P])
        c.ident_b = sb("ident_b", [P, P], bf16)
        c.earlier_b = sb("earlier_b", [P, P], bf16)
        c.ones = sb("ones", [P, P])
        c.ones_b = sb("ones_b", [P, P], bf16)
        c.zeros = sb("zeros", [P, P])
        c.eps_t = sb("eps_t", [P, 1])

        c.wf = sb("wf", [P, 3, d])
        c.w4 = sb("w4", [ef, d])
        c.wq = sb("wq", [P, d])
        c.wk = sb("wk", [P, d])
        c.wa = sb("wa", [P, 1])
        c.wu = sb("wu", [P, d])
        c.wqkT = sb("wqkT", [P, 2, P])
        c.wnode = sb("wnode", [P, 3 * d])
        c.wnode1 = sb("wnode1", [P, 2 * hid + d])
        c.bias_f = sb("bias_f", [P, d])
        c.bias_u = sb("bias_u", [P, d])
        c.bias_1 = sb("bias_1", [P, hid])
        c.bias_c = sb("bias_c", [P, d])
        c.w2_row = sb("w2_row", [P, hid])
        c.b2_col = sb("b2_col", [P, 1])

        c.blk = sb("blk", [1, 2, (1 + AHEAD) * G + pl.tiles], i32)

        setup_phase(nc, c)
        sort_phase(nc, c)

        c.hn = sb("hn", [P, nb, d])
        c.acc = sb("acc", [P, nb * ZW])
        c.acc3 = c.acc[:, :].rearrange("p (b w) -> p b w", w=ZW)
        c.accd = c.acc[:, 0:nb * d].rearrange("p (b w) -> p b w", w=d)
        c.stat = sb("stat", [P, 4, nb])
        c.dinv = sb("dinv", [P, nb])

        c.meta = sb("meta", [P, pl.tiles + AHEAD * G, 3], bf16)
        c.where = sb("where", [P, 2, pl.tiles + AHEAD * G], i32)
        with nc.sbuf_tensor("lut0", [P, nb * 3 * AGW], bf16) as c.lut:
            layer0_nodes(nc, c)
            layer0_edges(nc, c)
        c.lut = sb("lut1", [P, nb * 3 * (hid + d)], bf16)
        c.xn = sb("xn", [P, nb, d])
        c.ew = sb("ew", [P, pl.tiles])
        layer0_update(nc, c)
        weights_pass(nc, c)
        degree_pass(nc, c)
        message_pass(nc, c)
        target_pass(nc, c)
        finish(nc, c)


class Shared:
    pass


class Scope:

    def __init__(self, nc, tag):
        self.nc, self.tag, self.ctx = nc, tag, ExitStack()

    def __enter__(self):
        return self

    def __exit__(self, *error):
        self.ctx.close()

    def sb(self, name, shape, dt=f32):
        return self.ctx.enter_context(self.nc.sbuf_tensor(f"{self.tag}_{name}", shape, dt))

    def bank(self, name, banks=1, dt=f32):
        return self.ctx.enter_context(self.nc.psum_tensor(f"{self.tag}_{name}", [P, banks * 2048 // mybir.dt.size(dt)], dt))

    def sem(self, name):
        return self.ctx.enter_context(self.nc.semaphore(f"{self.tag}_{name}"))

    def sems(self, names):
        return [self.sem(n) for n in names.split()]


def setup_phase(nc, c):
    pl, nb, d, hid, ef, attr = c.pl, c.nb, c.d, c.hid, c.ef, c.attr
    FILL = 13
    with Scope(nc, "setup") as s:
        fill = s.sb("fill", [P, FILL * 4, attr])
        fill_d = s.sb("fill_d", [P, FILL, c.ZW])
        s_iota, s_const, s_fill, s_load, s_store, s_zero = s.sems(
            "s_iota s_const s_fill s_load s_store s_zero")

        with nc.Block() as block:
            @block.gpsimd
            def _(pool):
                nc.gpsimd.iota(c.iota_i[:, :], pattern=[[1, P]], base=0, channel_multiplier=0).then_inc(s_iota, 1)
                nc.gpsimd.iota(c.part_i[:, :], pattern=[[0, 1]], base=0, channel_multiplier=1).then_inc(s_iota, 1)
                nc.gpsimd.iota(c.tile_i[:, :], pattern=[[1, pl.tiles // P]], base=0,
                               channel_multiplier=pl.tiles // P).then_inc(s_iota, 1)

            @block.vector
            def _(dve):
                v = nc.vector
                v.memset(fill[:, :, :], 0.0).then_inc(s_zero, 1)
                v.memset(fill_d[:, :, :], 0.0).then_inc(s_zero, 1)
                dve.wait_ge(s_zero, 2)
                v.memset(fill[:, :, SRC_LO:DST_HI + 1], -1.0).then_inc(s_fill, 1)
                v.memset(fill[:, :, DROW:DROW + 1], float(FAR)).then_inc(s_fill, 1)
                v.memset(fill_d[:, :, d:d + 1], -1.0).then_inc(s_fill, 1)
                v.memset(c.ones[:, :], 1.0).then_inc(s_const, 1)
                v.memset(c.ones_b[:, :], 1.0).then_inc(s_const, 1)
                v.memset(c.zeros[:, :], 0.0).then_inc(s_const, 1)
                v.memset(c.eps_t[:, :], EPS).then_inc(s_const, 1)
                v.memset(c.blk[:, :, :], 0).then_inc(s_const, 1)
                dve.wait_ge(s_iota, 3)
                v.tensor_copy(c.iota[:, :], c.iota_i[:, :]).then_inc(s_const, 1)
                v.tensor_copy(c.iota_b[:, :], c.iota_i[:, :]).then_inc(s_const, 1)
                v.tensor_copy(c.part[:, :], c.part_i[:, :]).then_inc(s_const, 1)
                dve.wait_ge(s_const, 8)
                v.tensor_scalar(c.ident[:, :], c.iota[:, :], c.part[:, 0:1], None, ALU.is_equal).then_inc(s_const, 1)
                v.tensor_scalar(c.ident_b[:, :], c.iota[:, :], c.part[:, 0:1], None, ALU.is_equal).then_inc(s_const, 1)
                v.tensor_scalar(c.earlier_b[:, :], c.iota[:, :], c.part[:, 0:1], None, ALU.is_gt).then_inc(s_const, 1)
                dve.wait_ge(s_const, 11)

            @block.scalar
            def _(act):
                def row(ap, n):
                    return ap.rearrange("(a n) -> a n", a=1).to_broadcast([P, n])

                loads = [
                    (c.wf[:, :, :], c.Wf[0:3 * d, :].rearrange("(t p) n -> p t n", p=P)),
                    (c.w4[:, :], c.Wf[3 * d:3 * d + ef, :]),
                    (c.wq[:, :], c.Wq), (c.wk[:, :], c.Wk), (c.wa[:, :], c.Wa),
                    (c.wu[:, :], c.Wu),
                    (c.wnode1[:, 0:2 * hid].rearrange("p (t n) -> p t n", t=2), c.w1.rearrange("(t p) n -> p t n", p=P)),
                    (c.wnode1[:, 2 * hid:], c.conv_w),
                    (c.bias_f[:, :], row(c.bf, d)), (c.bias_u[:, :], row(c.bu, d)),
                    (c.bias_1[:, :], row(c.b1, hid)), (c.bias_c[:, :], row(c.conv_b, d)),
                    (c.w2_row[:, :], row(c.w2.rearrange("n a -> (n a)"), hid)),
                    (c.b2_col[:, :], row(c.b2, 1)),
                ]
                for dest, origin in loads:
                    act.dma_start(dest, origin).then_inc(s_load, 16)
                act.wait_ge(s_load, 16 * len(loads))

            @block.sync
            def _(sp):
                sp.wait_ge(s_fill, 3)
                n = 0
                per = pl.rows // P
                view = c.rows_s[0:pl.rows, :].rearrange("(p r) n -> p r n", p=P)
                for a in range(0, per, 4 * FILL):
                    sp.dma_start(view[:, a:min(a + 4 * FILL, per), :], fill[:, 0:min(4 * FILL, per - a), :]).then_inc(s_store, 16)
                    n += 1
                sp.dma_start(c.rows_s[pl.rows:, :].rearrange("(p r) n -> p r n", p=P), fill[:, 0:AHEAD * G, :]).then_inc(s_store, 16)
                n += 1
                view = c.rows_d.rearrange("(p r) n -> p r n", p=P)
                for a in range(0, per, FILL):
                    sp.dma_start(view[:, a:min(a + FILL, per), :], fill_d[:, 0:min(FILL, per - a), :]).then_inc(s_store, 16)
                    n += 1
                sp.wait_ge(s_store, 16 * n)


def sort_phase(nc, c):
    pl, nb, attr = c.pl, c.nb, c.attr
    C = pl.cols
    whole = pl.full * P
    with Scope(nc, "sort") as s:
        ends = s.sb("ends", [P, 2, C], i32)
        lo = s.sb("lo", [P, 4, C])
        src_hi = s.sb("src_hi", [P, C])
        half = s.sb("half", [P, C], i32)
        count = s.sb("count", [P, 2, nb])
        tot = s.sb("tot", [P, 2, nb])
        need_i = s.sb("need_i", [P, 2, nb], i32)
        need = s.sb("need", [P, 2, nb])
        upto = s.sb("upto", [P, 2, nb])
        run = s.sb("run", [P, 2, nb])
        NT = pl.tiles // P
        tile_f = s.sb("tile_f", [P, NT])
        cmp = s.sb("cmp", [P, 2, NT, nb])
        bot = s.sb("bot", [P, 2, NT])
        bot_i = s.sb("bot_i", [P, 2, NT], i32)
        junk = s.sb("junk", [P, C], bf16)
        hot = s.sb("hot", [P, U, 2, G * nb], bf16)
        rank = s.sb("rank", [P, U, 2, G, nb])
        row_f = s.sb("row_f", [P, U, 2, G])
        row_a = s.sb("row_a", [P, U, 2, G], i32)
        row_b = s.sb("row_b", [P, U, 2, G], i32)
        row_c = s.sb("row_c", [P, U, 2, G], i32)
        row_e = s.sb("row_e", [P, U, 2, G], i32)
        row_i = s.sb("row_i", [P, U, 2, G], i32)
        edge = s.sb("edge", [P, U, G, attr])
        pre = [s.bank(f"pre{u}")[:, 0:2 * G * nb].rearrange("p (k n) -> p k n", k=2) for u in range(U)]
        add = [s.bank(f"add{u}")[:, 0:2 * nb].rearrange("p (k n) -> p k n", k=2) for u in range(U)]

        (s_ends, s_pad, s_key, s_cnt, s_tot, s_base, s_bot, s_blkw, s_blkr) = s.sems(
            "s_ends s_pad s_key s_cnt s_tot s_base s_bot s_blkw s_blkr")

        with nc.Block() as block:
            @block.sync
            def _(sp):
                sp.wait_ge(s_pad, 1)
                for k, key in enumerate((c.src, c.dst)):
                    sp.dma_start(ends[:, k, 0:pl.full], key[0:whole].rearrange("(p r) -> p r", p=P)).then_inc(s_ends, 16)
                    sp.dma_start(ends[0:pl.rest, k, pl.full:pl.full + 1],
                                 key[whole:].rearrange("(p r) -> p r", r=1)).then_inc(s_ends, 16)
                sp.wait_ge(s_bot, 1)
                for k in range(2):
                    sp.dma_start(c.blk_dram[k, :].rearrange("(p r) -> p r", p=P), bot_i[:, k, :]).then_inc(s_blkw, 16)
                sp.wait_ge(s_blkw, 32)
                sp.dma_start(c.blk[0:1, :, G:G + pl.tiles], c.blk_dram.rearrange("(a k) r -> a k r", a=1)).then_inc(s_blkr, 16)
                sp.wait_ge(s_blkr, 16)

            @block.vector
            def _(dve):
                v = nc.vector
                v.memset(ends[:, :, :], nb * P).then_inc(s_pad, 1)
                v.memset(edge[:, :, :, :], 0.0).then_inc(s_pad, 1)
                dve.wait_ge(s_ends, 64)
                n = 0
                for k in range(2):
                    v.tensor_scalar(half[:, :], ends[:, k, :], 7, None, ALU.logical_shift_right).then_inc(s_key, 1)
                    n += 1
                    dve.wait_ge(s_key, n)
                    v.tensor_copy(src_hi[:, :] if k == 0 else lo[:, 2, :], half[:, :]).then_inc(s_key, 1)
                    n += 1
                    dve.wait_ge(s_key, n)
                    v.tensor_scalar(half[:, :], ends[:, k, :], P - 1, None, ALU.bitwise_and).then_inc(s_key, 1)
                    n += 1
                    dve.wait_ge(s_key, n)
                    v.tensor_copy(lo[:, k, :], half[:, :]).then_inc(s_key, 1)
                    n += 1
                    dve.wait_ge(s_key, n)
                v.tensor_copy(lo[:, 3, :], ends[:, 1, :]).then_inc(s_key, 1)
                m = 0
                with dve.Fori(0, nb) as b:
                    dve.wait_ge(s_cnt, b * 2)
                    v.tensor_scalar(junk[:, :], src_hi[:, :], c.iota[:, bass.ds(b, 1)], None, ALU.is_equal, ALU.add,
                                    accum_out=count[:, 0, bass.ds(b, 1)]).then_inc(s_cnt, 1)
                    dve.wait_ge(s_cnt, b * 2 + 1)
                    v.tensor_scalar(junk[:, :], lo[:, 2, :], c.iota[:, bass.ds(b, 1)], None, ALU.is_equal, ALU.add,
                                    accum_out=count[:, 1, bass.ds(b, 1)]).then_inc(s_cnt, 1)
                dve.wait_ge(s_tot, 1)
                n = 0

                def link(ins):
                    nonlocal n
                    n += 1
                    ins.then_inc(s_base, 1)
                    dve.wait_ge(s_base, n)

                link(v.tensor_scalar(tot[:, :, :], pre[0][:, :, 0:nb], float(P - 1), None, ALU.add))
                link(v.tensor_copy(need_i[:, :, :], tot[:, :, :]))
                link(v.tensor_scalar(need_i[:, :, :], need_i[:, :, :], 7, None, ALU.logical_shift_right))
                link(v.tensor_copy(need[:, :, :], need_i[:, :, :]))
                for k in range(2):
                    link(v.tensor_tensor_scan(upto[:, k, :], need[:, k, :], c.zeros[:, 0:nb], 0.0, ALU.add, ALU.add))
                link(v.tensor_tensor(run[:, :, :], upto[:, :, :], need[:, :, :], ALU.subtract))
                link(v.tensor_scalar(run[:, :, :], run[:, :, :], float(P), None, ALU.mult))
                link(v.tensor_copy(tile_f[:, :], c.tile_i[:, :]))
                for k in range(2):
                    link(v.tensor_tensor(cmp[:, k, :, :], tile_f[:, :].unsqueeze(2).to_broadcast([P, NT, nb]),
                                         upto[:, k, :].unsqueeze(1).to_broadcast([P, NT, nb]), ALU.is_ge))
                    link(v.tensor_reduce(bot[:, k, :], cmp[:, k, :, :], AX.X, ALU.add))
                link(v.tensor_scalar(bot[:, :, :], bot[:, :, :], float(nb - 1), None, ALU.min))
                v.tensor_copy(bot_i[:, :, :], bot[:, :, :]).then_inc(s_bot, 1)

            @block.tensor
            def _(pe):
                pe.wait_ge(s_cnt, 2 * nb)
                nc.tensor.matmul(pre[0][:, :, 0:nb], c.ones[:, :], count[:, :, :], start=True, stop=True).then_inc(s_tot, 1)

        (edge_free, edge_in0, edge_in1, edge_done0, edge_done1, hot_ready, prefix_ready, rank_a, rank_b, run_ready,
         row_cast, row_bits_b, row_bits_c, row_bits_e, row_ready, fields_ready, pool_step) = s.sems(
            "edge_free edge_in0 edge_in1 edge_done0 edge_done1 hot_ready prefix_ready rank_a rank_b run_ready "
            "row_cast row_bits_b row_bits_c row_bits_e row_ready fields_ready pool_step")
        edge_in, edge_done = (edge_in0, edge_in1), (edge_done0, edge_done1)
        groups = pl.prep_loops * U + 1

        with nc.Block() as block:
            def at(i, u, j=0, k=1):
                return bass.ds(i * (U * G) + (u * G + j), k)

            attr_v = c.edge_attr[0:whole, :].rearrange("(p r) n -> p (r n)", p=P)

            @block.sync
            def _(sp):
                with sp.Fori(0, pl.prep_loops) as i:
                    for u in range(U):
                        sp.wait_ge(edge_done[u], i * (16 * G))
                        sp.dma_start(edge[:, u, :, :].rearrange("p g n -> p (g n)"),
                                     attr_v[:, bass.ds(i * (U * G * attr) + u * G * attr, G * attr)]
                                     ).then_inc(edge_in[u], 16)
                L = pl.prep_loops
                sp.wait_ge(edge_done[0], L * 16 * G)
                sp.dma_start(edge[:, 0, 0:pl.peeled, :].rearrange("p g n -> p (g n)"),
                             attr_v[:, L * U * G * attr:]).then_inc(edge_in[0], 16)
                sp.dma_start(edge[0:pl.rest, 0, pl.peeled, :], c.edge_attr[whole:, :]).then_inc(edge_in[0], 16)
                sp.wait_ge(edge_in[0], L * 16 + 32)

            def one_hot(dve, i, u, g):
                if g is not None:
                    dve.wait_ge(prefix_ready, g(-1))
                hv = hot[:, u, :, :].rearrange("p k (g b) -> p k g b", b=nb)
                iota_v = c.iota[:, 0:nb].unsqueeze(1).to_broadcast([P, G, nb])
                nc.vector.tensor_tensor(hv[:, 0, :, :], src_hi[:, at(i, u, 0, G)].unsqueeze(2).to_broadcast([P, G, nb]),
                                        iota_v, ALU.is_equal)
                nc.vector.tensor_tensor(hv[:, 1, :, :], lo[:, 2, at(i, u, 0, G)].unsqueeze(2).to_broadcast([P, G, nb]),
                                        iota_v, ALU.is_equal).then_inc(hot_ready, 1)

            def rows(dve, i, u, g, last=False):
                v = nc.vector
                dve.wait_ge(prefix_ready, g(1))
                dve.wait_ge(run_ready, g(0))
                v.tensor_tensor(rank[:, u, :, :, :], pre[u][:, :, :].rearrange("p k (g b) -> p k g b", b=nb),
                                run[:, :, :].unsqueeze(2).to_broadcast([P, 2, G, nb]), ALU.add).then_inc(rank_a, 1)
                dve.wait_ge(rank_a, g(1))
                v.tensor_tensor(run[:, :, :], run[:, :, :], add[u][:, :, :], ALU.add).then_inc(run_ready, 1)
                v.tensor_tensor(rank[:, u, :, :, :].rearrange("p k g b -> p k (g b)"),
                                rank[:, u, :, :, :].rearrange("p k g b -> p k (g b)"), hot[:, u, :, :],
                                ALU.mult).then_inc(rank_b, 1)
                dve.wait_ge(rank_b, g(1))
                v.tensor_reduce(row_f[:, u, :, :], rank[:, u, :, :, :], AX.X, ALU.add).then_inc(row_cast, 1)
                dve.wait_ge(row_cast, g(0) * 2 + 1)
                if last:
                    v.tensor_scalar(rank[:, u, 0, 0, 0:1], src_hi[:, C - 1:C], float(nb), float(FAR),
                                    ALU.is_ge, ALU.mult).then_inc(rank_b, 1)
                    dve.wait_ge(rank_b, g(2))
                    v.tensor_tensor(row_f[:, u, 0, G - 1:G], row_f[:, u, 0, G - 1:G], rank[:, u, 0, 0, 0:1],
                                    ALU.add).then_inc(rank_b, 1)
                    dve.wait_ge(rank_b, g(3))
                v.tensor_copy(row_a[:, u, :, :], row_f[:, u, :, :]).then_inc(row_cast, 1)
                dve.wait_ge(row_cast, g(0) * 2 + 2)
                v.tensor_scalar(row_b[:, u, :, :], row_a[:, u, :, :], P - 1, 2, ALU.bitwise_and,
                                ALU.logical_shift_left).then_inc(row_bits_b, 1)
                v.tensor_scalar(row_c[:, u, :, :], row_a[:, u, :, :], 7, G - 1, ALU.logical_shift_right,
                                ALU.bitwise_and).then_inc(row_bits_c, 1)
                v.tensor_scalar(row_e[:, u, :, :], row_a[:, u, :, :], (FAR - 1) * 2 + 1 - (G * P - 1), None,
                                ALU.bitwise_and).then_inc(row_bits_e, 1)
                dve.wait_ge(row_bits_c, g(1))
                v.tensor_tensor(row_b[:, u, :, :], row_b[:, u, :, :], row_c[:, u, :, :], ALU.bitwise_or).then_inc(row_bits_b, 1)
                dve.wait_ge(row_bits_b, g(0) * 2 + 2)
                dve.wait_ge(edge_done[u], i * (16 * G))
                v.tensor_tensor(row_i[:, u, :, :], row_b[:, u, :, :], row_e[:, u, :, :], ALU.bitwise_or).then_inc(row_ready, 1)

            @block.vector
            def _(dve):
                one_hot(dve, 0, 0, None)
                with dve.Fori(0, pl.prep_loops) as i:
                    for u in range(U):
                        g = lambda k, i=i, u=u: i * U + (u + k)
                        one_hot(dve, i + (u + 1) // U, (u + 1) % U, lambda k, g=g: g(k + 1))
                        rows(dve, i, u, g)
                L = pl.prep_loops
                rows(dve, L, 0, lambda k: L * U + k, last=True)

            def prefix(pe, u, g):
                pe.wait_ge(hot_ready, g(1))
                pe.wait_ge(run_ready, g(0))
                t = nc.tensor
                t.matmul(pre[u][:, :, :], c.earlier_b[:, :], hot[:, u, :, :], start=True, stop=False)
                for k in range(1, G):
                    t.matmul(pre[u][:, :, k * nb:], c.ones_b[:, :], hot[:, u, :, 0:(G - k) * nb],
                             start=False, stop=(k == G - 1))
                for k in range(G):
                    last = t.matmul(add[u][:, :, :], c.ones_b[:, :], hot[:, u, :, k * nb:(k + 1) * nb],
                                    start=(k == 0), stop=(k == G - 1))
                last.then_inc(prefix_ready, 1)

            @block.tensor
            def _(pe):
                with pe.Fori(0, pl.prep_loops) as i:
                    for u in range(U):
                        prefix(pe, u, lambda k, i=i, u=u: i * U + (u + k))
                prefix(pe, 0, lambda k: pl.prep_loops * U + k)

            def fields(act, i, u, g, loaded):
                act.wait_ge(edge_in[u], loaded)
                nc.scalar.activation(edge[:, u, :, SRC_LO:DROW],
                                     lo[:, :, at(i, u, 0, G)].rearrange("p f g -> p g f"), ACT.Copy)
                act.wait_ge(row_ready, g(1))
                nc.scalar.activation(edge[:, u, :, DROW], row_i[:, u, 1, :], ACT.Copy).then_inc(fields_ready, 1)

            @block.scalar
            def _(act):
                with act.Fori(0, pl.prep_loops) as i:
                    for u in range(U):
                        fields(act, i, u, lambda k, i=i, u=u: i * U + (u + k), i * 16 + 16)
                L = pl.prep_loops
                fields(act, L, 0, lambda k: L * U + k, L * 16 + 32)

            @block.gpsimd
            def _(pool):
                limit = pool.to_reg(pl.rows - 1)

                def scatter(u, g):
                    pool.wait_ge(fields_ready, g(1))
                    pool.sem_inc(pool_step, 1)
                    for j in range(G):
                        nc.gpsimd.indirect_dma_start(
                            c.rows_s[0:pl.rows, :], bass.IndirectOffsetOnAxis(row_i[:, u, 0, j:j + 1], 0), edge[:, u, j, :], None,
                            bounds_check=limit, oob_is_err=False).then_inc(edge_done[u], 16)

                with pool.Fori(0, pl.prep_loops) as i:
                    for u in range(U):
                        scatter(u, lambda k, i=i, u=u: i * U + (u + k))
                L = pl.prep_loops
                scatter(0, lambda k: L * U + k)
                pool.wait_ge(edge_done[0], (L + 1) * 16 * G)
                pool.wait_ge(edge_done[1], L * 16 * G)


class At:

    def __init__(self, i, u):
        self.i, self.u = i, u

    def g(self, k=0):
        return self.i * UB + (self.u + k)

    def tiles(self, ahead=0):
        return bass.ds(self.i * (UB * G) + (self.u + ahead) * G, G)

    def tile(self, j, ahead=0):
        return bass.ds(self.i * (UB * G) + (self.u + ahead) * G + j, 1)

    def uses(self, slots, ahead=0, k=0):
        return self.i * (UB // slots) + ((self.u + ahead) // slots + 1 + k)


def split_bf16(dve, v, rest, parts, sem, n):
    v.tensor_copy(parts[0], rest).then_inc(sem, 1)
    dve.wait_ge(sem, n + 1)
    v.tensor_tensor(rest, rest, parts[0], ALU.subtract).then_inc(sem, 1)
    dve.wait_ge(sem, n + 2)
    v.tensor_copy(parts[1], rest).then_inc(sem, 1)
    dve.wait_ge(sem, n + 3)
    v.tensor_tensor(parts[2], rest, parts[1], ALU.subtract).then_inc(sem, 1)


def load_x(nc, c, tag, dest):
    whole = c.LAST * P
    with Scope(nc, f"load{tag}") as s:
        s_zero, s_x = s.sems("s_zero s_x")
        with nc.Block() as block:
            @block.vector
            def _(dve):
                nc.vector.memset(dest[:, c.LAST, :], 0.0).then_inc(s_zero, 1)

            @block.sync
            def _(sp):
                XB = 12
                x_v = c.x[0:whole, :].rearrange("(b p) n -> p b n", p=P)
                for b in range(0, c.LAST, XB):
                    sp.dma_start(dest[:, b:b + XB, :], x_v[:, b:b + XB, :]).then_inc(s_x, 16)
                sp.wait_ge(s_zero, 1)
                sp.dma_start(dest[0:c.pl.tail, c.LAST, :], c.x[whole:, :]).then_inc(s_x, 16)
                sp.wait_ge(s_x, 16 * (c.LAST // XB + 1))


def normalise(nc, c, tag, x):
    nb, d = c.nb, c.d
    with Scope(nc, f"norm{tag}") as s:
        s_step, s_var, s_std = s.sems("s_step s_var s_std")

        def wide(ap):
            return ap.unsqueeze(2).to_broadcast([P, nb, d])

        with nc.Block() as block:
            @block.vector
            def _(dve):
                v = nc.vector
                n = 0

                def link(ins):
                    nonlocal n
                    n += 1
                    ins.then_inc(s_step, 1)
                    dve.wait_ge(s_step, n)

                mean, var, rstd = c.stat[:, 0, :], c.stat[:, 1, :], c.stat[:, 2, :]
                link(v.tensor_reduce(mean, x, AX.X, ALU.add))
                link(v.tensor_scalar(mean, mean, 1.0 / d, None, ALU.mult))
                link(v.tensor_tensor(c.hn[:, :, :], x, wide(mean), ALU.subtract))
                link(v.tensor_tensor(c.accd, c.hn[:, :, :], c.hn[:, :, :], ALU.mult))
                v.tensor_reduce(var, c.accd, AX.X, ALU.add).then_inc(s_var, 1)
                dve.wait_ge(s_std, 1)
                link(v.reciprocal(rstd, var))
                v.scalar_tensor_tensor(c.hn[:, :, :], c.hn[:, :, :], 0.0, wide(rstd), ALU.max,
                                       ALU.mult).then_inc(s_step, 1)
                dve.wait_ge(s_step, n + 1)

            @block.scalar
            def _(act):
                var = c.stat[:, 1, :]
                act.wait_ge(s_var, 1)
                nc.scalar.activation(var, var, ACT.Sqrt, bias=c.eps_t[:, 0:1], scale=1.0 / d).then_inc(s_std, 1)


def project(nc, c, tag, weights, width, take_dve, take_act, store=None):
    nb, d = c.nb, c.d
    L = nb // U
    with Scope(nc, f"project{tag}") as s:
        copy = s.sb("copy", [P, U, d])
        turned_sb = s.sb("turned_sb", [P, U, P])
        ps_t = [s.bank(f"ps_t{u}") for u in range(U)]
        ps_n = [s.bank(f"ps_n{u}") for u in range(U)]
        s.tmp = s.sb("tmp", [P, U, 256])
        s.keep = s.sb("keep", [P, U, d])
        (copied, turned, turned_copied, projected, s.taken, s.kept, s.step, s.out0, s.out1) = s.sems(
            "copied turned turned_copied projected block_taken block_kept split_step out0 out1")
        with nc.Block() as block:
            def run(eng, body):
                assert nb % U == 1
                with eng.Fori(0, L) as i:
                    for u in range(U):
                        body(bass.ds(i * U + u, 1), u, lambda k, i=i, u=u: i * U + (u + k), i)
                body(slice(nb - 1, nb), 0, lambda k: nb - 1 + k, L)

            @block.scalar
            def _(act):
                act.sem_inc(turned, U)
                act.sem_inc(projected, U)

                def body(b, u, g, i):
                    act.wait_ge(turned, g(1))
                    nc.scalar.activation(copy[:, u, :], c.hn[:, b, :], ACT.Copy).then_inc(copied, 1)
                    act.wait_ge(turned, g(1 + U))
                    nc.scalar.activation(turned_sb[:, u, :], ps_t[u][:, 0:P], ACT.Copy).then_inc(turned_copied, 1)
                    act.wait_ge(s.taken, g(1 + U))
                    take_act(s, act, b, u, g, i, ps_n[u])

                run(act, body)

            @block.tensor
            def _(pe):
                pe.sem_inc(s.taken, U)
                pe.sem_inc(s.kept, U)

                def body(b, u, g, i):
                    pe.wait_ge(copied, g(1))
                    nc.tensor.transpose(ps_t[u][:, 0:P], copy[:, u, :], c.ident[:, :]).then_inc(turned, 1)
                    pe.wait_ge(turned_copied, g(1))
                    pe.wait_ge(s.taken, g(1))
                    pe.wait_ge(s.kept, g(1))
                    nc.tensor.matmul(ps_n[u][:, 0:width], turned_sb[:, u, :], weights, start=True,
                                     stop=True).then_inc(projected, 1)

                run(pe, body)

            @block.vector
            def _(dve):
                def body(b, u, g, i):
                    dve.wait_ge(projected, g(1 + U))
                    take_dve(s, dve, b, u, g, i, ps_n[u])

                run(dve, body)

            @block.sync
            def _(sp):
                if store is not None:
                    def body(b, u, g, i):
                        sp.wait_ge(s.kept, g(1 + U))
                        store(s, sp, b, u, g, i).then_inc((s.out0, s.out1)[u], 16)

                    run(sp, body)
                    sp.wait_ge(s.out0, 16 * (L + 1))
                    sp.wait_ge(s.out1, 16 * L)


def rows_of(b, width=1):
    if isinstance(b, slice):
        return slice(b.start * width, b.stop * width)
    return bass.ds(b.start * width, width)


def layer0_nodes(nc, c):
    nb, d = c.nb, c.d
    load_x(nc, c, "0", c.accd)
    normalise(nc, c, "0", c.accd)
    with Scope(nc, "fold") as s:
        ps_w = s.bank("ps_w")
        s_w, s_turn, s_m = s.sems("s_w s_turn s_m")
        with nc.Block() as block:
            @block.tensor
            def _(pe):
                nc.tensor.transpose(ps_w[:, 0:P], c.wq[:, :], c.ident[:, :])
                nc.tensor.transpose(ps_w[:, P:2 * P], c.wk[:, :], c.ident[:, :]).then_inc(s_turn, 1)
                pe.wait_ge(s_w, 4)
                nc.tensor.matmul(ps_w[:, 2 * P:3 * P], c.wqkT[:, 0, :], c.wqkT[:, 1, :], start=True,
                                 stop=True).then_inc(s_m, 1)

            @block.vector
            def _(dve):
                v = nc.vector
                v.tensor_tensor(c.wnode[:, 0:d], c.wf[:, 0, :], c.wf[:, 2, :], ALU.add).then_inc(s_w, 1)
                v.tensor_tensor(c.wnode[:, 2 * d:3 * d], c.wf[:, 1, :], c.wf[:, 2, :], ALU.subtract).then_inc(s_w, 1)
                dve.wait_ge(s_turn, 1)
                v.tensor_scalar(c.wqkT[:, 0, :], ps_w[:, 0:P], c.wa[:, 0:1], float(d) ** -0.5, ALU.mult,
                                ALU.mult).then_inc(s_w, 1)
                v.tensor_copy(c.wqkT[:, 1, :], ps_w[:, P:2 * P]).then_inc(s_w, 1)
                dve.wait_ge(s_m, 1)
                v.tensor_copy(c.wnode[:, d:2 * d], ps_w[:, 2 * P:3 * P]).then_inc(s_w, 1)
                dve.wait_ge(s_w, 5)

    STEPS = 6

    def take_dve(s, dve, b, u, g, i, ps):
        v = nc.vector
        n = g(0) * STEPS
        v.tensor_tensor(s.tmp[:, u, 0:d], ps[:, 0:d], c.bias_f[:, :], ALU.add).then_inc(s.step, 1)
        v.tensor_copy(s.tmp[:, u, d:2 * d], ps[:, d:2 * d]).then_inc(s.taken, 1)
        dve.wait_ge(s.step, n + 1)
        dve.wait_ge(s.taken, g(1 + U))
        row = rows_of(b, 3 * c.AGW)
        part = [c.lut[:, bass.ds(row.start + k * c.AGW, c.AGW)] if not isinstance(row, slice)
                else c.lut[:, row.start + k * c.AGW:row.start + (k + 1) * c.AGW] for k in range(3)]
        split_bf16(dve, v, s.tmp[:, u, :], part, s.step, n + 1)
        dve.wait_ge(s.step, n + 5)
        dve.sem_inc(s.step, 1)

    def take_act(s, act, b, u, g, i, ps):
        act.wait_ge((s.out0, s.out1)[u], i * 16)
        nc.scalar.activation(s.keep[:, u, :], ps[:, 2 * d:3 * d], ACT.Copy).then_inc(s.kept, 1)

    def store(s, sp, b, u, g, i):
        return sp.dma_start(c.tab_b[rows_of(b, P), :], s.keep[:, u, :])

    project(nc, c, "0", c.wnode[:, :], 3 * d, take_dve, take_act, store)


def load_blocks(eng, c, key, at, ahead, regs):
    eng.load(regs, c.blk[0:1, key, at.tiles(ahead + 1)])
    return [eng.snap(r, min_val=0, max_val=c.nb - 1) for r in regs]


def one_hots(c, out, at, ahead, field=0):
    for j in range(G):
        last = c.nc.vector.tensor_scalar(out[:, j, :], c.iota_b[:, :], c.meta[:, at.tile(j, ahead), field],
                                         None, ALU.is_equal)
    return last


def turn(c, ps, hot):
    for j in range(G):
        last = c.nc.tensor.transpose(ps[:, j * P:(j + 1) * P], hot[:, j, :], c.ident_b[:, :])
    return last


def layer0_edges(nc, c):
    pl, nb, d, ef, attr = c.pl, c.nb, c.d, c.ef, c.attr
    ZW, AGW = c.ZW, c.AGW
    SLOTS = 4
    PRIMED = 2
    with Scope(nc, "layer0") as s:
        row = s.sb("row", [P, SLOTS, G, attr])
        want = s.sb("want", [P, SLOTS, G], i32)
        hot = s.sb("hot", [P, 2, G, P], bf16)
        hot_t = s.sb("hot_t", [P, 2, G * P], bf16)
        attr_t = s.sb("attr_t", [ef, 2, G * P])
        bt = s.sb("bt", [P, 2, G, d])
        pre = s.sb("pre", [P, 2, G, d])
        ex = s.sb("ex", [P, 2, G, d])
        feat = s.sb("feat", [P, 2, G, ZW])
        hot_w = s.sb("hot_w", [P, 2, G, P])
        dot = s.sb("dot", [P, 2, G])
        att = s.sb("att", [P, 2, G])
        e_pos = s.sb("e_pos", [P, 2, G])
        e_neg = s.sb("e_neg", [P, 2, G])
        wt = s.sb("wt", [P, 2, G])
        ps_ag = [s.bank(f"ps_ag{u}", 2)[:, :].rearrange("p (g n) -> p g n", g=G) for u in range(2)]
        ps_hot = s.bank("ps_hot", 1, bf16)
        ps_attr = s.bank("ps_attr")
        ps_sum = s.bank("ps_sum", 2)

        def sum_of(j):
            at = (j // 2) * 512 + (j % 2) * ZW
            return ps_sum[:, at:at + ZW]

        row_in = [s.sem(f"row_in{q}") for q in range(SLOTS)]
        b_in = [s.sem(f"b_in{q}") for q in range(2)]
        (zeroed, fields_ready, hot_ready, turned, attr_turned, hot_t_ready, attr_t_ready, ag_ready, pre_ready, ex_ready,
         neg_ready, feat_ready, prod_ready, dot_ready, masked, att_ready, e_pos_ready, e_neg_ready, weight_ready,
         hot_w_ready, sums_ready, added, gather_step) = s.sems(
            "zeroed fields_ready hot_ready turned attr_turned hot_t_ready attr_t_ready ag_ready pre_ready ex_ready "
            "neg_ready feat_ready prod_ready dot_ready masked att_ready e_pos_ready e_neg_ready weight_ready "
            "hot_w_ready sums_ready added gather_step")
        with nc.Block() as block:
            @block.vector
            def _(dve):
                nc.vector.memset(c.acc[:, :], 0.0).then_inc(zeroed, 1)
                dve.wait_ge(zeroed, 1)
                dve.sem_inc(turned, PRIMED)
                dve.sem_inc(pre_ready, PRIMED)
                dve.sem_inc(ag_ready, PRIMED)
                dve.sem_inc(prod_ready, PRIMED)
                dve.sem_inc(hot_w_ready, SLOTS)

        with nc.Block() as block:
            @block.sync
            def _(sp):
                def load(i, u, at):
                    sp.wait_ge(hot_w_ready, at.g(1))
                    sp.dma_start(row[:, u % SLOTS, :, :].rearrange("p g n -> p (g n)"),
                                 c.rows_s.rearrange("(g p r) n -> g p (r n)", p=P, r=G)[
                                     bass.ds(at.g(), 1) if not isinstance(at.g(), int) else slice(at.g(), at.g() + 1), :, :
                                 ].rearrange("a p n -> (a p) n")
                                 ).then_inc(row_in[u % SLOTS], 16)

                with sp.Fori(0, pl.loops) as i:
                    for u in range(UB):
                        load(i, u, At(i, u))
                for u in range(AHEAD):
                    load(pl.loops, u, At(pl.loops, u))
                for u in range(AHEAD):
                    sp.wait_ge(row_in[u], 16 * (pl.loops + 1))

            @block.gpsimd
            def _(pool):
                limit = pool.to_reg(pl.n - 1)
                with pool.Fori(0, pl.loops) as i:
                    for u in range(UB):
                        at = At(i, u)
                        pool.wait_ge(fields_ready, at.g(1))
                        pool.wait_ge(pre_ready, at.g(1))
                        pool.sem_inc(gather_step, 1)
                        for j in range(G):
                            nc.gpsimd.indirect_dma_start(
                                bt[:, u % 2, j, :], None, c.tab_b[0:pl.n, :],
                                bass.IndirectOffsetOnAxis(want[:, u % SLOTS, j:j + 1], 0),
                                bounds_check=limit, oob_is_err=False).then_inc(b_in[u % 2], 16)

            @block.scalar
            def _(act):
                a = nc.scalar

                def fields(at, ahead):
                    q = (at.u + ahead) % SLOTS
                    act.wait_ge(row_in[q], at.uses(SLOTS, ahead) * 16)
                    a.activation(c.meta[:, at.tiles(ahead), :], row[:, q, :, SRC_LO:DST_HI + 1], ACT.Copy)
                    a.activation(c.where[:, :, at.tiles(ahead)], row[:, q, :, DST:DROW + 1].rearrange("p g f -> p f g"),
                                 ACT.Copy)
                    a.activation(want[:, q, :], row[:, q, :, DST], ACT.Copy).then_inc(fields_ready, 1)

                def evacuate(at, ahead):
                    t = (at.u + ahead) % 2
                    act.wait_ge(turned, at.g(ahead + 1 + PRIMED))
                    act.wait_ge(ag_ready, at.g(ahead + 1))
                    a.activation(hot_t[:, t, :], ps_hot[:, 0:G * P], ACT.Copy).then_inc(hot_t_ready, 1)
                    act.wait_ge(attr_turned, at.g(ahead + 1))
                    a.activation(attr_t[:, t, :], ps_attr[0:ef, :], ACT.Copy).then_inc(attr_t_ready, 1)

                first = At(0, 0)
                fields(first, 0)
                fields(first, 1)
                fields(first, 2)
                evacuate(first, 0)
                evacuate(first, 1)
                with act.Fori(0, pl.loops) as i:
                    for u in range(UB):
                        at, t = At(i, u), u % 2
                        act.wait_ge(pre_ready, at.g(1 + PRIMED))
                        a.activation(ex[:, t, :, :], pre[:, t, :, :], ACT.Exp).then_inc(ex_ready, 1)
                        evacuate(at, 2)
                        fields(at, 3)
                        act.wait_ge(masked, at.g(1))
                        a.activation(att[:, t, :], dot[:, t, :], ACT.Tanh).then_inc(att_ready, 1)
                        act.wait_ge(att_ready, at.g(1))
                        a.activation(e_pos[:, t, :], att[:, t, :], ACT.Exp).then_inc(e_pos_ready, 1)
                        a.activation(e_neg[:, t, :], att[:, t, :], ACT.Exp, scale=-1.0).then_inc(e_neg_ready, 1)

            @block.vector
            def _(dve):
                v = nc.vector
                regs = [dve.alloc_register(f"dve_blk{j}") for j in range(G)]

                def hots(at, ahead):
                    t = (at.u + ahead) % 2
                    dve.wait_ge(fields_ready, at.g(ahead + 1))
                    dve.wait_ge(turned, at.g(ahead + 1))
                    one_hots(c, hot[:, t, :, :], at, ahead).then_inc(hot_ready, 1)

                def add_sums(at):
                    blocks = load_blocks(dve, c, 0, at, -1, regs)
                    dve.wait_ge(sums_ready, at.g(1))
                    for j in range(G):
                        dve.wait_ge(added, at.g() * G + j)
                        dest = c.acc[:, bass.ds(blocks[j] * ZW, ZW)]
                        v.tensor_tensor(dest, dest, sum_of(j), ALU.add).then_inc(added, 1)

                first = At(0, 0)
                hots(first, 0)
                hots(first, 1)
                hots(first, 2)
                with dve.Fori(0, pl.loops) as i:
                    for u in range(UB):
                        at, t, q = At(i, u), u % 2, u % SLOTS
                        dve.wait_ge(b_in[t], at.uses(2) * (16 * G))
                        dve.wait_ge(ag_ready, at.g(1 + PRIMED))
                        v.tensor_tensor(pre[:, t, :, :], ps_ag[t][:, :, 0:d], bt[:, t, :, :], ALU.add).then_inc(pre_ready, 1)
                        add_sums(at)
                        dve.wait_ge(ex_ready, at.g(1))
                        v.tensor_scalar(ex[:, t, :, :], ex[:, t, :, :], 1.0, 1.0, ALU.min, ALU.subtract).then_inc(neg_ready, 1)
                        dve.wait_ge(neg_ready, at.g(1))
                        v.scalar_tensor_tensor(feat[:, t, :, 0:d], pre[:, t, :, :], 0.0, ex[:, t, :, :], ALU.max,
                                               ALU.add).then_inc(feat_ready, 1)
                        dve.wait_ge(feat_ready, at.g(1))
                        v.tensor_tensor(pre[:, t, :, :], feat[:, t, :, 0:d], ps_ag[t][:, :, d:2 * d], ALU.mult).then_inc(prod_ready, 1)
                        dve.wait_ge(prod_ready, at.g(1 + PRIMED))
                        v.tensor_reduce(dot[:, t, :], pre[:, t, :, :], AX.X, ALU.add).then_inc(dot_ready, 1)
                        dve.wait_ge(dot_ready, at.g(1))
                        v.scalar_tensor_tensor(dot[:, t, :], row[:, q, :, 0], 8.0, dot[:, t, :], ALU.is_lt,
                                               ALU.mult).then_inc(masked, 1)
                        hots(at, 3)
                        dve.wait_ge(e_pos_ready, at.g(1))
                        v.scalar_tensor_tensor(wt[:, t, :], row[:, q, :, 0], 8.0, e_pos[:, t, :], ALU.is_lt,
                                               ALU.mult).then_inc(weight_ready, 1)
                        dve.wait_ge(e_neg_ready, at.g(1))
                        v.tensor_tensor(feat[:, t, :, d], att[:, t, :], e_neg[:, t, :], ALU.mult)
                        dve.wait_ge(weight_ready, at.g(1))
                        for j in range(G):
                            last = v.tensor_scalar(hot_w[:, t, j, :], c.iota[:, :], row[:, q, j, SRC_LO:SRC_LO + 1],
                                                   wt[:, t, j:j + 1], ALU.is_equal, ALU.mult)
                        last.then_inc(hot_w_ready, 1)
                add_sums(At(pl.loops, 0))
                dve.wait_ge(added, (pl.groups + 1) * G)

            @block.tensor
            def _(pe):
                t_ = nc.tensor
                regs = [pe.alloc_register(f"pe_blk{j}") for j in range(G)]

                def turn_group(at, ahead):
                    t, q = (at.u + ahead) % 2, (at.u + ahead) % SLOTS
                    pe.wait_ge(hot_ready, at.g(ahead + 1))
                    pe.wait_ge(hot_t_ready, at.g(ahead))
                    turn(c, ps_hot, hot[:, t, :, :]).then_inc(turned, 1)
                    pe.wait_ge(attr_t_ready, at.g(ahead))
                    for j in range(G):
                        last = t_.transpose(ps_attr[0:ef, j * P:(j + 1) * P], row[:, q, j, 0:ef], c.ident[:, :])
                    last.then_inc(attr_turned, 1)

                def look_up(at, ahead):
                    t = (at.u + ahead) % 2
                    blocks = load_blocks(pe, c, 0, at, ahead, regs)
                    pe.wait_ge(hot_t_ready, at.g(ahead + 1))
                    pe.wait_ge(prod_ready, at.g(ahead + 1))
                    pe.wait_ge(attr_t_ready, at.g(ahead + 1))
                    for j in range(G):
                        for k in range(3):
                            t_.matmul(ps_ag[t][:, j, :], hot_t[:, t, j * P:(j + 1) * P],
                                      c.lut[:, bass.ds(blocks[j] * (3 * AGW) + k * AGW, AGW)], start=(k == 0), stop=False)
                        last = t_.matmul(ps_ag[t][:, j, 0:d], attr_t[:, t, j * P:(j + 1) * P], c.w4[:, :],
                                         start=False, stop=True)
                    last.then_inc(ag_ready, 1)

                def sum_up(at):
                    t = at.u % 2
                    pe.wait_ge(hot_w_ready, at.g(1 + SLOTS))
                    pe.wait_ge(added, (at.g(1)) * G)
                    for j in range(G):
                        last = t_.matmul(sum_of(j), hot_w[:, t, j, :], feat[:, t, j, :], start=True, stop=True)
                    last.then_inc(sums_ready, 1)

                for j in range(G):
                    last = t_.matmul(sum_of(j)[:, 0:P], c.zeros[:, :], c.zeros[:, :], start=True, stop=True)
                    last = t_.matmul(sum_of(j)[:, P:ZW], c.zeros[:, :], c.zeros[:, 0:ZW - P], start=True, stop=True)
                last.then_inc(sums_ready, 1)
                first = At(0, 0)
                turn_group(first, 0)
                look_up(first, 0)
                turn_group(first, 1)
                with pe.Fori(0, pl.loops) as i:
                    for u in range(UB):
                        at = At(i, u)
                        look_up(at, 1)
                        turn_group(at, 2)
                        sum_up(at)


def layer0_update(nc, c):
    nb, d, hid = c.nb, c.d, c.hid
    load_x(nc, c, "1", c.xn)
    with Scope(nc, "update") as s:
        s_step, s_exp = s.sems("s_step s_exp")
        with nc.Block() as block:
            @block.scalar
            def _(act):
                nc.scalar.activation(c.stat[:, 3, :], c.acc3[:, :, d], ACT.Exp, scale=-1.0).then_inc(s_exp, 1)

            @block.vector
            def _(dve):
                v = nc.vector
                v.tensor_tensor(c.xn[:, :, :], c.xn[:, :, :],
                                c.bias_u[:, :].unsqueeze(1).to_broadcast([P, nb, d]), ALU.add)
                dve.wait_ge(s_exp, 1)
                v.tensor_tensor(c.acc3[:, :, 0:d], c.acc3[:, :, 0:d],
                                c.stat[:, 3, :].unsqueeze(2).to_broadcast([P, nb, d]), ALU.mult).then_inc(s_step, 1)
                dve.wait_ge(s_step, 1)
                v.tensor_tensor(c.hn[:, :, :], c.hn[:, :, :], c.acc3[:, :, 0:d], ALU.add).then_inc(s_step, 1)
                dve.wait_ge(s_step, 2)

    def add_x(s, dve, b, u, g, i, ps):
        nc.vector.tensor_tensor(c.xn[:, b, :], c.xn[:, b, :], ps[:, 0:d].unsqueeze(1), ALU.add).then_inc(s.taken, 1)

    def nothing(s, act, b, u, g, i, ps):
        act.sem_inc(s.kept, 1)

    project(nc, c, "u", c.wu[:, :], d, add_x, nothing)
    normalise(nc, c, "1", c.xn[:, :, :])

    STEPS = 6

    def take_dve(s, dve, b, u, g, i, ps):
        v = nc.vector
        n = g(0) * STEPS
        v.tensor_tensor(s.tmp[:, u, 0:hid], ps[:, 0:hid], c.bias_1[:, :], ALU.add).then_inc(s.step, 1)
        v.tensor_copy(c.hn[:, b, :], ps[:, 2 * hid:2 * hid + d].unsqueeze(1)).then_inc(s.taken, 1)
        dve.wait_ge(s.step, n + 1)
        row = rows_of(b, 3 * hid)
        part = [c.lut[:, bass.ds(row.start + k * hid, hid)] if not isinstance(row, slice)
                else c.lut[:, row.start + k * hid:row.start + (k + 1) * hid] for k in range(3)]
        split_bf16(dve, v, s.tmp[:, u, 0:hid], part, s.step, n + 1)
        dve.wait_ge(s.step, n + 5)
        dve.sem_inc(s.step, 1)

    def take_act(s, act, b, u, g, i, ps):
        act.wait_ge((s.out0, s.out1)[u], i * 16)
        nc.scalar.activation(s.keep[:, u, 0:hid], ps[:, hid:2 * hid], ACT.Copy).then_inc(s.kept, 1)

    def store(s, sp, b, u, g, i):
        return sp.dma_start(c.tab_q[rows_of(b, P), :], s.keep[:, u, 0:hid])

    project(nc, c, "1", c.wnode1[:, :], 2 * hid + d, take_dve, take_act, store)


def weights_pass(nc, c):
    pl, nb, hid = c.pl, c.nb, c.hid
    PRIMED = 2
    with Scope(nc, "weights") as s:
        want = s.sb("want", [P, 2, G], i32)
        hot = s.sb("hot", [P, 2, G, P], bf16)
        hot_t = s.sb("hot_t", [P, 2, G * P], bf16)
        qt = s.sb("qt", [P, 2, G, hid])
        pre = s.sb("pre", [P, 2, G, hid])
        act_h = s.sb("act_h", [P, 2, G, hid])
        ps_p = [s.bank(f"ps_p{u}")[:, 0:G * hid].rearrange("p (g n) -> p g n", g=G) for u in range(2)]
        ps_hot = s.bank("ps_hot", 1, bf16)
        q_in = [s.sem(f"q_in{q}") for q in range(2)]
        (hot_ready, turned, hot_t_ready, want_ready, p_ready, pre_ready, gelu_ready, prod_ready, logit_ready, weight_ready,
         gather_step) = s.sems("hot_ready turned hot_t_ready want_ready p_ready pre_ready gelu_ready prod_ready "
                               "logit_ready weight_ready gather_step")
        with nc.Block() as block:
            @block.vector
            def _(dve):
                dve.sem_inc(turned, PRIMED)
                dve.sem_inc(p_ready, PRIMED)
                dve.sem_inc(pre_ready, PRIMED)

        with nc.Block() as block:
            @block.gpsimd
            def _(pool):
                limit = pool.to_reg(pl.n - 1)
                with pool.Fori(0, pl.loops) as i:
                    for u in range(UB):
                        at = At(i, u)
                        pool.wait_ge(want_ready, at.g(1))
                        pool.wait_ge(pre_ready, at.g(1))
                        pool.sem_inc(gather_step, 1)
                        for j in range(G):
                            nc.gpsimd.indirect_dma_start(
                                qt[:, u % 2, j, :], None, c.tab_q[0:pl.n, :],
                                bass.IndirectOffsetOnAxis(want[:, u % 2, j:j + 1], 0),
                                bounds_check=limit, oob_is_err=False).then_inc(q_in[u % 2], 16)

            @block.scalar
            def _(act):
                a = nc.scalar

                def indices(at, ahead):
                    act.wait_ge(pre_ready, at.g(ahead + 1))
                    a.activation(want[:, (at.u + ahead) % 2, :], c.where[:, 0, at.tiles(ahead)], ACT.Copy).then_inc(want_ready, 1)

                def evacuate(at, ahead):
                    act.wait_ge(turned, at.g(ahead + 1 + PRIMED))
                    act.wait_ge(p_ready, at.g(ahead + 1))
                    a.activation(hot_t[:, (at.u + ahead) % 2, :], ps_hot[:, 0:G * P], ACT.Copy).then_inc(hot_t_ready, 1)

                first = At(0, 0)
                indices(first, 0)
                indices(first, 1)
                evacuate(first, 0)
                evacuate(first, 1)
                with act.Fori(0, pl.loops) as i:
                    for u in range(UB):
                        at, t = At(i, u), u % 2
                        act.wait_ge(pre_ready, at.g(1 + PRIMED))
                        a.activation(act_h[:, t, :, :], pre[:, t, :, :], ACT.Gelu).then_inc(gelu_ready, 1)
                        indices(at, 2)
                        evacuate(at, 2)
                act.wait_ge(logit_ready, pl.groups)
                a.activation(c.ew[:, :], c.ew[:, :], ACT.Sigmoid, bias=c.b2_col[:, 0:1]).then_inc(weight_ready, 1)
                act.wait_ge(weight_ready, 1)

            @block.vector
            def _(dve):
                v = nc.vector

                def hots(at, ahead):
                    t = (at.u + ahead) % 2
                    dve.wait_ge(turned, at.g(ahead + 1))
                    one_hots(c, hot[:, t, :, :], at, ahead).then_inc(hot_ready, 1)

                first = At(0, 0)
                hots(first, 0)
                hots(first, 1)
                hots(first, 2)
                w2 = c.w2_row[:, :].unsqueeze(1).to_broadcast([P, G, hid])
                with dve.Fori(0, pl.loops) as i:
                    for u in range(UB):
                        at, t = At(i, u), u % 2
                        dve.wait_ge(q_in[t], at.uses(2) * (16 * G))
                        dve.wait_ge(p_ready, at.g(1 + PRIMED))
                        v.tensor_tensor(pre[:, t, :, :], ps_p[t], qt[:, t, :, :], ALU.add).then_inc(pre_ready, 1)
                        hots(at, 3)
                        dve.wait_ge(gelu_ready, at.g(1))
                        v.tensor_tensor(act_h[:, t, :, :], act_h[:, t, :, :], w2, ALU.mult).then_inc(prod_ready, 1)
                        dve.wait_ge(prod_ready, at.g(1))
                        v.tensor_reduce(c.ew[:, at.tiles()], act_h[:, t, :, :], AX.X, ALU.add).then_inc(logit_ready, 1)

            @block.tensor
            def _(pe):
                t_ = nc.tensor
                regs = [pe.alloc_register(f"pe_w_blk{j}") for j in range(G)]

                def turn_group(at, ahead):
                    pe.wait_ge(hot_ready, at.g(ahead + 1))
                    pe.wait_ge(hot_t_ready, at.g(ahead))
                    turn(c, ps_hot, hot[:, (at.u + ahead) % 2, :, :]).then_inc(turned, 1)

                def look_up(at, ahead):
                    t = (at.u + ahead) % 2
                    blocks = load_blocks(pe, c, 0, at, ahead, regs)
                    pe.wait_ge(hot_t_ready, at.g(ahead + 1))
                    pe.wait_ge(pre_ready, at.g(ahead + 1))
                    for j in range(G):
                        for k in range(3):
                            last = t_.matmul(ps_p[t][:, j, :], hot_t[:, t, j * P:(j + 1) * P],
                                             c.lut[:, bass.ds(blocks[j] * (3 * hid) + k * hid, hid)],
                                             start=(k == 0), stop=(k == 2))
                    last.then_inc(p_ready, 1)

                first = At(0, 0)
                turn_group(first, 0)
                look_up(first, 0)
                turn_group(first, 1)
                with pe.Fori(0, pl.loops) as i:
                    for u in range(UB):
                        look_up(At(i, u), 1)
                        turn_group(At(i, u), 2)


def degree_pass(nc, c):
    pl, nb, d = c.pl, c.nb, c.d
    PRIMED = 2
    with Scope(nc, "degree") as s:
        hot_lo = s.sb("hot_lo", [P, 2, G, P])
        hot_hi = s.sb("hot_hi", [P, 2, G, nb])
        ps_deg = s.bank("ps_deg")
        hots_ready, summed, started, s_step, s_root = s.sems("hots_ready summed started s_step s_root")
        with nc.Block() as block:
            @block.vector
            def _(dve):
                dve.sem_inc(summed, PRIMED)

        with nc.Block() as block:
            @block.vector
            def _(dve):
                v = nc.vector
                with dve.Fori(0, pl.loops) as i:
                    for u in range(UB):
                        at, t = At(i, u), u % 2
                        dve.wait_ge(summed, at.g(1))
                        for j in range(G):
                            v.tensor_scalar(hot_lo[:, t, j, :], c.iota[:, :], c.meta[:, at.tile(j), 1], None, ALU.is_equal)
                            last = v.tensor_scalar(hot_hi[:, t, j, :], c.iota[:, 0:nb], c.meta[:, at.tile(j), 2],
                                                   None, ALU.is_equal)
                        last.then_inc(hots_ready, 1)
                        dve.wait_ge(hots_ready, at.g(0) * 2 + 1)
                        v.tensor_tensor(hot_hi[:, t, :, :], hot_hi[:, t, :, :],
                                        c.ew[:, at.tiles()].unsqueeze(2).to_broadcast([P, G, nb]), ALU.mult).then_inc(hots_ready, 1)
                n = 0

                def link(ins):
                    nonlocal n
                    n += 1
                    ins.then_inc(s_step, 1)
                    dve.wait_ge(s_step, n)

                dve.wait_ge(summed, pl.groups + PRIMED + 1)
                link(v.tensor_scalar(c.stat[:, 0, :], ps_deg[:, 0:nb], 1.0, None, ALU.add))
                dve.wait_ge(s_root, 1)
                link(v.reciprocal(c.dinv[:, :], c.stat[:, 1, :]))
                link(v.tensor_tensor(c.hn[:, :, :], c.hn[:, :, :], c.dinv[:, :].unsqueeze(2).to_broadcast([P, nb, d]), ALU.mult))
                x_lut = c.lut[:, c.X_AT:c.X_AT + nb * 3 * d].rearrange("p (b k n) -> p b k n", k=3, n=d)
                rest = c.accd.rearrange("p b n -> p (b n)")
                link(v.tensor_copy(c.accd, c.hn[:, :, :]))
                split_bf16(dve, v, c.accd, [x_lut[:, :, k, :] for k in range(3)], s_step, n)
                dve.wait_ge(s_step, n + 4)

            @block.scalar
            def _(act):
                act.wait_ge(s_step, 1)
                nc.scalar.activation(c.stat[:, 1, :], c.stat[:, 0, :], ACT.Sqrt).then_inc(s_root, 1)

            @block.tensor
            def _(pe):
                t_ = nc.tensor
                t_.matmul(ps_deg[:, 0:nb], c.zeros[:, :], c.zeros[:, 0:nb], start=True, stop=False)
                with pe.Fori(0, pl.loops) as i:
                    for u in range(UB):
                        at, t = At(i, u), u % 2
                        pe.wait_ge(hots_ready, at.g(1) * 2)
                        for j in range(G):
                            last = t_.matmul(ps_deg[:, 0:nb], hot_lo[:, t, j, :], hot_hi[:, t, j, :], start=False, stop=False)
                        last.then_inc(summed, 1)
                t_.matmul(ps_deg[:, 0:nb], c.zeros[:, :], c.zeros[:, 0:nb], start=False,
                          stop=True).then_inc(summed, 1)


def message_pass(nc, c):
    pl, nb, d = c.pl, c.nb, c.d
    ZW = c.ZW
    PRIMED = 2
    with Scope(nc, "message") as s:
        want = s.sb("want", [P, 2, G], i32)
        hot = s.sb("hot", [P, 2, G, P], bf16)
        hot_t = s.sb("hot_t", [P, 2, G * P], bf16)
        msg = s.sb("msg", [P, 2, G, ZW])
        ps_x = [s.bank(f"ps_x{u}")[:, :].rearrange("p (g n) -> p g n", g=G) for u in range(2)]
        ps_hot = s.bank("ps_hot", 1, bf16)
        sent = [s.sem(f"sent{q}") for q in range(2)]
        (hot_ready, turned, hot_t_ready, want_ready, x_ready, msg_ready, scatter_step) = s.sems(
            "hot_ready turned hot_t_ready want_ready x_ready msg_ready scatter_step")
        with nc.Block() as block:
            @block.vector
            def _(dve):
                dve.sem_inc(turned, PRIMED)
                dve.sem_inc(x_ready, PRIMED)
                dve.sem_inc(msg_ready, PRIMED)

        with nc.Block() as block:
            @block.gpsimd
            def _(pool):
                limit = pool.to_reg(pl.rows - 1)
                with pool.Fori(0, pl.loops) as i:
                    for u in range(UB):
                        at = At(i, u)
                        pool.wait_ge(want_ready, at.g(1))
                        pool.wait_ge(msg_ready, at.g(1 + PRIMED))
                        pool.sem_inc(scatter_step, 1)
                        for j in range(G):
                            nc.gpsimd.indirect_dma_start(
                                c.rows_d[:, :], bass.IndirectOffsetOnAxis(want[:, u % 2, j:j + 1], 0), msg[:, u % 2, j, :], None,
                                bounds_check=limit, oob_is_err=False).then_inc(sent[u % 2], 16)
                for q in range(2):
                    pool.wait_ge(sent[q], pl.groups // 2 * 16 * G)

            @block.scalar
            def _(act):
                a = nc.scalar

                def evacuate(at, ahead):
                    act.wait_ge(turned, at.g(ahead + 1 + PRIMED))
                    act.wait_ge(x_ready, at.g(ahead + 1))
                    a.activation(hot_t[:, (at.u + ahead) % 2, :], ps_hot[:, 0:G * P], ACT.Copy).then_inc(hot_t_ready, 1)

                evacuate(At(0, 0), 0)
                evacuate(At(0, 0), 1)
                with act.Fori(0, pl.loops) as i:
                    for u in range(UB):
                        at, t = At(i, u), u % 2
                        act.wait_ge(sent[t], at.uses(2, 0, -1) * (16 * G))
                        a.activation(msg[:, t, :, d], c.meta[:, at.tiles(), 1], ACT.Copy)
                        a.activation(want[:, t, :], c.where[:, 1, at.tiles()], ACT.Copy).then_inc(want_ready, 1)
                        evacuate(at, 2)

            @block.vector
            def _(dve):
                v = nc.vector

                def hots(at, ahead):
                    dve.wait_ge(turned, at.g(ahead + 1))
                    one_hots(c, hot[:, (at.u + ahead) % 2, :, :], at, ahead).then_inc(hot_ready, 1)

                first = At(0, 0)
                hots(first, 0)
                hots(first, 1)
                hots(first, 2)
                with dve.Fori(0, pl.loops) as i:
                    for u in range(UB):
                        at, t = At(i, u), u % 2
                        dve.wait_ge(x_ready, at.g(1 + PRIMED))
                        dve.wait_ge(sent[t], at.uses(2, 0, -1) * (16 * G))
                        v.tensor_tensor(msg[:, t, :, 0:d], ps_x[t], c.ew[:, at.tiles()].unsqueeze(2).to_broadcast([P, G, d]),
                                        ALU.mult).then_inc(msg_ready, 1)
                        hots(at, 3)

            @block.tensor
            def _(pe):
                t_ = nc.tensor
                regs = [pe.alloc_register(f"pe_m_blk{j}") for j in range(G)]

                def turn_group(at, ahead):
                    pe.wait_ge(hot_ready, at.g(ahead + 1))
                    pe.wait_ge(hot_t_ready, at.g(ahead))
                    turn(c, ps_hot, hot[:, (at.u + ahead) % 2, :, :]).then_inc(turned, 1)

                def look_up(at, ahead):
                    t = (at.u + ahead) % 2
                    blocks = load_blocks(pe, c, 0, at, ahead, regs)
                    pe.wait_ge(hot_t_ready, at.g(ahead + 1))
                    pe.wait_ge(msg_ready, at.g(ahead + 1))
                    for j in range(G):
                        for k in range(3):
                            last = t_.matmul(ps_x[t][:, j, :], hot_t[:, t, j * P:(j + 1) * P],
                                             c.lut[:, bass.ds(blocks[j] * (3 * d) + (c.X_AT + k * d), d)],
                                             start=(k == 0), stop=(k == 2))
                    last.then_inc(x_ready, 1)

                first = At(0, 0)
                turn_group(first, 0)
                look_up(first, 0)
                turn_group(first, 1)
                with pe.Fori(0, pl.loops) as i:
                    for u in range(UB):
                        look_up(At(i, u), 1)
                        turn_group(At(i, u), 2)


def target_pass(nc, c):
    pl, nb, d, ZW = c.pl, c.nb, c.d, c.ZW
    SLOTS = 4
    with Scope(nc, "target") as s:
        msg = s.sb("msg", [P, SLOTS, G, ZW])
        hot = s.sb("hot", [P, 2, G, P])
        ps = [s.bank(f"ps{u}")[:, :].rearrange("p (g n) -> p g n", g=G) for u in range(2)]
        msg_in = [s.sem(f"msg_in{q}") for q in range(SLOTS)]
        zeroed, hot_ready, sums_ready, added = s.sems("zeroed hot_ready sums_ready added")
        with nc.Block() as block:
            @block.vector
            def _(dve):
                nc.vector.memset(c.accd, 0.0).then_inc(zeroed, 1)
                dve.wait_ge(zeroed, 1)
                dve.sem_inc(sums_ready, SLOTS - 1)

        with nc.Block() as block:
            @block.sync
            def _(sp):
                rows = c.rows_d.rearrange("(g p r) n -> g p (r n)", p=P, r=G)
                with sp.Fori(0, pl.loops) as i:
                    for u in range(UB):
                        at = At(i, u)
                        sp.wait_ge(sums_ready, at.g(1))
                        sp.dma_start(msg[:, u, :, :].rearrange("p g n -> p (g n)"),
                                     rows[bass.ds(at.g(), 1), :, :].rearrange("a p n -> (a p) n")).then_inc(msg_in[u], 16)

            @block.vector
            def _(dve):
                v = nc.vector
                regs = [dve.alloc_register(f"dve_t_blk{j}") for j in range(G)]

                def add_sums(at):
                    blocks = load_blocks(dve, c, 1, at, -1, regs)
                    dve.wait_ge(sums_ready, at.g(SLOTS))
                    for j in range(G):
                        dve.wait_ge(added, at.g() * G + j)
                        dest = c.acc[:, bass.ds(blocks[j] * d, d)]
                        v.tensor_tensor(dest, dest, ps[(at.u - 1) % 2][:, j, :], ALU.add).then_inc(added, 1)

                with dve.Fori(0, pl.loops) as i:
                    for u in range(UB):
                        at, t = At(i, u), u % 2
                        dve.wait_ge(msg_in[u], at.uses(SLOTS) * 16)
                        dve.wait_ge(sums_ready, at.g(SLOTS - 1))
                        for j in range(G):
                            last = v.tensor_scalar(hot[:, t, j, :], c.iota[:, :], msg[:, u, j, d:d + 1], None, ALU.is_equal)
                        last.then_inc(hot_ready, 1)
                        add_sums(at)
                add_sums(At(pl.loops, 0))
                dve.wait_ge(added, (pl.groups + 1) * G)

            @block.tensor
            def _(pe):
                t_ = nc.tensor
                for j in range(G):
                    last = t_.matmul(ps[1][:, j, :], c.zeros[:, :], c.zeros[:, :], start=True, stop=True)
                last.then_inc(sums_ready, 1)
                with pe.Fori(0, pl.loops) as i:
                    for u in range(UB):
                        at, t = At(i, u), u % 2
                        pe.wait_ge(hot_ready, at.g(1))
                        pe.wait_ge(added, at.g() * G)
                        for j in range(G):
                            last = t_.matmul(ps[t][:, j, :], hot[:, t, j, :], msg[:, u, j, 0:d], start=True, stop=True)
                        last.then_inc(sums_ready, 1)


def finish(nc, c):
    nb, d, pl = c.nb, c.d, c.pl
    with Scope(nc, "finish") as s:
        s_step, s_out = s.sems("s_step s_out")
        with nc.Block() as block:
            @block.vector
            def _(dve):
                v = nc.vector
                v.tensor_tensor(c.xn[:, :, :], c.xn[:, :, :],
                                c.bias_c[:, :].unsqueeze(1).to_broadcast([P, nb, d]), ALU.add)
                v.tensor_tensor(c.accd, c.accd, c.hn[:, :, :], ALU.add).then_inc(s_step, 1)
                dve.wait_ge(s_step, 1)
                v.tensor_tensor(c.accd, c.accd, c.dinv[:, :].unsqueeze(2).to_broadcast([P, nb, d]), ALU.mult).then_inc(s_step, 1)
                dve.wait_ge(s_step, 2)
                v.tensor_tensor(c.accd, c.accd, c.xn[:, :, :], ALU.add).then_inc(s_step, 1)

            @block.sync
            def _(sp):
                whole = c.LAST * P
                sp.wait_ge(s_step, 3)
                sp.dma_start(c.out[0:whole, :].rearrange("(b p) n -> p b n", p=P), c.accd[:, 0:c.LAST, :]).then_inc(s_out, 16)
                sp.dma_start(c.out[whole:, :], c.accd[0:pl.tail, c.LAST, :]).then_inc(s_out, 16)
                sp.wait_ge(s_out, 32)


_INS = ["x", "src", "dst", "edge_attr_70", "L0_gnn_Wf", "L0_gnn_bf", "L0_gnn_Wq", "L0_gnn_Wk", "L0_gnn_Wa",
        "L0_gnn_Wu", "L0_gnn_bu", "L1_gnn_mlp_w1", "L1_gnn_mlp_b1", "L1_gnn_mlp_w2", "L1_gnn_mlp_b2",
        "L1_gnn_conv_w", "L1_gnn_conv_b"]


def kernel(**inputs):
    import concourse.bacc as bacc
    from concourse.bass_utils import run_bass_kernel_spmd

    nc = bacc.Bacc("TRN2", target_bir_lowering=False, num_devices=1)
    arrays, args = {}, []
    for name in _INS:
        a = np.ascontiguousarray(inputs[name])
        arrays[name] = a
        args.append(nc.dram_tensor(name, a.shape, mybir.dt.from_np(a.dtype), kind="ExternalInput").ap())
    out = nc.dram_tensor("out", inputs["x"].shape, f32, kind="ExternalOutput").ap()
    gnn(nc, *args, out)
    r = run_bass_kernel_spmd(nc, [arrays], core_ids=[0])
    return r.results[0]["out"]
```

```python
import numpy as np
from contextlib import ExitStack

import concourse.bass as bass
from concourse import mybir

f32 = mybir.dt.float32
bf16 = mybir.dt.bfloat16
i32 = mybir.dt.int32
ALU = mybir.AluOpType
ACT = mybir.ActivationFunctionType
AX = mybir.AxisListType

P = 128
G = 4
U = 2
UB = 4
FIRST = 4
UNIT = (2, 4)
FAR = 1 << 20
EPS = 1e-5

SRC_1, DST_LO, DST_HI, DST, DROW = 65, 66, 67, 68, 69
META = 5


class Plan:

    def __init__(self, n_nodes, n_edges, d, attr, attr_used, hid):
        self.n, self.e, self.d, self.attr, self.ef, self.hid = n_nodes, n_edges, d, attr, attr_used, hid
        self.nb = -(-n_nodes // P)
        self.tail = n_nodes - (self.nb - 1) * P
        self.full = n_edges // P
        self.rest = n_edges - self.full * P
        self.prep_loops = self.full // (G * U)
        self.peeled = self.full - self.prep_loops * G * U
        assert self.rest and self.peeled < G
        self.cols = self.prep_loops * G * U + G
        self.units = [(n_edges + self.nb * (k * P - 1)) // (k * P) for k in UNIT]
        self.groups = [-(-n * k // G) for n, k in zip(self.units, UNIT)]
        self.tiles = self.groups[0] * G
        self.rows = [n * G * P for n in self.groups]
        self.map = -(-max(self.units) // P) * P


def gnn(nc, x, src, dst, edge_attr, Wf, bf, Wq, Wk, Wa, Wu, bu, w1, b1, w2, b2, conv_w, conv_b, out):
    n_nodes, d = x.shape
    n_edges, attr = edge_attr.shape
    pl = Plan(n_nodes, n_edges, d, attr, Wf.shape[0] - 3 * d, w1.shape[1])
    nb, hid, ef = pl.nb, pl.hid, pl.ef
    assert d == P and ef == SRC_1 and attr == ef + META

    c = Shared()
    c.nc, c.pl, c.nb, c.d, c.hid, c.ef, c.attr = nc, pl, nb, d, hid, ef, attr
    c.x, c.src, c.dst, c.edge_attr, c.out = x, src, dst, edge_attr, out
    c.Wf, c.bf, c.Wq, c.Wk, c.Wa, c.Wu, c.bu = Wf, bf, Wq, Wk, Wa, Wu, bu
    c.w1, c.b1, c.w2, c.b2, c.conv_w, c.conv_b = w1, b1, w2, b2, conv_w, conv_b
    c.LAST = nb - 1
    c.AGW = AGW = 2 * d
    c.X_AT = nb * 3 * hid
    c.ZW = ZW = d + 1

    c.rows_s = nc.dram_tensor("rows_by_source", [pl.rows[0] + nb * UNIT[0] * P, attr], f32).ap()
    c.rows_d = nc.dram_tensor("messages_by_target", [pl.rows[1] + nb * UNIT[1] * P, ZW], f32).ap()
    c.tab_b = nc.dram_tensor("table_b", [nb * P, d], f32).ap()
    c.tab_q = nc.dram_tensor("table_q", [nb * P, hid], f32).ap()
    c.blk_dram = nc.dram_tensor("block_of_unit", [2, pl.map], i32).ap()

    ctx = ExitStack()
    with ctx:
        def sb(name, shape, dt=f32):
            return ctx.enter_context(nc.sbuf_tensor(name, shape, dt))

        c.iota_i = sb("iota_i", [P, P], i32)
        c.part_i = sb("part_i", [P, 1], i32)
        c.unit_i = sb("unit_i", [P, pl.map // P], i32)
        c.iota = sb("iota", [P, P])
        c.iota1 = sb("iota1", [P, P])
        c.iota1_b = sb("iota1_b", [P, P], bf16)
        c.part = sb("part", [P, 1])
        c.ident = sb("ident", [P, P])
        c.ident_b = sb("ident_b", [P, P], bf16)
        c.earlier_b = sb("earlier_b", [P, P], bf16)
        c.ones = sb("ones", [P, P])
        c.ones_b = sb("ones_b", [P, P], bf16)
        c.zeros = sb("zeros", [P, P])
        c.eps_t = sb("eps_t", [P, 1])
        c.minus_1 = sb("minus_1", [P, 1])

        c.wf = sb("wf", [P, 3, d])
        c.w4 = sb("w4", [ef, d])
        c.wq = sb("wq", [P, d])
        c.wk = sb("wk", [P, d])
        c.wa = sb("wa", [P, 1])
        c.wu = sb("wu", [P, d])
        c.wqkT = sb("wqkT", [P, 2, P])
        c.wnode = sb("wnode", [P, 3 * d])
        c.wnode1 = sb("wnode1", [P, 2 * hid + d])
        c.bias_f = sb("bias_f", [P, d])
        c.bias_u = sb("bias_u", [P, d])
        c.bias_1 = sb("bias_1", [P, hid])
        c.bias_c = sb("bias_c", [P, d])
        c.w2_row = sb("w2_row", [P, hid])
        c.b2_col = sb("b2_col", [P, 1])

        c.blk = sb("blk", [1, 2, pl.map], i32)

        with nc.sbuf_tensor("fill_s", [P, G, attr], f32) as c.fill_s, nc.sbuf_tensor("fill_d", [P, G, ZW], f32) as c.fill_d:
            setup_phase(nc, c)
            sort_phase(nc, c)

        c.hn = sb("hn", [P, nb, d])
        c.acc = sb("acc", [P, nb * ZW])
        c.acc3 = c.acc[:, :].rearrange("p (b w) -> p b w", w=ZW)
        c.accd = c.acc[:, 0:nb * d].rearrange("p (b w) -> p b w", w=d)
        c.stat = sb("stat", [P, 4, nb])
        c.dinv = sb("dinv", [P, nb])

        c.meta = sb("meta", [P, pl.tiles, 3], bf16)
        c.where = sb("where", [P, 2, pl.tiles], i32)
        with nc.sbuf_tensor("lut0", [P, nb * 3 * AGW], bf16) as c.lut:
            layer0_nodes(nc, c)
            layer0_edges(nc, c)
        c.lut = sb("lut1", [P, nb * 3 * (hid + d)], bf16)
        c.xn = sb("xn", [P, nb, d])
        c.ew = sb("ew", [P, pl.tiles])
        layer0_update(nc, c)
        weights_pass(nc, c)
        scale_nodes(nc, c)
        message_pass(nc, c)
        target_pass(nc, c)
        finish(nc, c)


class Shared:
    pass


class Scope:

    def __init__(self, nc, tag):
        self.nc, self.tag, self.ctx = nc, tag, ExitStack()

    def __enter__(self):
        return self

    def __exit__(self, *error):
        self.ctx.close()

    def sb(self, name, shape, dt=f32):
        return self.ctx.enter_context(self.nc.sbuf_tensor(f"{self.tag}_{name}", shape, dt))

    def bank(self, name, banks=1, dt=f32):
        return self.ctx.enter_context(self.nc.psum_tensor(f"{self.tag}_{name}", [P, banks * 2048 // mybir.dt.size(dt)], dt))

    def sem(self, name):
        return self.ctx.enter_context(self.nc.semaphore(f"{self.tag}_{name}"))

    def sems(self, names):
        return [self.sem(n) for n in names.split()]


def setup_phase(nc, c):
    pl, nb, d, hid, ef, attr = c.pl, c.nb, c.d, c.hid, c.ef, c.attr
    with Scope(nc, "setup") as s:
        fill, fill_d = c.fill_s, c.fill_d
        s_iota, s_const, s_fill, s_load, s_zero = s.sems(
            "s_iota s_const s_fill s_load s_zero")

        with nc.Block() as block:
            @block.gpsimd
            def _(pool):
                nc.gpsimd.iota(c.iota_i[:, :], pattern=[[1, P]], base=0, channel_multiplier=0).then_inc(s_iota, 1)
                nc.gpsimd.iota(c.part_i[:, :], pattern=[[0, 1]], base=0, channel_multiplier=1).then_inc(s_iota, 1)
                nc.gpsimd.iota(c.unit_i[:, :], pattern=[[1, pl.map // P]], base=0,
                               channel_multiplier=pl.map // P).then_inc(s_iota, 1)

            @block.vector
            def _(dve):
                v = nc.vector
                v.memset(fill[:, :, :], 0.0).then_inc(s_zero, 1)
                v.memset(fill_d[:, :, :], 0.0).then_inc(s_zero, 1)
                dve.wait_ge(s_zero, 2)
                v.memset(fill[:, :, DST_LO:DST_HI + 1], -1.0).then_inc(s_fill, 1)
                v.memset(fill[:, :, DROW:DROW + 1], float(FAR)).then_inc(s_fill, 1)
                v.memset(fill_d[:, :, d:d + 1], -1.0).then_inc(s_fill, 1)
                v.memset(c.ones[:, :], 1.0).then_inc(s_const, 1)
                v.memset(c.ones_b[:, :], 1.0).then_inc(s_const, 1)
                v.memset(c.zeros[:, :], 0.0).then_inc(s_const, 1)
                v.memset(c.eps_t[:, :], EPS).then_inc(s_const, 1)
                v.memset(c.minus_1[:, :], -1.0).then_inc(s_const, 1)
                dve.wait_ge(s_iota, 3)
                v.tensor_copy(c.iota[:, :], c.iota_i[:, :]).then_inc(s_const, 1)
                v.tensor_scalar(c.iota1[:, :], c.iota_i[:, :], 1, None, ALU.add).then_inc(s_const, 1)
                v.tensor_scalar(c.iota1_b[:, :], c.iota_i[:, :], 1, None, ALU.add).then_inc(s_const, 1)
                v.tensor_copy(c.part[:, :], c.part_i[:, :]).then_inc(s_const, 1)
                dve.wait_ge(s_const, 9)
                v.tensor_scalar(c.ident[:, :], c.iota[:, :], c.part[:, 0:1], None, ALU.is_equal).then_inc(s_const, 1)
                v.tensor_scalar(c.ident_b[:, :], c.iota[:, :], c.part[:, 0:1], None, ALU.is_equal).then_inc(s_const, 1)
                v.tensor_scalar(c.earlier_b[:, :], c.iota[:, :], c.part[:, 0:1], None, ALU.is_gt).then_inc(s_const, 1)
                dve.wait_ge(s_const, 12)

            @block.scalar
            def _(act):
                def row(ap, n):
                    return ap.rearrange("(a n) -> a n", a=1).to_broadcast([P, n])

                loads = [
                    (c.wf[:, :, :], c.Wf[0:3 * d, :].rearrange("(t p) n -> p t n", p=P)),
                    (c.w4[:, :], c.Wf[3 * d:3 * d + ef, :]),
                    (c.wq[:, :], c.Wq), (c.wk[:, :], c.Wk), (c.wa[:, :], c.Wa),
                    (c.wu[:, :], c.Wu),
                    (c.wnode1[:, 0:2 * hid].rearrange("p (t n) -> p t n", t=2), c.w1.rearrange("(t p) n -> p t n", p=P)),
                    (c.wnode1[:, 2 * hid:], c.conv_w),
                    (c.bias_f[:, :], row(c.bf, d)), (c.bias_u[:, :], row(c.bu, d)),
                    (c.bias_1[:, :], row(c.b1, hid)), (c.bias_c[:, :], row(c.conv_b, d)),
                    (c.w2_row[:, :], row(c.w2.rearrange("n a -> (n a)"), hid)),
                    (c.b2_col[:, :], row(c.b2, 1)),
                ]
                for dest, origin in loads:
                    act.dma_start(dest, origin).then_inc(s_load, 16)
                act.wait_ge(s_load, 16 * len(loads))


def sort_phase(nc, c):
    pl, nb, attr = c.pl, c.nb, c.attr
    C = pl.cols
    whole = pl.full * P
    with Scope(nc, "sort") as s:
        ends = s.sb("ends", [P, 2, C], i32)
        lo = s.sb("lo", [P, 4, C])
        src_hi = s.sb("src_hi", [P, C])
        last_run = s.sb("last_run", [P, 2, nb], i32)
        none = s.sb("none", [P, 2, nb])
        rest = s.sb("rest", [P, 2, nb])
        odd = s.sb("odd", [P, nb], i32)
        half = s.sb("half", [P, C], i32)
        count = s.sb("count", [P, 2, nb])
        tot = s.sb("tot", [P, 2, nb])
        need_i = s.sb("need_i", [P, 2, nb], i32)
        need = s.sb("need", [P, 2, nb])
        upto = s.sb("upto", [P, 2, nb])
        run = s.sb("run", [P, 2, nb])
        NT = pl.map // P
        unit_f = s.sb("unit_f", [P, NT])
        cmp = s.sb("cmp", [P, 2, NT, nb])
        bot = s.sb("bot", [P, 2, NT])
        bot_i = s.sb("bot_i", [P, 2, NT], i32)
        junk = s.sb("junk", [P, C], bf16)
        hot = s.sb("hot", [P, U, 2, G * nb], bf16)
        SLOTS = 4
        rank = s.sb("rank", [P, U, 2, G, nb])
        row_f = s.sb("row_f", [P, U, 2, G])
        row_a = s.sb("row_a", [P, U, 2, G], i32)
        row_b = s.sb("row_b", [P, U, 2, G], i32)
        row_c = s.sb("row_c", [P, U, 2, G], i32)
        row_e = s.sb("row_e", [P, U, 2, G], i32)
        row_i = s.sb("row_i", [P, SLOTS, 2, G], i32)
        edge = s.sb("edge", [P, SLOTS, G, attr])
        pre = [s.bank(f"pre{u}")[:, 0:2 * G * nb].rearrange("p (k n) -> p k n", k=2) for u in range(U)]
        add = [s.bank(f"add{u}")[:, 0:2 * nb].rearrange("p (k n) -> p k n", k=2) for u in range(U)]

        (s_ends, s_tails, s_pad, s_key, s_cnt, s_tot, s_base, s_bot, s_blkw, s_blkr) = s.sems(
            "s_ends s_tails s_pad s_key s_cnt s_tot s_base s_bot s_blkw s_blkr")

        runs = [rows.rearrange("(x r) n -> x (r n)", r=k) for rows, k in zip((c.rows_s, c.rows_d), UNIT)]
        fills = (c.fill_s, c.fill_d)

        with nc.Block() as block:
            @block.sync
            def _(sp):
                sp.wait_ge(s_pad, 1)
                for k, key in enumerate((c.src, c.dst)):
                    sp.dma_start(ends[:, k, 0:pl.full], key[0:whole].rearrange("(p r) -> p r", p=P)).then_inc(s_ends, 16)
                    sp.dma_start(ends[0:pl.rest, k, pl.full:pl.full + 1],
                                 key[whole:].rearrange("(p r) -> p r", r=1)).then_inc(s_ends, 16)
                sp.wait_ge(s_bot, 1)
                for k in range(2):
                    sp.dma_start(c.blk_dram[k, :].rearrange("(p r) -> p r", p=P), bot_i[:, k, :]).then_inc(s_blkw, 16)
                sp.wait_ge(s_blkw, 32)
                sp.dma_start(c.blk[0:1, :, :], c.blk_dram.rearrange("(a k) r -> a k r", a=1)).then_inc(s_blkr, 16)
                sp.wait_ge(s_blkr, 16)

            @block.vector
            def _(dve):
                v = nc.vector
                v.memset(ends[:, :, :], nb * P).then_inc(s_pad, 1)
                v.memset(edge[:, :, :, :], 0.0).then_inc(s_pad, 1)
                dve.wait_ge(s_ends, 64)
                n = 0
                for k in range(2):
                    v.tensor_scalar(half[:, :], ends[:, k, :], 7, None, ALU.logical_shift_right).then_inc(s_key, 1)
                    n += 1
                    dve.wait_ge(s_key, n)
                    v.tensor_copy(src_hi[:, :] if k == 0 else lo[:, 2, :], half[:, :]).then_inc(s_key, 1)
                    n += 1
                    dve.wait_ge(s_key, n)
                    v.tensor_scalar(half[:, :], ends[:, k, :], P - 1, None, ALU.bitwise_and).then_inc(s_key, 1)
                    n += 1
                    dve.wait_ge(s_key, n)
                    v.tensor_copy(lo[:, k, :], half[:, :]).then_inc(s_key, 1)
                    n += 1
                    dve.wait_ge(s_key, n)
                v.tensor_copy(lo[:, 3, :], ends[:, 1, :]).then_inc(s_key, 1)
                v.tensor_scalar(lo[:, 0, :], lo[:, 0, :], 1.0, None, ALU.add).then_inc(s_key, 1)
                m = 0
                with dve.Fori(0, nb) as b:
                    dve.wait_ge(s_cnt, b * 2)
                    v.tensor_scalar(junk[:, :], src_hi[:, :], c.iota[:, bass.ds(b, 1)], None, ALU.is_equal, ALU.add,
                                    accum_out=count[:, 0, bass.ds(b, 1)]).then_inc(s_cnt, 1)
                    dve.wait_ge(s_cnt, b * 2 + 1)
                    v.tensor_scalar(junk[:, :], lo[:, 2, :], c.iota[:, bass.ds(b, 1)], None, ALU.is_equal, ALU.add,
                                    accum_out=count[:, 1, bass.ds(b, 1)]).then_inc(s_cnt, 1)
                dve.wait_ge(s_tot, 1)
                n = 0

                def link(ins):
                    nonlocal n
                    n += 1
                    ins.then_inc(s_base, 1)
                    dve.wait_ge(s_base, n)

                for k in range(2):
                    link(v.tensor_scalar(tot[:, k, :], pre[0][:, k, 0:nb], float(UNIT[k] * P - 1), None, ALU.add))
                link(v.tensor_copy(need_i[:, :, :], tot[:, :, :]))
                for k in range(2):
                    link(v.tensor_scalar(need_i[:, k, :], need_i[:, k, :], (UNIT[k] * P).bit_length() - 1, None,
                                         ALU.logical_shift_right))
                link(v.tensor_copy(need[:, :, :], need_i[:, :, :]))
                for k in range(2):
                    link(v.tensor_tensor_scan(upto[:, k, :], need[:, k, :], c.zeros[:, 0:nb], 0.0, ALU.add, ALU.add))
                link(v.tensor_tensor(run[:, :, :], upto[:, :, :], need[:, :, :], ALU.subtract))
                for k in range(2):
                    link(v.tensor_scalar(run[:, k, :], run[:, k, :], float(UNIT[k] * P), None, ALU.mult))
                link(v.tensor_scalar(none[:, :, :], need[:, :, :], 0.5, None, ALU.is_lt))
                link(v.tensor_scalar(need[:, :, :], upto[:, :, :], -1.0, None, ALU.add))
                for k in range(2):
                    link(v.scalar_tensor_tensor(rest[:, k, :], c.iota[:, 0:nb], float(pl.groups[k] * G // UNIT[k]), need[:, k, :],
                                                ALU.add, ALU.subtract))
                link(v.tensor_tensor(rest[:, :, :], rest[:, :, :], none[:, :, :], ALU.mult))
                link(v.tensor_tensor(need[:, :, :], need[:, :, :], rest[:, :, :], ALU.add))
                link(v.tensor_copy(last_run[:, :, :], need[:, :, :]))
                link(v.tensor_scalar(odd[:, :], last_run[:, 0, :], 1, None, ALU.bitwise_and))
                link(v.tensor_scalar(last_run[:, 0, :], last_run[:, 0, :], 1, 8, ALU.logical_shift_right, ALU.logical_shift_left))
                link(v.tensor_tensor(last_run[:, 0, :], last_run[:, 0, :], odd[:, :], ALU.bitwise_or))
                link(v.tensor_scalar(last_run[:, 1, :], last_run[:, 1, :], 7, None, ALU.logical_shift_left))
                link(v.tensor_copy(unit_f[:, :], c.unit_i[:, :]))
                for k in range(2):
                    link(v.tensor_tensor(cmp[:, k, :, :], unit_f[:, :].unsqueeze(2).to_broadcast([P, NT, nb]),
                                         upto[:, k, :].unsqueeze(1).to_broadcast([P, NT, nb]), ALU.is_ge))
                    link(v.tensor_reduce(bot[:, k, :], cmp[:, k, :, :], AX.X, ALU.add))
                link(v.tensor_scalar(bot[:, :, :], bot[:, :, :], float(nb - 1), None, ALU.min))
                v.tensor_copy(bot_i[:, :, :], bot[:, :, :]).then_inc(s_bot, 1)

            @block.scalar
            def _(act):
                n = 0
                for k in range(2):
                    view = (c.rows_s, c.rows_d)[k][0:pl.rows[k], :].rearrange("(g p r) n -> g p (r n)", p=P, r=G)
                    for g in range(-(-pl.e // (UNIT[k] * P)) * UNIT[k] // G, pl.groups[k]):
                        act.dma_start(view[g, :, :], fills[k][:, :, :].rearrange("p r n -> p (r n)")).then_inc(s_tails, 16)
                        n += 1
                act.wait_ge(s_tails, 16 * n)

            @block.tensor
            def _(pe):
                pe.wait_ge(s_cnt, 2 * nb)
                nc.tensor.matmul(pre[0][:, :, 0:nb], c.ones[:, :], count[:, :, :], start=True, stop=True).then_inc(s_tot, 1)

        (row_cast, rank_a, rank_b, run_ready, hot_ready, prefix_ready, row_bits_b, row_bits_c, row_bits_e, row_ready,
         fields_ready, filled_s, filled_d, pool_step) = s.sems(
            "row_cast rank_a rank_b run_ready hot_ready prefix_ready row_bits_b row_bits_c row_bits_e row_ready "
            "fields_ready filled_s filled_d pool_step")
        edge_in = [s.sem(f"edge_in{q}") for q in range(SLOTS)]
        edge_done = [s.sem(f"edge_done{q}") for q in range(SLOTS)]
        groups = C // G
        LAST = groups - 1
        assert pl.peeled == G - 1

        def fill_padding(eng, key, name, filled):
            reg = eng.alloc_register(name)
            with eng.Fori(0, nb) as b:
                eng.load([reg], last_run[0:1, key, bass.ds(b, 1)])
                first = eng.snap(reg, min_val=0, max_val=runs[key].shape[0] - P * G // UNIT[key])
                eng.dma_start(runs[key][bass.ds(first, P, G // UNIT[key]), :],
                              fills[key][:, 0:UNIT[key], :].rearrange("p r n -> p (r n)")).then_inc(filled, 16)

        with nc.Block() as block:
            attr_v = c.edge_attr[0:whole, :].rearrange("(p r) n -> p (r n)", p=P)

            @block.sync
            def _(sp):
                fill_padding(sp, 0, "last_run_s", filled_s)

                def body(at):
                    q = at.slot(SLOTS)
                    wait(sp, edge_done[q], at.uses(SLOTS, 0, -1) * (16 * G))
                    if at.last:
                        sp.dma_start(edge[:, q, 0:pl.peeled, :].rearrange("p g n -> p (g n)"),
                                     attr_v[:, LAST * G * attr:]).then_inc(edge_in[q], 16)
                        sp.dma_start(edge[0:pl.rest, q, pl.peeled, :], c.edge_attr[whole:, :]).then_inc(edge_in[q], 16)
                    else:
                        sp.dma_start(edge[:, q, :, :].rearrange("p g n -> p (g n)"),
                                     attr_v[:, bass.ds(at.g() * (G * attr), G * attr)]).then_inc(edge_in[q], 16)

                run_groups(sp, groups, 0, body, peel=1)

            @block.vector
            def _(dve):
                v = nc.vector

                def one_hot(at, ahead):
                    u = at.slot(U, ahead)
                    wait(dve, prefix_ready, at.g(ahead + 1 - U))
                    hv = hot[:, u, :, :].rearrange("p k (g b) -> p k g b", b=nb)
                    iota_v = c.iota[:, 0:nb].unsqueeze(1).to_broadcast([P, G, nb])
                    v.tensor_tensor(hv[:, 0, :, :], src_hi[:, at.tiles(ahead)].unsqueeze(2).to_broadcast([P, G, nb]),
                                    iota_v, ALU.is_equal)
                    v.tensor_tensor(hv[:, 1, :, :], lo[:, 2, at.tiles(ahead)].unsqueeze(2).to_broadcast([P, G, nb]),
                                    iota_v, ALU.is_equal).then_inc(hot_ready, 1)

                def rows(at):
                    u, q = at.slot(U), at.slot(SLOTS)
                    dve.wait_ge(prefix_ready, at.g(1))
                    wait(dve, run_ready, at.g(0))
                    v.tensor_tensor(rank[:, u, :, :, :], pre[u][:, :, :].rearrange("p k (g b) -> p k g b", b=nb),
                                    run[:, :, :].unsqueeze(2).to_broadcast([P, 2, G, nb]), ALU.add).then_inc(rank_a, 1)
                    dve.wait_ge(rank_a, at.g(1))
                    v.tensor_tensor(run[:, :, :], run[:, :, :], add[u][:, :, :], ALU.add).then_inc(run_ready, 1)
                    v.tensor_tensor(rank[:, u, :, :, :].rearrange("p k g b -> p k (g b)"),
                                    rank[:, u, :, :, :].rearrange("p k g b -> p k (g b)"), hot[:, u, :, :],
                                    ALU.mult).then_inc(rank_b, 1)
                    dve.wait_ge(rank_b, at.g(1))
                    v.tensor_reduce(row_f[:, u, :, :], rank[:, u, :, :, :], AX.X, ALU.add).then_inc(row_cast, 1)
                    if at.has(2):
                        one_hot(at, 2)
                    dve.wait_ge(row_cast, at.g(0) * 2 + 1)
                    if at.last:
                        v.tensor_scalar(rank[:, u, 0, 0, 0:1], src_hi[:, C - 1:C], float(nb), float(FAR),
                                        ALU.is_ge, ALU.mult).then_inc(rank_b, 1)
                        dve.wait_ge(rank_b, at.g(2))
                        v.tensor_tensor(row_f[:, u, 0, G - 1:G], row_f[:, u, 0, G - 1:G], rank[:, u, 0, 0, 0:1],
                                        ALU.add).then_inc(rank_b, 1)
                        dve.wait_ge(rank_b, at.g(3))
                    v.tensor_copy(row_a[:, u, :, :], row_f[:, u, :, :]).then_inc(row_cast, 1)
                    dve.wait_ge(row_cast, at.g(0) * 2 + 2)
                    v.tensor_scalar(row_b[:, u, :, :], row_a[:, u, :, :], P - 1, 2, ALU.bitwise_and,
                                    ALU.logical_shift_left).then_inc(row_bits_b, 1)
                    v.tensor_scalar(row_c[:, u, :, :], row_a[:, u, :, :], 7, G - 1, ALU.logical_shift_right,
                                    ALU.bitwise_and).then_inc(row_bits_c, 1)
                    v.tensor_scalar(row_e[:, u, :, :], row_a[:, u, :, :], (FAR - 1) * 2 + 1 - (G * P - 1), None,
                                    ALU.bitwise_and).then_inc(row_bits_e, 1)
                    dve.wait_ge(row_bits_c, at.g(1))
                    v.tensor_tensor(row_b[:, u, :, :], row_b[:, u, :, :], row_c[:, u, :, :], ALU.bitwise_or).then_inc(row_bits_b, 1)
                    dve.wait_ge(row_bits_b, at.g(0) * 2 + 2)
                    wait(dve, edge_done[q], at.uses(SLOTS, 0, -1) * (16 * G))
                    v.tensor_tensor(row_i[:, q, :, :], row_b[:, u, :, :], row_e[:, u, :, :], ALU.bitwise_or).then_inc(row_ready, 1)

                def body(at):
                    if at.has(0):
                        rows(at)
                    else:
                        one_hot(at, 2)

                run_groups(dve, groups, 2, body, peel=1)

            @block.tensor
            def _(pe):
                t = nc.tensor

                def body(at):
                    u = at.slot(U)
                    pe.wait_ge(hot_ready, at.g(1))
                    wait(pe, run_ready, at.g(1 - U))
                    t.matmul(pre[u][:, :, :], c.earlier_b[:, :], hot[:, u, :, :], start=True, stop=False)
                    for k in range(1, G):
                        t.matmul(pre[u][:, :, k * nb:], c.ones_b[:, :], hot[:, u, :, 0:(G - k) * nb],
                                 start=False, stop=(k == G - 1))
                    for k in range(G):
                        last = t.matmul(add[u][:, :, :], c.ones_b[:, :], hot[:, u, :, k * nb:(k + 1) * nb],
                                        start=(k == 0), stop=(k == G - 1))
                    last.then_inc(prefix_ready, 1)

                run_groups(pe, groups, 0, body)

            @block.scalar
            def _(act):
                fill_padding(act, 1, "last_run_d", filled_d)

                def body(at):
                    q = at.slot(SLOTS)
                    act.wait_ge(edge_in[q], at.uses(SLOTS) * 16 + (16 if at.last else 0))
                    nc.scalar.activation(edge[:, q, :, SRC_1:DROW],
                                         lo[:, :, at.tiles()].rearrange("p f g -> p g f"), ACT.Copy)
                    act.wait_ge(row_ready, at.g(1))
                    nc.scalar.activation(edge[:, q, :, DROW], row_i[:, q, 1, :], ACT.Copy).then_inc(fields_ready, 1)

                run_groups(act, groups, 0, body, peel=1)
                act.wait_ge(filled_d, nb * 16)

            @block.gpsimd
            def _(pool):
                limit = pool.to_reg(pl.rows[0] - 1)
                pool.wait_ge(filled_s, nb * 16)

                def body(at):
                    q = at.slot(SLOTS)
                    pool.wait_ge(fields_ready, at.g(1))
                    pool.sem_inc(pool_step, 1)
                    for j in range(G):
                        nc.gpsimd.indirect_dma_start(
                            c.rows_s[0:pl.rows[0], :], bass.IndirectOffsetOnAxis(row_i[:, q, 0, j:j + 1], 0), edge[:, q, j, :], None,
                            bounds_check=limit, oob_is_err=False).then_inc(edge_done[q], 16)

                run_groups(pool, groups, 0, body)
                for q in range(SLOTS):
                    pool.wait_ge(edge_done[q], -(-(groups - q) // SLOTS) * 16 * G)


class At:

    def __init__(self, i, u, groups=None):
        self.i, self.u, self.groups = i, u, groups
        self.last = groups is not None and u == groups - 1

    def has(self, ahead):
        return self.groups is None or 0 <= self.u + ahead < self.groups

    def g(self, k=0):
        return self.i * UB + (self.u + k)

    def slot(self, slots, ahead=0):
        return (self.u + ahead) % slots

    def tiles(self, ahead=0):
        return bass.ds(self.i * (UB * G) + (self.u + ahead) * G, G)

    def tile(self, j, ahead=0):
        return bass.ds(self.i * (UB * G) + (self.u + ahead) * G + j, 1)

    def uses(self, slots, ahead=0, k=0):
        return self.i * (UB // slots) + ((self.u + ahead) // slots + 1 + k)


def run_groups(eng, groups, lead, body, peel=0):
    for u in range(-lead, FIRST):
        body(At(0, u, groups))
    loops = (groups - max(lead, peel) - FIRST) // UB
    with eng.Fori(0, loops) as i:
        for u in range(FIRST, FIRST + UB):
            body(At(i, u))
    for u in range(FIRST + loops * UB, groups):
        body(At(0, u, groups))


def wait(eng, sem, value):
    if not isinstance(value, int) or value > 0:
        eng.wait_ge(sem, value)


def split_bf16(dve, v, rest, parts, sem, n):
    v.tensor_copy(parts[0], rest).then_inc(sem, 1)
    dve.wait_ge(sem, n + 1)
    v.tensor_tensor(rest, rest, parts[0], ALU.subtract).then_inc(sem, 1)
    dve.wait_ge(sem, n + 2)
    v.tensor_copy(parts[1], rest).then_inc(sem, 1)
    dve.wait_ge(sem, n + 3)
    v.tensor_tensor(parts[2], rest, parts[1], ALU.subtract).then_inc(sem, 1)


def load_x(nc, c, tag, dest):
    whole = c.LAST * P
    with Scope(nc, f"load{tag}") as s:
        s_zero, s_x = s.sems("s_zero s_x")
        with nc.Block() as block:
            @block.vector
            def _(dve):
                nc.vector.memset(dest[:, c.LAST, :], 0.0).then_inc(s_zero, 1)

            @block.sync
            def _(sp):
                XB = 12
                x_v = c.x[0:whole, :].rearrange("(b p) n -> p b n", p=P)
                for b in range(0, c.LAST, XB):
                    sp.dma_start(dest[:, b:b + XB, :], x_v[:, b:b + XB, :]).then_inc(s_x, 16)
                sp.wait_ge(s_zero, 1)
                sp.dma_start(dest[0:c.pl.tail, c.LAST, :], c.x[whole:, :]).then_inc(s_x, 16)
                sp.wait_ge(s_x, 16 * (c.LAST // XB + 1))


def normalise(nc, c, tag, x):
    nb, d = c.nb, c.d
    with Scope(nc, f"norm{tag}") as s:
        s_step, s_var, s_std = s.sems("s_step s_var s_std")

        def wide(ap):
            return ap.unsqueeze(2).to_broadcast([P, nb, d])

        with nc.Block() as block:
            @block.vector
            def _(dve):
                v = nc.vector
                n = 0

                def link(ins):
                    nonlocal n
                    n += 1
                    ins.then_inc(s_step, 1)
                    dve.wait_ge(s_step, n)

                mean, var, rstd = c.stat[:, 0, :], c.stat[:, 1, :], c.stat[:, 2, :]
                link(v.tensor_reduce(mean, x, AX.X, ALU.add))
                link(v.tensor_scalar(mean, mean, 1.0 / d, None, ALU.mult))
                link(v.tensor_tensor(c.hn[:, :, :], x, wide(mean), ALU.subtract))
                link(v.tensor_tensor(c.accd, c.hn[:, :, :], c.hn[:, :, :], ALU.mult))
                v.tensor_reduce(var, c.accd, AX.X, ALU.add).then_inc(s_var, 1)
                dve.wait_ge(s_std, 1)
                link(v.reciprocal(rstd, var))
                v.scalar_tensor_tensor(c.hn[:, :, :], c.hn[:, :, :], 0.0, wide(rstd), ALU.max,
                                       ALU.mult).then_inc(s_step, 1)
                dve.wait_ge(s_step, n + 1)

            @block.scalar
            def _(act):
                var = c.stat[:, 1, :]
                act.wait_ge(s_var, 1)
                nc.scalar.activation(var, var, ACT.Sqrt, bias=c.eps_t[:, 0:1], scale=1.0 / d).then_inc(s_std, 1)


def project(nc, c, tag, weights, width, take_dve, take_act, store=None):
    nb, d = c.nb, c.d
    L = nb // U
    with Scope(nc, f"project{tag}") as s:
        copy = s.sb("copy", [P, U, d])
        turned_sb = s.sb("turned_sb", [P, U, P])
        ps_t = [s.bank(f"ps_t{u}") for u in range(U)]
        ps_n = [s.bank(f"ps_n{u}") for u in range(U)]
        s.tmp = s.sb("tmp", [P, U, 256])
        s.keep = s.sb("keep", [P, U, d])
        (copied, turned, turned_copied, projected, s.taken, s.kept, s.step, s.out0, s.out1) = s.sems(
            "copied turned turned_copied projected block_taken block_kept split_step out0 out1")
        with nc.Block() as block:
            def run(eng, body):
                assert nb % U == 1
                with eng.Fori(0, L) as i:
                    for u in range(U):
                        body(bass.ds(i * U + u, 1), u, lambda k, i=i, u=u: i * U + (u + k), i)
                body(slice(nb - 1, nb), 0, lambda k: nb - 1 + k, L)

            @block.scalar
            def _(act):
                act.sem_inc(turned, U)
                act.sem_inc(projected, U)

                def body(b, u, g, i):
                    act.wait_ge(turned, g(1))
                    nc.scalar.activation(copy[:, u, :], c.hn[:, b, :], ACT.Copy).then_inc(copied, 1)
                    act.wait_ge(turned, g(1 + U))
                    nc.scalar.activation(turned_sb[:, u, :], ps_t[u][:, 0:P], ACT.Copy).then_inc(turned_copied, 1)
                    act.wait_ge(s.taken, g(1 + U))
                    take_act(s, act, b, u, g, i, ps_n[u])

                run(act, body)

            @block.tensor
            def _(pe):
                pe.sem_inc(s.taken, U)
                pe.sem_inc(s.kept, U)

                def body(b, u, g, i):
                    pe.wait_ge(copied, g(1))
                    nc.tensor.transpose(ps_t[u][:, 0:P], copy[:, u, :], c.ident[:, :]).then_inc(turned, 1)
                    pe.wait_ge(turned_copied, g(1))
                    pe.wait_ge(s.taken, g(1))
                    pe.wait_ge(s.kept, g(1))
                    nc.tensor.matmul(ps_n[u][:, 0:width], turned_sb[:, u, :], weights, start=True,
                                     stop=True).then_inc(projected, 1)

                run(pe, body)

            @block.vector
            def _(dve):
                def body(b, u, g, i):
                    dve.wait_ge(projected, g(1 + U))
                    take_dve(s, dve, b, u, g, i, ps_n[u])

                run(dve, body)

            @block.sync
            def _(sp):
                if store is not None:
                    def body(b, u, g, i):
                        sp.wait_ge(s.kept, g(1 + U))
                        store(s, sp, b, u, g, i).then_inc((s.out0, s.out1)[u], 16)

                    run(sp, body)
                    sp.wait_ge(s.out0, 16 * (L + 1))
                    sp.wait_ge(s.out1, 16 * L)


def rows_of(b, width=1):
    if isinstance(b, slice):
        return slice(b.start * width, b.stop * width)
    return bass.ds(b.start * width, width)


def layer0_nodes(nc, c):
    nb, d = c.nb, c.d
    load_x(nc, c, "0", c.accd)
    normalise(nc, c, "0", c.accd)
    with Scope(nc, "fold") as s:
        ps_w = s.bank("ps_w")
        s_w, s_turn, s_m = s.sems("s_w s_turn s_m")
        with nc.Block() as block:
            @block.tensor
            def _(pe):
                nc.tensor.transpose(ps_w[:, 0:P], c.wq[:, :], c.ident[:, :])
                nc.tensor.transpose(ps_w[:, P:2 * P], c.wk[:, :], c.ident[:, :]).then_inc(s_turn, 1)
                pe.wait_ge(s_w, 4)
                nc.tensor.matmul(ps_w[:, 2 * P:3 * P], c.wqkT[:, 0, :], c.wqkT[:, 1, :], start=True,
                                 stop=True).then_inc(s_m, 1)

            @block.vector
            def _(dve):
                v = nc.vector
                v.tensor_scalar(c.bias_f[:, :], c.bias_f[:, :], 1.0, None, ALU.add)
                v.tensor_tensor(c.wnode[:, 0:d], c.wf[:, 0, :], c.wf[:, 2, :], ALU.add).then_inc(s_w, 1)
                v.tensor_tensor(c.wnode[:, 2 * d:3 * d], c.wf[:, 1, :], c.wf[:, 2, :], ALU.subtract).then_inc(s_w, 1)
                dve.wait_ge(s_turn, 1)
                v.tensor_scalar(c.wqkT[:, 0, :], ps_w[:, 0:P], c.wa[:, 0:1], float(d) ** -0.5, ALU.mult,
                                ALU.mult).then_inc(s_w, 1)
                v.tensor_copy(c.wqkT[:, 1, :], ps_w[:, P:2 * P]).then_inc(s_w, 1)
                dve.wait_ge(s_m, 1)
                v.tensor_copy(c.wnode[:, d:2 * d], ps_w[:, 2 * P:3 * P]).then_inc(s_w, 1)
                dve.wait_ge(s_w, 5)

    STEPS = 6

    def take_dve(s, dve, b, u, g, i, ps):
        v = nc.vector
        n = g(0) * STEPS
        v.tensor_tensor(s.tmp[:, u, 0:d], ps[:, 0:d], c.bias_f[:, :], ALU.add).then_inc(s.step, 1)
        v.tensor_copy(s.tmp[:, u, d:2 * d], ps[:, d:2 * d]).then_inc(s.taken, 1)
        dve.wait_ge(s.step, n + 1)
        dve.wait_ge(s.taken, g(1 + U))
        row = rows_of(b, 3 * c.AGW)
        part = [c.lut[:, bass.ds(row.start + k * c.AGW, c.AGW)] if not isinstance(row, slice)
                else c.lut[:, row.start + k * c.AGW:row.start + (k + 1) * c.AGW] for k in range(3)]
        split_bf16(dve, v, s.tmp[:, u, :], part, s.step, n + 1)
        dve.wait_ge(s.step, n + 5)
        dve.sem_inc(s.step, 1)

    def take_act(s, act, b, u, g, i, ps):
        act.wait_ge((s.out0, s.out1)[u], i * 16)
        nc.scalar.activation(s.keep[:, u, :], ps[:, 2 * d:3 * d], ACT.Copy).then_inc(s.kept, 1)

    def store(s, sp, b, u, g, i):
        return sp.dma_start(c.tab_b[rows_of(b, P), :], s.keep[:, u, :])

    project(nc, c, "0", c.wnode[:, :], 3 * d, take_dve, take_act, store)


def load_blocks(eng, c, key, at, ahead, regs):
    n = len(regs)
    eng.load(regs, c.blk[0:1, key, bass.ds(at.g(ahead) * n, n)])
    return [eng.snap(r, min_val=0, max_val=c.nb - 1) for r in regs]


def source_hots(c, out, at, ahead):
    for j in range(G):
        last = c.nc.vector.tensor_scalar(out[:, j, :], c.iota1_b[:, :], c.meta[:, at.tile(j, ahead), 0],
                                         None, ALU.is_equal)
    return last


def turn(c, ps, hot):
    for j in range(G):
        last = c.nc.tensor.transpose(ps[:, j * P:(j + 1) * P], hot[:, j, :], c.ident_b[:, :])
    return last


def group_rows(rows, at):
    view = rows.rearrange("(g p r) n -> g p (r n)", p=P, r=G)
    return view[bass.ds(at.g(), 1), :, :].rearrange("a p n -> (a p) n")


def layer0_edges(nc, c):
    pl, nb, d, ef, attr = c.pl, c.nb, c.d, c.ef, c.attr
    ZW, AGW = c.ZW, c.AGW
    groups = pl.groups[0]
    PER = G // UNIT[0]
    with Scope(nc, "layer0") as s:
        row = s.sb("row", [P, 4, G, attr])
        want = s.sb("want", [P, 4, G], i32)
        source = s.sb("source", [P, 4, G])
        hot = s.sb("hot", [P, 4, G, P])
        hot_t = s.sb("hot_t", [P, 2, G * P], bf16)
        attr_t = s.sb("attr_t", [ef, 2, G * P])
        bt = s.sb("bt", [P, 4, G, d])
        pre = s.sb("pre", [P, 2, G, d])
        feat = s.sb("feat", [P, 2, G, d])
        z = s.sb("z", [P, 2, G, ZW])
        dot = s.sb("dot", [P, 2, G])
        e_att = s.sb("e_att", [P, 2, G])
        e_minus = s.sb("e_minus", [P, 2, G])
        ps_ag = [s.bank(f"ps_ag{u}", 2)[:, :].rearrange("p (g n) -> p g n", g=G) for u in range(2)]
        ps_hot = s.bank("ps_hot")
        ps_attr = s.bank("ps_attr")
        ps_sum = [s.bank(f"ps_sum{u}") for u in range(2)]
        row_in = [s.sem(f"row_in{q}") for q in range(4)]
        b_in = [s.sem(f"b_in{q}") for q in range(4)]
        (zeroed, fields_ready, source_ready, hot_ready, turned, attr_turned, hot_t_ready, attr_t_ready, ag_ready,
         pre_ready, ex_ready, feat_ready, prod_ready, dot_ready, att_ready, e_ready, e_minus_ready, z_ready,
         sums_ready, added, gather_step) = s.sems(
            "zeroed fields_ready source_ready hot_ready turned attr_turned hot_t_ready attr_t_ready ag_ready "
            "pre_ready ex_ready feat_ready prod_ready dot_ready att_ready e_ready e_minus_ready z_ready "
            "sums_ready added gather_step")

        with nc.Block() as block:
            @block.sync
            def _(sp):
                def body(at):
                    q = at.slot(4)
                    wait(sp, fields_ready, at.g(1 - 4))
                    wait(sp, attr_turned, at.g(1 - 4))
                    wait(sp, source_ready, at.g(1 - 4))
                    sp.dma_start(row[:, q, :, :].rearrange("p g n -> p (g n)"), group_rows(c.rows_s[0:pl.rows[0], :], at)).then_inc(row_in[q], 16)

                run_groups(sp, groups, 0, body)

            @block.gpsimd
            def _(pool):
                limit = pool.to_reg(pl.n - 1)

                def body(at):
                    q = at.slot(4)
                    pool.wait_ge(fields_ready, at.g(1))
                    wait(pool, pre_ready, at.g(1 - 4))
                    pool.sem_inc(gather_step, 1)
                    for j in range(G):
                        nc.gpsimd.indirect_dma_start(
                            bt[:, q, j, :], None, c.tab_b[0:pl.n, :],
                            bass.IndirectOffsetOnAxis(want[:, q, j:j + 1], 0),
                            bounds_check=limit, oob_is_err=False).then_inc(b_in[q], 16)

                run_groups(pool, groups, 0, body)

            @block.scalar
            def _(act):
                a = nc.scalar

                def exponential(at, ahead):
                    t = at.slot(2, ahead)
                    act.wait_ge(pre_ready, at.g(ahead + 1))
                    wait(act, prod_ready, at.g(ahead + 1 - 2))
                    wait(act, z_ready, at.g(ahead + 1 - 2))
                    a.activation(feat[:, t, :, :], pre[:, t, :, :], ACT.Exp, bias=c.minus_1[:, 0:1]).then_inc(ex_ready, 1)

                def evacuate_hot(at, ahead):
                    act.wait_ge(turned, at.g(ahead + 1))
                    wait(act, ag_ready, at.g(ahead + 1 - 2))
                    a.activation(hot_t[:, at.slot(2, ahead), :], ps_hot[:, :], ACT.Copy).then_inc(hot_t_ready, 1)

                def evacuate_attr(at, ahead):
                    act.wait_ge(attr_turned, at.g(ahead + 1))
                    a.activation(attr_t[:, at.slot(2, ahead), :], ps_attr[0:ef, :], ACT.Copy).then_inc(attr_t_ready, 1)

                def fields(at, ahead):
                    q = at.slot(4, ahead)
                    act.wait_ge(row_in[q], at.uses(4, ahead) * 16)
                    wait(act, pre_ready, at.g(ahead + 1 - 4))
                    a.activation(want[:, q, :], row[:, q, :, DST], ACT.Copy)
                    a.activation(c.meta[:, at.tiles(ahead), :], row[:, q, :, SRC_1:DST_HI + 1], ACT.Copy)
                    a.activation(c.where[:, :, at.tiles(ahead)], row[:, q, :, DST:DROW + 1].rearrange("p g f -> p f g"),
                                 ACT.Copy).then_inc(fields_ready, 1)

                def attention(at, ahead):
                    t, n = at.slot(2, ahead), at.g(ahead + 1)
                    act.wait_ge(dot_ready, n)
                    wait(act, sums_ready, at.g(ahead + 1 - 2))
                    a.activation(z[:, t, :, d], dot[:, t, :], ACT.Tanh).then_inc(att_ready, 1)
                    act.wait_ge(att_ready, n)
                    a.activation(e_att[:, t, :], z[:, t, :, d], ACT.Exp).then_inc(e_ready, 1)
                    act.wait_ge(e_ready, n)
                    a.activation(e_minus[:, t, :], e_att[:, t, :], ACT.Copy, scale=-1.0).then_inc(e_minus_ready, 1)
                    act.wait_ge(e_minus_ready, n)
                    for j in range(G):
                        last = a.activation(z[:, t, j, 0:d], feat[:, t, j, :], ACT.Identity,
                                            bias=e_minus[:, t, j:j + 1], scale=e_att[:, t, j:j + 1])
                    last.then_inc(z_ready, 1)

                def body(at):
                    if at.has(1):
                        attention(at, 1)
                    if at.has(4):
                        evacuate_hot(at, 4)
                        evacuate_attr(at, 4)
                    if at.has(3):
                        exponential(at, 3)
                    if at.has(6):
                        fields(at, 6)

                run_groups(act, groups, 6, body)

            @block.vector
            def _(dve):
                v = nc.vector
                regs = [dve.alloc_register(f"dve_blk{j}") for j in range(PER)]

                def add_sums(at):
                    blocks = load_blocks(dve, c, 0, at, 0, regs)
                    dve.wait_ge(sums_ready, at.g(1))
                    for j in range(PER):
                        dve.wait_ge(added, at.g() * PER + (j + 1))
                        dest = c.acc[:, bass.ds(blocks[j] * ZW, ZW)]
                        v.tensor_tensor(dest, dest, ps_sum[at.slot(2)][:, j * ZW:(j + 1) * ZW], ALU.add).then_inc(added, 1)

                def arguments(at, ahead):
                    t, q = at.slot(2, ahead), at.slot(4, ahead)
                    dve.wait_ge(b_in[q], at.uses(4, ahead) * (16 * G))
                    dve.wait_ge(ag_ready, at.g(ahead + 1))
                    wait(dve, dot_ready, at.g(ahead + 1 - 2))
                    v.tensor_tensor(pre[:, t, :, :], ps_ag[t][:, :, 0:d], bt[:, q, :, :], ALU.add).then_inc(pre_ready, 1)

                def features(at, ahead):
                    t = at.slot(2, ahead)
                    dve.wait_ge(ex_ready, at.g(ahead + 1))
                    v.scalar_tensor_tensor(feat[:, t, :, :], feat[:, t, :, :], 1.0, pre[:, t, :, :], ALU.min,
                                           ALU.max).then_inc(feat_ready, 1)
                    dve.wait_ge(feat_ready, at.g(ahead + 1))
                    v.scalar_tensor_tensor(pre[:, t, :, :], feat[:, t, :, :], 1.0, ps_ag[t][:, :, d:2 * d],
                                           ALU.subtract, ALU.mult).then_inc(prod_ready, 1)
                    dve.wait_ge(prod_ready, at.g(ahead + 1))
                    wait(dve, att_ready, at.g(ahead + 1 - 2))
                    v.tensor_reduce(dot[:, t, :], pre[:, t, :, :], AX.X, ALU.add).then_inc(dot_ready, 1)

                def hots(at, ahead):
                    q = at.slot(4, ahead)
                    dve.wait_ge(row_in[q], at.uses(4, ahead) * 16)
                    wait(dve, sums_ready, at.g(ahead + 1 - 4))
                    v.scalar_tensor_tensor(source[:, q, :], row[:, q, :, 0], 8.0, row[:, q, :, SRC_1], ALU.is_lt,
                                           ALU.mult).then_inc(source_ready, 1)
                    dve.wait_ge(source_ready, at.g(ahead + 1))
                    for j in range(G):
                        last = v.tensor_scalar(hot[:, q, j, :], c.iota1[:, :], source[:, q, j:j + 1], None, ALU.is_equal)
                    last.then_inc(hot_ready, 1)

                def body(at):
                    if at.has(0):
                        add_sums(at)
                    if at.has(3):
                        arguments(at, 3)
                    if at.has(2):
                        features(at, 2)
                    if at.has(5):
                        hots(at, 5)

                v.memset(c.acc[:, :], 0.0).then_inc(added, 1)
                run_groups(dve, groups, 5, body)
                dve.wait_ge(added, groups * PER + 1)

            @block.tensor
            def _(pe):
                t_ = nc.tensor
                regs = [pe.alloc_register(f"pe_blk{j}") for j in range(PER)]

                def turn_group(at, ahead):
                    q = at.slot(4, ahead)
                    pe.wait_ge(row_in[q], at.uses(4, ahead) * 16)
                    wait(pe, attr_t_ready, at.g(ahead))
                    for j in range(G):
                        last = t_.transpose(ps_attr[0:ef, j * P:(j + 1) * P], row[:, q, j, 0:ef], c.ident[:, :])
                    last.then_inc(attr_turned, 1)
                    pe.wait_ge(hot_ready, at.g(ahead + 1))
                    wait(pe, hot_t_ready, at.g(ahead))
                    for j in range(G):
                        last = t_.transpose(ps_hot[:, j * P:(j + 1) * P], hot[:, q, j, :], c.ident[:, :])
                    last.then_inc(turned, 1)

                def look_up(at, ahead):
                    t = at.slot(2, ahead)
                    blocks = load_blocks(pe, c, 0, at, ahead, regs)
                    pe.wait_ge(hot_t_ready, at.g(ahead + 1))
                    pe.wait_ge(attr_t_ready, at.g(ahead + 1))
                    wait(pe, prod_ready, at.g(ahead + 1 - 2))
                    for j in range(G):
                        for k in range(3):
                            t_.matmul(ps_ag[t][:, j, :], hot_t[:, t, j * P:(j + 1) * P],
                                      c.lut[:, bass.ds(blocks[j // UNIT[0]] * (3 * AGW) + k * AGW, AGW)],
                                      start=(k == 0), stop=False)
                        last = t_.matmul(ps_ag[t][:, j, 0:d], attr_t[:, t, j * P:(j + 1) * P], c.w4[:, :],
                                         start=False, stop=True)
                    last.then_inc(ag_ready, 1)

                def sum_up(at, ahead):
                    t, q = at.slot(2, ahead), at.slot(4, ahead)
                    pe.wait_ge(z_ready, at.g(ahead + 1))
                    wait(pe, added, at.g(ahead + 1 - 2) * PER + 1 if at.groups is None or at.u + ahead >= 2 else 0)
                    for j in range(G):
                        b, k = j // UNIT[0], j % UNIT[0]
                        last = t_.matmul(ps_sum[t][:, b * ZW:(b + 1) * ZW], hot[:, q, j, :], z[:, t, j, :],
                                         start=(k == 0), stop=(k == UNIT[0] - 1))
                    last.then_inc(sums_ready, 1)

                def body(at):
                    if at.has(1):
                        sum_up(at, 1)
                    if at.has(4):
                        look_up(at, 4)
                    if at.has(5):
                        turn_group(at, 5)

                run_groups(pe, groups, 5, body)


def layer0_update(nc, c):
    nb, d, hid = c.nb, c.d, c.hid
    load_x(nc, c, "1", c.xn)
    with Scope(nc, "update") as s:
        s_step, s_exp = s.sems("s_step s_exp")
        with nc.Block() as block:
            @block.scalar
            def _(act):
                nc.scalar.activation(c.stat[:, 3, :], c.acc3[:, :, d], ACT.Exp, scale=-1.0).then_inc(s_exp, 1)

            @block.vector
            def _(dve):
                v = nc.vector
                v.tensor_tensor(c.xn[:, :, :], c.xn[:, :, :],
                                c.bias_u[:, :].unsqueeze(1).to_broadcast([P, nb, d]), ALU.add)
                dve.wait_ge(s_exp, 1)
                v.tensor_tensor(c.acc3[:, :, 0:d], c.acc3[:, :, 0:d],
                                c.stat[:, 3, :].unsqueeze(2).to_broadcast([P, nb, d]), ALU.mult).then_inc(s_step, 1)
                dve.wait_ge(s_step, 1)
                v.tensor_tensor(c.hn[:, :, :], c.hn[:, :, :], c.acc3[:, :, 0:d], ALU.add).then_inc(s_step, 1)
                dve.wait_ge(s_step, 2)

    def add_x(s, dve, b, u, g, i, ps):
        nc.vector.tensor_tensor(c.xn[:, b, :], c.xn[:, b, :], ps[:, 0:d].unsqueeze(1), ALU.add).then_inc(s.taken, 1)

    def nothing(s, act, b, u, g, i, ps):
        act.sem_inc(s.kept, 1)

    project(nc, c, "u", c.wu[:, :], d, add_x, nothing)
    normalise(nc, c, "1", c.xn[:, :, :])

    STEPS = 6

    def take_dve(s, dve, b, u, g, i, ps):
        v = nc.vector
        n = g(0) * STEPS
        v.tensor_tensor(s.tmp[:, u, 0:hid], ps[:, 0:hid], c.bias_1[:, :], ALU.add).then_inc(s.step, 1)
        v.tensor_copy(c.hn[:, b, :], ps[:, 2 * hid:2 * hid + d].unsqueeze(1)).then_inc(s.taken, 1)
        dve.wait_ge(s.step, n + 1)
        row = rows_of(b, 3 * hid)
        part = [c.lut[:, bass.ds(row.start + k * hid, hid)] if not isinstance(row, slice)
                else c.lut[:, row.start + k * hid:row.start + (k + 1) * hid] for k in range(3)]
        split_bf16(dve, v, s.tmp[:, u, 0:hid], part, s.step, n + 1)
        dve.wait_ge(s.step, n + 5)
        dve.sem_inc(s.step, 1)

    def take_act(s, act, b, u, g, i, ps):
        act.wait_ge((s.out0, s.out1)[u], i * 16)
        nc.scalar.activation(s.keep[:, u, 0:hid], ps[:, hid:2 * hid], ACT.Copy).then_inc(s.kept, 1)

    def store(s, sp, b, u, g, i):
        return sp.dma_start(c.tab_q[rows_of(b, P), :], s.keep[:, u, 0:hid])

    project(nc, c, "1", c.wnode1[:, :], 2 * hid + d, take_dve, take_act, store)


def weights_pass(nc, c):
    pl, nb, d, hid = c.pl, c.nb, c.d, c.hid
    groups = pl.groups[0]
    PER = G // UNIT[0]
    with Scope(nc, "weights") as s:
        want = s.sb("want", [P, 4, G], i32)
        hot = s.sb("hot", [P, 2, G, P], bf16)
        hot_t = s.sb("hot_t", [P, 2, G * P], bf16)
        qt = s.sb("qt", [P, 4, G, hid])
        pre = s.sb("pre", [P, 2, G, hid])
        act_h = s.sb("act_h", [P, 2, G, hid])
        half_tanh = s.sb("half_tanh", [P, 2, G])
        weight = s.sb("weight", [P, 2, G])
        b2_half = s.sb("b2_half", [P, 1])
        hot_lo = s.sb("hot_lo", [P, 2, G, P])
        hot_hi = s.sb("hot_hi", [P, 2, G, nb])
        ps_p = [s.bank(f"ps_p{u}")[:, 0:G * hid].rearrange("p (g n) -> p g n", g=G) for u in range(2)]
        ps_hot = s.bank("ps_hot", 1, bf16)
        ps_deg = s.bank("ps_deg")
        q_in = [s.sem(f"q_in{q}") for q in range(4)]
        (half_ready, hot_ready, turned, hot_t_ready, want_ready, p_ready, pre_ready, gelu_ready, prod_ready,
         logit_ready, tanh_ready, weight_ready, hi_ready, summed, sigmoid_ready, gather_step) = s.sems(
            "half_ready hot_ready turned hot_t_ready want_ready p_ready pre_ready gelu_ready prod_ready "
            "logit_ready tanh_ready weight_ready hi_ready summed sigmoid_ready gather_step")

        with nc.Block() as block:
            @block.gpsimd
            def _(pool):
                limit = pool.to_reg(pl.n - 1)

                def body(at):
                    q = at.slot(4)
                    pool.wait_ge(want_ready, at.g(1))
                    wait(pool, pre_ready, at.g(1 - 4))
                    pool.sem_inc(gather_step, 1)
                    for j in range(G):
                        nc.gpsimd.indirect_dma_start(
                            qt[:, q, j, :], None, c.tab_q[0:pl.n, :],
                            bass.IndirectOffsetOnAxis(want[:, q, j:j + 1], 0),
                            bounds_check=limit, oob_is_err=False).then_inc(q_in[q], 16)

                run_groups(pool, groups, 0, body)

            @block.scalar
            def _(act):
                a = nc.scalar

                def body(at):
                    if at.has(0):
                        act.wait_ge(logit_ready, at.g(1))
                        wait(act, weight_ready, at.g(1 - 2))
                        a.activation(half_tanh[:, at.slot(2), :], c.ew[:, at.tiles()], ACT.Tanh, bias=b2_half[:, 0:1],
                                     scale=0.5).then_inc(tanh_ready, 1)
                    if at.has(2):
                        act.wait_ge(pre_ready, at.g(3))
                        wait(act, logit_ready, at.g(3 - 2))
                        a.activation(act_h[:, at.slot(2, 2), :, :], pre[:, at.slot(2, 2), :, :], ACT.Gelu).then_inc(gelu_ready, 1)
                    if at.has(4):
                        act.wait_ge(turned, at.g(5))
                        wait(act, p_ready, at.g(5 - 2))
                        a.activation(hot_t[:, at.slot(2, 4), :], ps_hot[:, 0:G * P], ACT.Copy).then_inc(hot_t_ready, 1)
                    if at.has(5):
                        wait(act, pre_ready, at.g(6 - 4))
                        a.activation(want[:, at.slot(4, 5), :], c.where[:, 0, at.tiles(5)], ACT.Copy).then_inc(want_ready, 1)

                act.wait_ge(half_ready, 1)
                run_groups(act, groups, 5, body)
                act.wait_ge(weight_ready, groups)
                a.activation(c.ew[:, :], c.ew[:, :], ACT.Sigmoid, bias=c.b2_col[:, 0:1]).then_inc(sigmoid_ready, 1)
                act.wait_ge(sigmoid_ready, 1)

            @block.vector
            def _(dve):
                v = nc.vector
                w2 = c.w2_row[:, :].unsqueeze(1).to_broadcast([P, G, hid])
                hi_iota = c.iota[:, 0:nb].unsqueeze(1).to_broadcast([P, G, nb])

                def arguments(at, ahead):
                    t, q = at.slot(2, ahead), at.slot(4, ahead)
                    dve.wait_ge(q_in[q], at.uses(4, ahead) * (16 * G))
                    dve.wait_ge(p_ready, at.g(ahead + 1))
                    wait(dve, gelu_ready, at.g(ahead + 1 - 2))
                    v.tensor_tensor(pre[:, t, :, :], ps_p[t], qt[:, q, :, :], ALU.add).then_inc(pre_ready, 1)

                def logits(at, ahead):
                    t = at.slot(2, ahead)
                    dve.wait_ge(gelu_ready, at.g(ahead + 1))
                    v.tensor_tensor(act_h[:, t, :, :], act_h[:, t, :, :], w2, ALU.mult).then_inc(prod_ready, 1)
                    dve.wait_ge(prod_ready, at.g(ahead + 1))
                    v.tensor_reduce(c.ew[:, at.tiles(ahead)], act_h[:, t, :, :], AX.X, ALU.add).then_inc(logit_ready, 1)

                def hots(at, ahead):
                    wait(dve, turned, at.g(ahead + 1 - 2))
                    source_hots(c, hot[:, at.slot(2, ahead), :, :], at, ahead).then_inc(hot_ready, 1)

                def target_hots(at):
                    t = at.slot(2)
                    wait(dve, summed, at.g(1 - 2))
                    v.tensor_tensor(hot_hi[:, t, :, :], c.meta[:, at.tiles(), 2].unsqueeze(2).to_broadcast([P, G, nb]),
                                    hi_iota, ALU.is_equal).then_inc(hi_ready, 1)
                    dve.wait_ge(tanh_ready, at.g(1))
                    v.tensor_scalar(weight[:, t, :], half_tanh[:, t, :], 0.5, 0.5, ALU.mult, ALU.add).then_inc(weight_ready, 1)
                    for j in range(G):
                        v.tensor_scalar(hot_lo[:, t, j, :], c.iota[:, :], c.meta[:, at.tile(j), 1], None, ALU.is_equal)
                    dve.wait_ge(hi_ready, at.g(0) * 2 + 1)
                    dve.wait_ge(weight_ready, at.g(1))
                    v.tensor_tensor(hot_hi[:, t, :, :], hot_hi[:, t, :, :],
                                    weight[:, t, :].unsqueeze(2).to_broadcast([P, G, nb]), ALU.mult).then_inc(hi_ready, 1)

                def body(at):
                    if at.has(2):
                        arguments(at, 2)
                    if at.has(0):
                        target_hots(at)
                    if at.has(4):
                        hots(at, 4)
                    if at.has(1):
                        logits(at, 1)

                v.tensor_scalar(b2_half[:, :], c.b2_col[:, :], 0.5, None, ALU.mult).then_inc(half_ready, 1)
                run_groups(dve, groups, 4, body)
                dve.wait_ge(summed, groups + 1)
                v.tensor_scalar(c.stat[:, 0, :], ps_deg[:, 0:nb], 1.0, None, ALU.add).then_inc(half_ready, 1)
                dve.wait_ge(half_ready, 2)

            @block.tensor
            def _(pe):
                t_ = nc.tensor
                regs = [pe.alloc_register(f"pe_w_blk{j}") for j in range(PER)]

                def turn_group(at, ahead):
                    pe.wait_ge(hot_ready, at.g(ahead + 1))
                    wait(pe, hot_t_ready, at.g(ahead))
                    turn(c, ps_hot, hot[:, at.slot(2, ahead), :, :]).then_inc(turned, 1)

                def look_up(at, ahead):
                    t = at.slot(2, ahead)
                    blocks = load_blocks(pe, c, 0, at, ahead, regs)
                    pe.wait_ge(hot_t_ready, at.g(ahead + 1))
                    wait(pe, pre_ready, at.g(ahead + 1 - 2))
                    for j in range(G):
                        for k in range(3):
                            last = t_.matmul(ps_p[t][:, j, :], hot_t[:, t, j * P:(j + 1) * P],
                                             c.lut[:, bass.ds(blocks[j // UNIT[0]] * (3 * hid) + k * hid, hid)],
                                             start=(k == 0), stop=(k == 2))
                    last.then_inc(p_ready, 1)

                def add_degrees(at):
                    t = at.slot(2)
                    pe.wait_ge(hi_ready, at.g(1) * 2)
                    for j in range(G):
                        last = t_.matmul(ps_deg[:, 0:nb], hot_lo[:, t, j, :], hot_hi[:, t, j, :], start=False, stop=False)
                    last.then_inc(summed, 1)

                def body(at):
                    if at.has(3):
                        look_up(at, 3)
                    if at.has(4):
                        turn_group(at, 4)
                    if at.has(0):
                        add_degrees(at)

                t_.matmul(ps_deg[:, 0:nb], c.zeros[:, :], c.zeros[:, 0:nb], start=True, stop=False)
                run_groups(pe, groups, 4, body)
                t_.matmul(ps_deg[:, 0:nb], c.zeros[:, :], c.zeros[:, 0:nb], start=False, stop=True).then_inc(summed, 1)


def scale_nodes(nc, c):
    nb, d = c.nb, c.d
    with Scope(nc, "scale") as s:
        s_step, s_root = s.sems("s_step s_root")
        with nc.Block() as block:
            @block.vector
            def _(dve):
                v = nc.vector
                n = 0

                def link(ins):
                    nonlocal n
                    n += 1
                    ins.then_inc(s_step, 1)
                    dve.wait_ge(s_step, n)

                dve.wait_ge(s_root, 1)
                link(v.reciprocal(c.dinv[:, :], c.stat[:, 1, :]))
                link(v.tensor_tensor(c.hn[:, :, :], c.hn[:, :, :], c.dinv[:, :].unsqueeze(2).to_broadcast([P, nb, d]), ALU.mult))
                x_lut = c.lut[:, c.X_AT:c.X_AT + nb * 3 * d].rearrange("p (b k n) -> p b k n", k=3, n=d)
                link(v.tensor_copy(x_lut[:, :, 0, :], c.hn[:, :, :]))
                link(v.tensor_tensor(c.accd, c.hn[:, :, :], x_lut[:, :, 0, :], ALU.subtract))
                link(v.tensor_copy(x_lut[:, :, 1, :], c.accd))
                link(v.tensor_tensor(x_lut[:, :, 2, :], c.accd, x_lut[:, :, 1, :], ALU.subtract))

            @block.scalar
            def _(act):
                nc.scalar.activation(c.stat[:, 1, :], c.stat[:, 0, :], ACT.Sqrt).then_inc(s_root, 1)
                act.wait_ge(s_root, 1)


def message_pass(nc, c):
    pl, nb, d = c.pl, c.nb, c.d
    ZW = c.ZW
    groups = pl.groups[0]
    PER = G // UNIT[0]
    with Scope(nc, "message") as s:
        want = s.sb("want", [P, 4, G], i32)
        hot = s.sb("hot", [P, 2, G, P], bf16)
        hot_t = s.sb("hot_t", [P, 2, G * P], bf16)
        msg = s.sb("msg", [P, 4, G, ZW])
        ps_x = [s.bank(f"ps_x{u}")[:, :].rearrange("p (g n) -> p g n", g=G) for u in range(2)]
        ps_hot = s.bank("ps_hot", 1, bf16)
        sent = [s.sem(f"sent{q}") for q in range(4)]
        (hot_ready, turned, hot_t_ready, want_ready, x_ready, msg_ready, scatter_step) = s.sems(
            "hot_ready turned hot_t_ready want_ready x_ready msg_ready scatter_step")

        with nc.Block() as block:
            @block.gpsimd
            def _(pool):
                limit = pool.to_reg(pl.rows[1] - 1)

                def body(at):
                    q = at.slot(4)
                    pool.wait_ge(want_ready, at.g(1))
                    pool.wait_ge(msg_ready, at.g(1))
                    pool.sem_inc(scatter_step, 1)
                    for j in range(G):
                        nc.gpsimd.indirect_dma_start(
                            c.rows_d[0:pl.rows[1], :], bass.IndirectOffsetOnAxis(want[:, q, j:j + 1], 0), msg[:, q, j, :], None,
                            bounds_check=limit, oob_is_err=False).then_inc(sent[q], 16)

                run_groups(pool, groups, 0, body)
                for q in range(4):
                    pool.wait_ge(sent[q], -(-(groups - q) // 4) * 16 * G)

            @block.scalar
            def _(act):
                a = nc.scalar

                def body(at):
                    if at.has(2):
                        act.wait_ge(turned, at.g(3))
                        wait(act, x_ready, at.g(3 - 2))
                        a.activation(hot_t[:, at.slot(2, 2), :], ps_hot[:, 0:G * P], ACT.Copy).then_inc(hot_t_ready, 1)
                    if at.has(0):
                        q = at.slot(4)
                        wait(act, sent[q], at.uses(4, 0, -1) * (16 * G))
                        a.activation(msg[:, q, :, d], c.meta[:, at.tiles(), 1], ACT.Copy)
                        a.activation(want[:, q, :], c.where[:, 1, at.tiles()], ACT.Copy).then_inc(want_ready, 1)

                run_groups(act, groups, 2, body)

            @block.vector
            def _(dve):
                v = nc.vector

                def body(at):
                    if at.has(3):
                        wait(dve, turned, at.g(4 - 2))
                        source_hots(c, hot[:, at.slot(2, 3), :, :], at, 3).then_inc(hot_ready, 1)
                    if at.has(0):
                        q = at.slot(4)
                        dve.wait_ge(x_ready, at.g(1))
                        wait(dve, sent[q], at.uses(4, 0, -1) * (16 * G))
                        v.tensor_tensor(msg[:, q, :, 0:d], ps_x[at.slot(2)],
                                        c.ew[:, at.tiles()].unsqueeze(2).to_broadcast([P, G, d]), ALU.mult).then_inc(msg_ready, 1)

                run_groups(dve, groups, 3, body)

            @block.tensor
            def _(pe):
                t_ = nc.tensor
                regs = [pe.alloc_register(f"pe_m_blk{j}") for j in range(PER)]

                def body(at):
                    if at.has(1):
                        t = at.slot(2, 1)
                        blocks = load_blocks(pe, c, 0, at, 1, regs)
                        pe.wait_ge(hot_t_ready, at.g(2))
                        wait(pe, msg_ready, at.g(2 - 2))
                        for j in range(G):
                            for k in range(3):
                                last = t_.matmul(ps_x[t][:, j, :], hot_t[:, t, j * P:(j + 1) * P],
                                                 c.lut[:, bass.ds(blocks[j // UNIT[0]] * (3 * d) + (c.X_AT + k * d), d)],
                                                 start=(k == 0), stop=(k == 2))
                        last.then_inc(x_ready, 1)
                    if at.has(2):
                        pe.wait_ge(hot_ready, at.g(3))
                        wait(pe, hot_t_ready, at.g(2))
                        turn(c, ps_hot, hot[:, at.slot(2, 2), :, :]).then_inc(turned, 1)

                run_groups(pe, groups, 2, body)


def target_pass(nc, c):
    pl, nb, d, ZW = c.pl, c.nb, c.d, c.ZW
    groups = pl.groups[1]
    assert UNIT[1] == G
    with Scope(nc, "target") as s:
        msg = s.sb("msg", [P, 4, G, ZW])
        hot = s.sb("hot", [P, 4, G, P])
        ps = [s.bank(f"ps{u}") for u in range(4)]
        msg_in = [s.sem(f"msg_in{q}") for q in range(4)]
        hot_ready, sums_ready, added = s.sems("hot_ready sums_ready added")
        with nc.Block() as block:
            @block.sync
            def _(sp):
                def body(at):
                    q = at.slot(4)
                    wait(sp, sums_ready, at.g(1 - 4))
                    sp.dma_start(msg[:, q, :, :].rearrange("p g n -> p (g n)"), group_rows(c.rows_d[0:pl.rows[1], :], at)).then_inc(msg_in[q], 16)

                run_groups(sp, groups, 0, body)

            @block.vector
            def _(dve):
                v = nc.vector
                regs = [dve.alloc_register("dve_t_blk")]

                def body(at):
                    if at.has(2):
                        q = at.slot(4, 2)
                        dve.wait_ge(msg_in[q], at.uses(4, 2) * 16)
                        wait(dve, sums_ready, at.g(3 - 4))
                        for j in range(G):
                            last = v.tensor_scalar(hot[:, q, j, :], c.iota[:, :], msg[:, q, j, d:d + 1], None, ALU.is_equal)
                        last.then_inc(hot_ready, 1)
                    if at.has(0):
                        blocks = load_blocks(dve, c, 1, at, 0, regs)
                        dve.wait_ge(sums_ready, at.g(1))
                        dve.wait_ge(added, at.g(1))
                        dest = c.acc[:, bass.ds(blocks[0] * d, d)]
                        v.tensor_tensor(dest, dest, ps[at.slot(4)][:, 0:d], ALU.add).then_inc(added, 1)

                v.memset(c.accd, 0.0).then_inc(added, 1)
                run_groups(dve, groups, 2, body)
                dve.wait_ge(added, groups + 1)

            @block.tensor
            def _(pe):
                t_ = nc.tensor

                def body(at):
                    q = at.slot(4)
                    pe.wait_ge(hot_ready, at.g(1))
                    if at.has(-4):
                        pe.wait_ge(added, at.g(2 - 4))
                    for j in range(G):
                        last = t_.matmul(ps[q][:, 0:d], hot[:, q, j, :], msg[:, q, j, 0:d], start=(j == 0), stop=(j == G - 1))
                    last.then_inc(sums_ready, 1)

                run_groups(pe, groups, 0, body)


def finish(nc, c):
    nb, d, pl = c.nb, c.d, c.pl
    with Scope(nc, "finish") as s:
        s_step, s_out = s.sems("s_step s_out")
        with nc.Block() as block:
            @block.vector
            def _(dve):
                v = nc.vector
                v.tensor_tensor(c.xn[:, :, :], c.xn[:, :, :],
                                c.bias_c[:, :].unsqueeze(1).to_broadcast([P, nb, d]), ALU.add)
                v.tensor_tensor(c.accd, c.accd, c.hn[:, :, :], ALU.add).then_inc(s_step, 1)
                dve.wait_ge(s_step, 1)
                v.tensor_tensor(c.accd, c.accd, c.dinv[:, :].unsqueeze(2).to_broadcast([P, nb, d]), ALU.mult).then_inc(s_step, 1)
                dve.wait_ge(s_step, 2)
                v.tensor_tensor(c.accd, c.accd, c.xn[:, :, :], ALU.add).then_inc(s_step, 1)

            @block.sync
            def _(sp):
                whole = c.LAST * P
                sp.wait_ge(s_step, 3)
                sp.dma_start(c.out[0:whole, :].rearrange("(b p) n -> p b n", p=P), c.accd[:, 0:c.LAST, :]).then_inc(s_out, 16)
                sp.dma_start(c.out[whole:, :], c.accd[0:pl.tail, c.LAST, :]).then_inc(s_out, 16)
                sp.wait_ge(s_out, 32)


_INS = ["x", "src", "dst", "edge_attr_70", "L0_gnn_Wf", "L0_gnn_bf", "L0_gnn_Wq", "L0_gnn_Wk", "L0_gnn_Wa",
        "L0_gnn_Wu", "L0_gnn_bu", "L1_gnn_mlp_w1", "L1_gnn_mlp_b1", "L1_gnn_mlp_w2", "L1_gnn_mlp_b2",
        "L1_gnn_conv_w", "L1_gnn_conv_b"]


def kernel(**inputs):
    import concourse.bacc as bacc
    from concourse.bass_utils import run_bass_kernel_spmd

    nc = bacc.Bacc("TRN2", target_bir_lowering=False, num_devices=1)
    arrays, args = {}, []
    for name in _INS:
        a = np.ascontiguousarray(inputs[name])
        arrays[name] = a
        args.append(nc.dram_tensor(name, a.shape, mybir.dt.from_np(a.dtype), kind="ExternalInput").ap())
    out = nc.dram_tensor("out", inputs["x"].shape, f32, kind="ExternalOutput").ap()
    gnn(nc, *args, out)
    r = run_bass_kernel_spmd(nc, [arrays], core_ids=[0])
    return r.results[0]["out"]
```

```python
import numpy as np
from contextlib import ExitStack

import concourse.bass as bass
from concourse import mybir

f32 = mybir.dt.float32
bf16 = mybir.dt.bfloat16
i32 = mybir.dt.int32
ALU = mybir.AluOpType
ACT = mybir.ActivationFunctionType
AX = mybir.AxisListType

P = 128
G = 4
U = 2
UB = 4
FIRST = 4
SET = 7
UNIT = (2, 4)
FAR = 1 << 20
EPS = 1e-5

SRC_1, DST_LO, DST_HI, DST, DROW = 65, 66, 67, 68, 69
META = 5


class Plan:

    def __init__(self, n_nodes, n_edges, d, attr, attr_used, hid):
        self.n, self.e, self.d, self.attr, self.ef, self.hid = n_nodes, n_edges, d, attr, attr_used, hid
        self.nb = -(-n_nodes // P)
        self.tail = n_nodes - (self.nb - 1) * P
        self.full = n_edges // P
        self.rest = n_edges - self.full * P
        self.prep_loops = self.full // (G * U)
        self.peeled = self.full - self.prep_loops * G * U
        assert self.rest and self.peeled == G - 1
        self.cols = self.prep_loops * G * U + G
        self.units = [(n_edges + self.nb * (k * P - 1)) // (k * P) for k in UNIT]
        self.groups = [-(-n * k // G) for n, k in zip(self.units, UNIT)]
        self.tiles = self.groups[0] * G
        self.rows = [n * G * P for n in self.groups]
        self.spare = [-(-self.nb * k // G) * G * P for k in UNIT]
        self.map = -(-max(self.units) // P) * P


def gnn(nc, x, src, dst, edge_attr, Wf, bf, Wq, Wk, Wa, Wu, bu, w1, b1, w2, b2, conv_w, conv_b, out):
    n_nodes, d = x.shape
    n_edges, attr = edge_attr.shape
    pl = Plan(n_nodes, n_edges, d, attr, Wf.shape[0] - 3 * d, w1.shape[1])
    nb, hid, ef = pl.nb, pl.hid, pl.ef
    assert d == P and ef == SRC_1 and attr == ef + META

    c = Shared()
    c.nc, c.pl, c.nb, c.d, c.hid, c.ef, c.attr = nc, pl, nb, d, hid, ef, attr
    c.x, c.src, c.dst, c.edge_attr, c.out = x, src, dst, edge_attr, out
    c.Wf, c.bf, c.Wq, c.Wk, c.Wa, c.Wu, c.bu = Wf, bf, Wq, Wk, Wa, Wu, bu
    c.w1, c.b1, c.w2, c.b2, c.conv_w, c.conv_b = w1, b1, w2, b2, conv_w, conv_b
    c.LAST = nb - 1
    c.AGW = AGW = 2 * d
    c.X_AT = nb * 3 * hid
    c.ZW = ZW = d + 1

    c.rows_s = nc.dram_tensor("rows_by_source", [pl.rows[0] + pl.spare[0], attr], f32).ap()
    c.rows_d = nc.dram_tensor("messages_by_target", [pl.rows[1] + pl.spare[1], ZW], f32).ap()
    c.tab_b = nc.dram_tensor("table_b", [nb * P, d], f32).ap()
    c.tab_q = nc.dram_tensor("table_q", [nb * P, hid], f32).ap()
    c.blk_dram = nc.dram_tensor("block_of_unit", [2, pl.map], i32).ap()

    ctx = ExitStack()
    with ctx:
        def sb(name, shape, dt=f32):
            return ctx.enter_context(nc.sbuf_tensor(name, shape, dt))

        c.iota_i = sb("iota_i", [P, P], i32)
        c.part_i = sb("part_i", [P, 1], i32)
        c.unit_i = sb("unit_i", [P, pl.map // P], i32)
        c.iota = sb("iota", [P, P])
        c.iota1 = sb("iota1", [P, P])
        c.iota1_b = sb("iota1_b", [P, P], bf16)
        c.part = sb("part", [P, 1])
        c.ident = sb("ident", [P, P])
        c.ident_b = sb("ident_b", [P, P], bf16)
        c.earlier_b = sb("earlier_b", [P, P], bf16)
        c.ones = sb("ones", [P, P])
        c.ones_b = sb("ones_b", [P, P], bf16)
        c.zeros = sb("zeros", [P, P])
        c.eps_t = sb("eps_t", [P, 1])
        c.minus_1 = sb("minus_1", [P, 1])

        c.wf = sb("wf", [P, 3, d])
        c.w4 = sb("w4", [ef, d])
        c.wq = sb("wq", [P, d])
        c.wk = sb("wk", [P, d])
        c.wa = sb("wa", [P, 1])
        c.wu = sb("wu", [P, d])
        c.wqkT = sb("wqkT", [P, 2, P])
        c.wnode = sb("wnode", [P, 3 * d])
        c.wnode1 = sb("wnode1", [P, 2 * hid + d])
        c.bias_f = sb("bias_f", [P, d])
        c.bias_u = sb("bias_u", [P, d])
        c.bias_1 = sb("bias_1", [P, hid])
        c.bias_c = sb("bias_c", [P, d])
        c.w2_row = sb("w2_row", [P, hid])
        c.b2_col = sb("b2_col", [P, 1])

        c.blk = sb("blk", [1, 2, pl.map], i32)

        c.hn = sb("hn", [P, nb, d])
        c.acc = sb("acc", [P, nb * ZW])
        c.acc3 = c.acc[:, :].rearrange("p (b w) -> p b w", w=ZW)
        c.accd = c.acc[:, 0:nb * d].rearrange("p (b w) -> p b w", w=d)
        c.stat = sb("stat", [P, 4, nb])
        c.dinv = sb("dinv", [P, nb])

        c.last_run = sb("last_run", [P, 2, nb], i32)
        c.weights_in = ctx.enter_context(nc.semaphore("weights_in"))
        with nc.sbuf_tensor("fill_s", [P, G, attr], f32) as c.fill_s, nc.sbuf_tensor("fill_d", [P, G, ZW], f32) as c.fill_d:
            setup_phase(nc, c)
            sort_phase(nc, c)

        c.meta = sb("meta", [P, pl.tiles, 3], bf16)
        c.where = sb("where", [P, 2, pl.tiles], i32)
        with nc.sbuf_tensor("lut0", [P, nb * 3 * AGW], bf16) as c.lut:
            layer0_nodes(nc, c)
            layer0_edges(nc, c)
        c.lut = sb("lut1", [P, nb * 3 * (hid + d)], bf16)
        c.xn = sb("xn", [P, nb, d])
        c.ew = sb("ew", [P, pl.tiles])
        layer0_update(nc, c)
        weights_pass(nc, c)
        scale_nodes(nc, c)
        message_pass(nc, c)
        target_pass(nc, c)
        finish(nc, c)


class Shared:
    pass


class Scope:

    def __init__(self, nc, tag):
        self.nc, self.tag, self.ctx = nc, tag, ExitStack()

    def __enter__(self):
        return self

    def __exit__(self, *error):
        self.ctx.close()

    def sb(self, name, shape, dt=f32):
        return self.ctx.enter_context(self.nc.sbuf_tensor(f"{self.tag}_{name}", shape, dt))

    def bank(self, name, banks=1, dt=f32):
        return self.ctx.enter_context(self.nc.psum_tensor(f"{self.tag}_{name}", [P, banks * 2048 // mybir.dt.size(dt)], dt))

    def sem(self, name):
        return self.ctx.enter_context(self.nc.semaphore(f"{self.tag}_{name}"))

    def sems(self, names):
        return [self.sem(n) for n in names.split()]


def setup_phase(nc, c):
    pl, nb, d, hid, ef, attr = c.pl, c.nb, c.d, c.hid, c.ef, c.attr
    with Scope(nc, "setup") as s:
        fill, fill_d = c.fill_s, c.fill_d
        s_iota, s_const, s_fill, s_zero = s.sems(
            "s_iota s_const s_fill s_zero")

        with nc.Block() as block:
            @block.gpsimd
            def _(pool):
                nc.gpsimd.iota(c.iota_i[:, :], pattern=[[1, P]], base=0, channel_multiplier=0).then_inc(s_iota, 1)
                nc.gpsimd.iota(c.part_i[:, :], pattern=[[0, 1]], base=0, channel_multiplier=1).then_inc(s_iota, 1)
                nc.gpsimd.iota(c.unit_i[:, :], pattern=[[1, pl.map // P]], base=0,
                               channel_multiplier=pl.map // P).then_inc(s_iota, 1)

            @block.vector
            def _(dve):
                v = nc.vector
                v.memset(fill[:, :, :], 0.0).then_inc(s_zero, 1)
                v.memset(fill_d[:, :, :], 0.0).then_inc(s_zero, 1)
                dve.wait_ge(s_zero, 2)
                v.memset(fill[:, :, DST_LO:DST_HI + 1], -1.0).then_inc(s_fill, 1)
                v.memset(fill[:, :, :].bitcast(i32)[:, :, DROW:DROW + 1], FAR).then_inc(s_fill, 1)
                v.memset(fill_d[:, :, d:d + 1], -1.0).then_inc(s_fill, 1)
                v.memset(c.ones[:, :], 1.0).then_inc(s_const, 1)
                v.memset(c.ones_b[:, :], 1.0).then_inc(s_const, 1)
                v.memset(c.zeros[:, :], 0.0).then_inc(s_const, 1)
                v.memset(c.eps_t[:, :], EPS).then_inc(s_const, 1)
                v.memset(c.minus_1[:, :], -1.0).then_inc(s_const, 1)
                dve.wait_ge(s_iota, 3)
                v.tensor_copy(c.iota[:, :], c.iota_i[:, :]).then_inc(s_const, 1)
                v.tensor_scalar(c.iota1[:, :], c.iota_i[:, :], 1, None, ALU.add).then_inc(s_const, 1)
                v.tensor_scalar(c.iota1_b[:, :], c.iota_i[:, :], 1, None, ALU.add).then_inc(s_const, 1)
                v.tensor_copy(c.part[:, :], c.part_i[:, :]).then_inc(s_const, 1)
                dve.wait_ge(s_const, 9)
                v.tensor_scalar(c.ident[:, :], c.iota[:, :], c.part[:, 0:1], None, ALU.is_equal).then_inc(s_const, 1)
                v.tensor_scalar(c.ident_b[:, :], c.iota[:, :], c.part[:, 0:1], None, ALU.is_equal).then_inc(s_const, 1)
                v.tensor_scalar(c.earlier_b[:, :], c.iota[:, :], c.part[:, 0:1], None, ALU.is_gt).then_inc(s_const, 1)
                dve.wait_ge(s_const, 12)

            @block.scalar
            def _(act):
                def row(ap, n):
                    return ap.rearrange("(a n) -> a n", a=1).to_broadcast([P, n])

                loads = [
                    (c.wf[:, :, :], c.Wf[0:3 * d, :].rearrange("(t p) n -> p t n", p=P)),
                    (c.w4[:, :], c.Wf[3 * d:3 * d + ef, :]),
                    (c.wq[:, :], c.Wq), (c.wk[:, :], c.Wk), (c.wa[:, :], c.Wa),
                    (c.wu[:, :], c.Wu),
                    (c.wnode1[:, 0:2 * hid].rearrange("p (t n) -> p t n", t=2), c.w1.rearrange("(t p) n -> p t n", p=P)),
                    (c.wnode1[:, 2 * hid:], c.conv_w),
                    (c.bias_f[:, :], row(c.bf, d)), (c.bias_u[:, :], row(c.bu, d)),
                    (c.bias_1[:, :], row(c.b1, hid)), (c.bias_c[:, :], row(c.conv_b, d)),
                    (c.w2_row[:, :], row(c.w2.rearrange("n a -> (n a)"), hid)),
                    (c.b2_col[:, :], row(c.b2, 1)),
                ]
                for dest, origin in loads:
                    act.dma_start(dest, origin).then_inc(c.weights_in, 16)
                c.weight_loads = len(loads)


def sort_phase(nc, c):
    pl, nb, attr = c.pl, c.nb, c.attr
    C = pl.cols
    whole = pl.full * P
    with Scope(nc, "sort") as s:
        ends = s.sb("ends", [P, 2, C], i32)
        lo = s.sb("lo", [P, 3, C])
        src_hi = s.sb("src_hi", [P, C])
        hi_b = s.sb("hi_b", [P, 2, C], bf16)
        last_run = c.last_run
        none = s.sb("none", [P, 2, nb])
        rest = s.sb("rest", [P, 2, nb])
        odd = s.sb("odd", [P, nb], i32)
        half = s.sb("half", [P, C], i32)
        count = s.sb("count", [P, 2, nb])
        tot = s.sb("tot", [P, 2, nb])
        need_i = s.sb("need_i", [P, 2, nb], i32)
        need = s.sb("need", [P, 2, nb])
        upto = s.sb("upto", [P, 2, nb])
        run = s.sb("run", [P, 2, nb])
        NT = pl.map // P
        unit_f = s.sb("unit_f", [P, NT])
        cmp = s.sb("cmp", [P, 2, NT, nb])
        bot = s.sb("bot", [P, 2, NT])
        bot_i = s.sb("bot_i", [P, 2, NT], i32)
        junk = s.sb("junk", [P, 2, C], bf16)
        hot = s.sb("hot", [P, U, 2, G * nb], bf16)
        SLOTS = 4
        rank = s.sb("rank", [P, U, 2, G, nb])
        row_f = s.sb("row_f", [P, U, 2, G])
        row_a = s.sb("row_a", [P, U, 2, G], i32)
        row_b = s.sb("row_b", [P, U, 2, G], i32)
        row_c = s.sb("row_c", [P, U, 2, G], i32)
        row_e = s.sb("row_e", [P, U, 2, G], i32)
        row_i = s.sb("row_i", [P, SLOTS, 2, G], i32)
        edge = s.sb("edge", [P, SLOTS, G, attr])
        edge_i = edge[:, :, :, :].bitcast(i32)
        pre = [s.bank(f"pre{u}")[:, 0:2 * G * nb].rearrange("p (k n) -> p k n", k=2) for u in range(U)]
        add = [s.bank(f"add{u}")[:, 0:2 * nb].rearrange("p (k n) -> p k n", k=2) for u in range(U)]

        (s_ends, s_tails, s_pad, s_key, s_cnt, s_tot, s_base, s_bot, s_blkw, s_blkr) = s.sems(
            "s_ends s_tails s_pad s_key s_cnt s_tot s_base s_bot s_blkw s_blkr")

        fills = (c.fill_s, c.fill_d)

        with nc.Block() as block:
            @block.sync
            def _(sp):
                sp.wait_ge(s_pad, 1)
                for k, key in enumerate((c.src, c.dst)):
                    sp.dma_start(ends[:, k, 0:pl.full], key[0:whole].rearrange("(p r) -> p r", p=P)).then_inc(s_ends, 16)
                    sp.dma_start(ends[0:pl.rest, k, pl.full:pl.full + 1],
                                 key[whole:].rearrange("(p r) -> p r", r=1)).then_inc(s_ends, 16)
                sp.wait_ge(s_bot, 1)
                for k in range(2):
                    sp.dma_start(c.blk_dram[k, :].rearrange("(p r) -> p r", p=P), bot_i[:, k, :]).then_inc(s_blkw, 16)
                sp.wait_ge(s_blkw, 32)
                sp.dma_start(c.blk[0:1, :, :], c.blk_dram.rearrange("(a k) r -> a k r", a=1)).then_inc(s_blkr, 16)
                sp.wait_ge(s_blkr, 16)

            @block.vector
            def _(dve):
                v = nc.vector
                v.memset(ends[:, :, :], nb * P).then_inc(s_pad, 1)
                v.memset(edge[:, :, :, :], 0.0).then_inc(s_pad, 1)
                v.memset(c.accd[:, c.LAST, :], 0.0).then_inc(s_pad, 1)
                dve.wait_ge(s_ends, 64)
                n = 0
                for k in range(2):
                    v.tensor_scalar(half[:, :], ends[:, k, :], 7, None, ALU.logical_shift_right).then_inc(s_key, 1)
                    n += 1
                    dve.wait_ge(s_key, n)
                    v.tensor_copy(src_hi[:, :] if k == 0 else lo[:, 2, :], half[:, :]).then_inc(s_key, 1)
                    n += 1
                    dve.wait_ge(s_key, n)
                    v.tensor_scalar(half[:, :], ends[:, k, :], P - 1, None, ALU.bitwise_and).then_inc(s_key, 1)
                    n += 1
                    dve.wait_ge(s_key, n)
                    v.tensor_copy(lo[:, k, :], half[:, :]).then_inc(s_key, 1)
                    n += 1
                    dve.wait_ge(s_key, n)
                v.tensor_scalar(lo[:, 0, :], lo[:, 0, :], 1.0, None, ALU.add).then_inc(s_key, 1)
                v.tensor_copy(hi_b[:, 0, :], src_hi[:, :]).then_inc(s_key, 1)
                v.tensor_copy(hi_b[:, 1, :], lo[:, 2, :]).then_inc(s_key, 1)
                dve.wait_ge(s_key, n + 3)
                dve.sem_inc(s_cnt, 2)
                with dve.Fori(0, nb // SET) as i:
                    for j in range(SET):
                        for k in range(2):
                            b = bass.ds(i * SET + j, 1)
                            dve.wait_ge(s_cnt, i * (2 * SET) + (2 * j + k + 1))
                            v.tensor_scalar(junk[:, k, :], hi_b[:, k, :], c.iota[:, b], None, ALU.is_equal, ALU.add,
                                            accum_out=count[:, k, b]).then_inc(s_cnt, 1)
                dve.wait_ge(s_tot, 1)
                n = 0

                def link(ins):
                    nonlocal n
                    n += 1
                    ins.then_inc(s_base, 1)
                    dve.wait_ge(s_base, n)

                for k in range(2):
                    link(v.tensor_scalar(tot[:, k, :], pre[0][:, k, 0:nb], float(UNIT[k] * P - 1), None, ALU.add))
                link(v.tensor_copy(need_i[:, :, :], tot[:, :, :]))
                for k in range(2):
                    link(v.tensor_scalar(need_i[:, k, :], need_i[:, k, :], (UNIT[k] * P).bit_length() - 1, None,
                                         ALU.logical_shift_right))
                link(v.tensor_copy(need[:, :, :], need_i[:, :, :]))
                for k in range(2):
                    link(v.tensor_tensor_scan(upto[:, k, :], need[:, k, :], c.zeros[:, 0:nb], 0.0, ALU.add, ALU.add))
                link(v.tensor_tensor(run[:, :, :], upto[:, :, :], need[:, :, :], ALU.subtract))
                for k in range(2):
                    link(v.tensor_scalar(run[:, k, :], run[:, k, :], float(UNIT[k] * P), None, ALU.mult))
                link(v.tensor_scalar(none[:, :, :], need[:, :, :], 0.5, None, ALU.is_lt))
                link(v.tensor_scalar(need[:, :, :], upto[:, :, :], -1.0, None, ALU.add))
                for k in range(2):
                    link(v.scalar_tensor_tensor(rest[:, k, :], c.iota[:, 0:nb], float(pl.groups[k] * G // UNIT[k]), need[:, k, :],
                                                ALU.add, ALU.subtract))
                link(v.tensor_tensor(rest[:, :, :], rest[:, :, :], none[:, :, :], ALU.mult))
                link(v.tensor_tensor(need[:, :, :], need[:, :, :], rest[:, :, :], ALU.add))
                link(v.tensor_copy(last_run[:, :, :], need[:, :, :]))
                link(v.tensor_scalar(odd[:, :], last_run[:, 0, :], 1, None, ALU.bitwise_and))
                link(v.tensor_scalar(last_run[:, 0, :], last_run[:, 0, :], 1, 8, ALU.logical_shift_right, ALU.logical_shift_left))
                link(v.tensor_tensor(last_run[:, 0, :], last_run[:, 0, :], odd[:, :], ALU.bitwise_or))
                link(v.tensor_scalar(last_run[:, 1, :], last_run[:, 1, :], 7, None, ALU.logical_shift_left))
                link(v.tensor_copy(unit_f[:, :], c.unit_i[:, :]))
                for k in range(2):
                    link(v.tensor_tensor(cmp[:, k, :, :], unit_f[:, :].unsqueeze(2).to_broadcast([P, NT, nb]),
                                         upto[:, k, :].unsqueeze(1).to_broadcast([P, NT, nb]), ALU.is_ge))
                    link(v.tensor_reduce(bot[:, k, :], cmp[:, k, :, :], AX.X, ALU.add))
                link(v.tensor_scalar(bot[:, :, :], bot[:, :, :], float(nb - 1), None, ALU.min))
                v.tensor_copy(bot_i[:, :, :], bot[:, :, :]).then_inc(s_bot, 1)

            @block.scalar
            def _(act):
                n = 0
                for k in range(2):
                    view = (c.rows_s, c.rows_d)[k][0:pl.rows[k], :].rearrange("(g p r) n -> g p (r n)", p=P, r=G)
                    for g in range(-(-pl.e // (UNIT[k] * P)) * UNIT[k] // G, pl.groups[k]):
                        act.dma_start(view[g, :, :], fills[k][:, :, :].rearrange("p r n -> p (r n)")).then_inc(s_tails, 16)
                        n += 1
                act.wait_ge(s_tails, 16 * n)

            @block.tensor
            def _(pe):
                pe.wait_ge(s_cnt, 2 * nb + 2)
                nc.tensor.matmul(pre[0][:, :, 0:nb], c.ones[:, :], count[:, :, :], start=True, stop=True).then_inc(s_tot, 1)

        (row_cast, rank_a, rank_b, run_ready, hot_ready, prefix_ready, row_bits_b, row_bits_c, row_bits_e, row_ready,
         fields_ready, filled_s, x_in, pool_step) = s.sems(
            "row_cast rank_a rank_b run_ready hot_ready prefix_ready row_bits_b row_bits_c row_bits_e row_ready "
            "fields_ready filled_s x_in pool_step")
        edge_in = [s.sem(f"edge_in{q}") for q in range(SLOTS)]
        edge_done = [s.sem(f"edge_done{q}") for q in range(SLOTS)]
        groups = C // G
        half_blocks = nb // SET // 2 * SET
        LAST = groups - 1
        assert pl.peeled == G - 1

        with nc.Block() as block:
            attr_v = c.edge_attr[0:whole, :].rearrange("(p r) n -> p (r n)", p=P)

            @block.sync
            def _(sp):
                fill_padding(sp, c, 0, 0, half_blocks, "sp_last_run", filled_s)

                def body(at):
                    q = at.slot(SLOTS)
                    wait(sp, edge_done[q], at.uses(SLOTS, 0, -1) * (16 * G))
                    if at.last:
                        sp.dma_start(edge[:, q, 0:pl.peeled, :].rearrange("p g n -> p (g n)"),
                                     attr_v[:, LAST * G * attr:]).then_inc(edge_in[q], 16)
                        sp.dma_start(edge[0:pl.rest, q, pl.peeled, :], c.edge_attr[whole:, :]).then_inc(edge_in[q], 16)
                    else:
                        sp.dma_start(edge[:, q, :, :].rearrange("p g n -> p (g n)"),
                                     attr_v[:, bass.ds(at.g() * (G * attr), G * attr)]).then_inc(edge_in[q], 16)

                run_groups(sp, groups, 0, body, peel=1)

            @block.vector
            def _(dve):
                v = nc.vector

                def one_hot(at, ahead):
                    u = at.slot(U, ahead)
                    wait(dve, prefix_ready, at.g(ahead + 1 - U))
                    hv = hot[:, u, :, :].rearrange("p k (g b) -> p k g b", b=nb)
                    iota_v = c.iota[:, 0:nb].unsqueeze(1).to_broadcast([P, G, nb])
                    v.tensor_tensor(hv[:, 0, :, :], src_hi[:, at.tiles(ahead)].unsqueeze(2).to_broadcast([P, G, nb]),
                                    iota_v, ALU.is_equal)
                    v.tensor_tensor(hv[:, 1, :, :], lo[:, 2, at.tiles(ahead)].unsqueeze(2).to_broadcast([P, G, nb]),
                                    iota_v, ALU.is_equal).then_inc(hot_ready, 1)

                def rows(at):
                    u, q = at.slot(U), at.slot(SLOTS)
                    dve.wait_ge(prefix_ready, at.g(1))
                    wait(dve, run_ready, at.g(0))
                    v.tensor_tensor(rank[:, u, :, :, :], pre[u][:, :, :].rearrange("p k (g b) -> p k g b", b=nb),
                                    run[:, :, :].unsqueeze(2).to_broadcast([P, 2, G, nb]), ALU.add).then_inc(rank_a, 1)
                    dve.wait_ge(rank_a, at.g(1))
                    v.tensor_tensor(run[:, :, :], run[:, :, :], add[u][:, :, :], ALU.add).then_inc(run_ready, 1)
                    v.tensor_tensor(rank[:, u, :, :, :].rearrange("p k g b -> p k (g b)"),
                                    rank[:, u, :, :, :].rearrange("p k g b -> p k (g b)"), hot[:, u, :, :],
                                    ALU.mult).then_inc(rank_b, 1)
                    dve.wait_ge(rank_b, at.g(1))
                    v.tensor_reduce(row_f[:, u, :, :], rank[:, u, :, :, :], AX.X, ALU.add).then_inc(row_cast, 1)
                    if at.has(2):
                        one_hot(at, 2)
                    dve.wait_ge(row_cast, at.g(0) * 2 + 1)
                    if at.last:
                        v.tensor_scalar(rank[:, u, 0, 0, 0:1], src_hi[:, C - 1:C], float(nb), float(FAR),
                                        ALU.is_ge, ALU.mult).then_inc(rank_b, 1)
                        dve.wait_ge(rank_b, at.g(2))
                        v.tensor_tensor(row_f[:, u, 0, G - 1:G], row_f[:, u, 0, G - 1:G], rank[:, u, 0, 0, 0:1],
                                        ALU.add).then_inc(rank_b, 1)
                        dve.wait_ge(rank_b, at.g(3))
                    v.tensor_copy(row_a[:, u, :, :], row_f[:, u, :, :]).then_inc(row_cast, 1)
                    dve.wait_ge(row_cast, at.g(0) * 2 + 2)
                    v.tensor_scalar(row_b[:, u, :, :], row_a[:, u, :, :], P - 1, 2, ALU.bitwise_and,
                                    ALU.logical_shift_left).then_inc(row_bits_b, 1)
                    v.tensor_scalar(row_c[:, u, :, :], row_a[:, u, :, :], 7, G - 1, ALU.logical_shift_right,
                                    ALU.bitwise_and).then_inc(row_bits_c, 1)
                    v.tensor_scalar(row_e[:, u, :, :], row_a[:, u, :, :], (FAR - 1) * 2 + 1 - (G * P - 1), None,
                                    ALU.bitwise_and).then_inc(row_bits_e, 1)
                    dve.wait_ge(row_bits_c, at.g(1))
                    v.tensor_tensor(row_b[:, u, :, :], row_b[:, u, :, :], row_c[:, u, :, :], ALU.bitwise_or).then_inc(row_bits_b, 1)
                    dve.wait_ge(row_bits_b, at.g(0) * 2 + 2)
                    wait(dve, edge_done[q], at.uses(SLOTS, 0, -1) * (16 * G))
                    v.tensor_tensor(row_i[:, q, :, :], row_b[:, u, :, :], row_e[:, u, :, :], ALU.bitwise_or).then_inc(row_ready, 1)

                def body(at):
                    if at.has(0):
                        rows(at)
                    else:
                        one_hot(at, 2)

                run_groups(dve, groups, 2, body, peel=1)

            @block.tensor
            def _(pe):
                t = nc.tensor

                def body(at):
                    u = at.slot(U)
                    pe.wait_ge(hot_ready, at.g(1))
                    wait(pe, run_ready, at.g(1 - U))
                    t.matmul(pre[u][:, :, :], c.earlier_b[:, :], hot[:, u, :, :], start=True, stop=False)
                    for k in range(1, G):
                        t.matmul(pre[u][:, :, k * nb:], c.ones_b[:, :], hot[:, u, :, 0:(G - k) * nb],
                                 start=False, stop=(k == G - 1))
                    for k in range(G):
                        last = t.matmul(add[u][:, :, :], c.ones_b[:, :], hot[:, u, :, k * nb:(k + 1) * nb],
                                        start=(k == 0), stop=(k == G - 1))
                    last.then_inc(prefix_ready, 1)

                run_groups(pe, groups, 0, body)

            @block.scalar
            def _(act):
                fill_padding(act, c, 0, half_blocks, nb, "act_last_run", filled_s)
                x_loads = load_x(c, act, c.accd, x_in)

                def body(at):
                    q = at.slot(SLOTS)
                    act.wait_ge(edge_in[q], at.uses(SLOTS) * 16 + (16 if at.last else 0))
                    nc.scalar.activation(edge[:, q, :, SRC_1:DST],
                                         lo[:, :, at.tiles()].rearrange("p f g -> p g f"), ACT.Copy)
                    nc.scalar.activation(edge_i[:, q, :, DST], ends[:, 1, at.tiles()], ACT.Copy)
                    act.wait_ge(row_ready, at.g(1))
                    nc.scalar.activation(edge_i[:, q, :, DROW], row_i[:, q, 1, :], ACT.Copy).then_inc(fields_ready, 1)

                run_groups(act, groups, 0, body, peel=1)
                act.wait_ge(c.weights_in, 16 * c.weight_loads)
                act.wait_ge(x_in, x_loads)

            @block.gpsimd
            def _(pool):
                limit = pool.to_reg(pl.rows[0] - 1)
                pool.wait_ge(filled_s, nb * 16)

                def body(at):
                    q = at.slot(SLOTS)
                    pool.wait_ge(fields_ready, at.g(1))
                    pool.sem_inc(pool_step, 1)
                    for j in range(G):
                        nc.gpsimd.indirect_dma_start(
                            c.rows_s[0:pl.rows[0], :], bass.IndirectOffsetOnAxis(row_i[:, q, 0, j:j + 1], 0), edge[:, q, j, :], None,
                            bounds_check=limit, oob_is_err=False).then_inc(edge_done[q], 16)

                run_groups(pool, groups, 0, body)
                for q in range(SLOTS):
                    pool.wait_ge(edge_done[q], -(-(groups - q) // SLOTS) * 16 * G)


def fill_padding(eng, c, key, first, end, name, filled):
    rows, fill = ((c.rows_s, c.fill_s), (c.rows_d, c.fill_d))[key]
    runs = rows.rearrange("(x r) n -> x (r n)", r=UNIT[key])
    regs = [eng.alloc_register(f"{name}{j}") for j in range(SET)]
    with eng.Fori(0, (end - first) // SET) as i:
        eng.load(regs, c.last_run[0:1, key, bass.ds(i * SET + first, SET)])
        for reg in regs:
            run = eng.snap(reg, min_val=0, max_val=runs.shape[0] - P * G // UNIT[key])
            eng.dma_start(runs[bass.ds(run, P, G // UNIT[key]), :],
                          fill[:, 0:UNIT[key], :].rearrange("p r n -> p (r n)")).then_inc(filled, 16)


class At:

    def __init__(self, i, u, groups=None):
        self.i, self.u, self.groups = i, u, groups
        self.last = groups is not None and u == groups - 1

    def has(self, ahead):
        return self.groups is None or 0 <= self.u + ahead < self.groups

    def g(self, k=0):
        return self.i * UB + (self.u + k)

    def slot(self, slots, ahead=0):
        return (self.u + ahead) % slots

    def tiles(self, ahead=0):
        return bass.ds(self.i * (UB * G) + (self.u + ahead) * G, G)

    def tile(self, j, ahead=0):
        return bass.ds(self.i * (UB * G) + (self.u + ahead) * G + j, 1)

    def uses(self, slots, ahead=0, k=0):
        return self.i * (UB // slots) + ((self.u + ahead) // slots + 1 + k)


def run_groups(eng, groups, lead, body, peel=0):
    for u in range(-lead, FIRST):
        body(At(0, u, groups))
    loops = (groups - max(lead, peel) - FIRST) // UB
    with eng.Fori(0, loops) as i:
        for u in range(FIRST, FIRST + UB):
            body(At(i, u))
    for u in range(FIRST + loops * UB, groups):
        body(At(0, u, groups))


def wait(eng, sem, value):
    if not isinstance(value, int) or value > 0:
        eng.wait_ge(sem, value)


def load_x(c, eng, dest, sem):
    whole = c.LAST * P
    step = 12
    x_v = c.x[0:whole, :].rearrange("(b p) n -> p b n", p=P)
    for b in range(0, c.LAST, step):
        eng.dma_start(dest[:, b:b + step, :], x_v[:, b:b + step, :]).then_inc(sem, 16)
    eng.dma_start(dest[0:c.pl.tail, c.LAST, :], c.x[whole:, :]).then_inc(sem, 16)
    return 16 * (-(-c.LAST // step) + 1)


def normalise(nc, c, tag, x):
    nb, d = c.nb, c.d
    with Scope(nc, f"norm{tag}") as s:
        s_step, s_var, s_std = s.sems("s_step s_var s_std")

        def wide(ap):
            return ap.unsqueeze(2).to_broadcast([P, nb, d])

        with nc.Block() as block:
            @block.vector
            def _(dve):
                v = nc.vector
                n = 0

                def link(ins):
                    nonlocal n
                    n += 1
                    ins.then_inc(s_step, 1)
                    dve.wait_ge(s_step, n)

                mean, var, rstd = c.stat[:, 0, :], c.stat[:, 1, :], c.stat[:, 2, :]
                link(v.tensor_reduce(mean, x, AX.X, ALU.add))
                link(v.tensor_scalar(mean, mean, 1.0 / d, None, ALU.mult))
                link(v.tensor_tensor(c.hn[:, :, :], x, wide(mean), ALU.subtract))
                link(v.tensor_tensor(c.accd, c.hn[:, :, :], c.hn[:, :, :], ALU.mult))
                v.tensor_reduce(var, c.accd, AX.X, ALU.add).then_inc(s_var, 1)
                dve.wait_ge(s_std, 1)
                link(v.reciprocal(rstd, var))
                v.scalar_tensor_tensor(c.hn[:, :, :], c.hn[:, :, :], 0.0, wide(rstd), ALU.max,
                                       ALU.mult).then_inc(s_step, 1)
                dve.wait_ge(s_step, n + 1)

            @block.scalar
            def _(act):
                var = c.stat[:, 1, :]
                act.wait_ge(s_var, 1)
                nc.scalar.activation(var, var, ACT.Sqrt, bias=c.eps_t[:, 0:1], scale=1.0 / d).then_inc(s_std, 1)


def project(nc, c, tag, products, take_act, take_dve, end_dve=None, store=None):
    nb, d = c.nb, c.d
    assert nb % SET == 0
    last = nb // SET - 1
    HALVES = ((0, 4), (4, SET))
    with Scope(nc, f"project{tag}") as s:
        copy = s.sb("copy", [P, SET, d])
        turned_sb = s.sb("turned_sb", [P, SET * P])
        ps_t = s.bank("ps_t")
        ps_n = [s.bank(f"ps_n{p}") for p in range(SET)]
        s.rest = s.sb("rest", [P, SET, 256])
        s.keep = s.sb("keep", [P, SET, d])
        (copied, turned, turned_copied, projected, s.kept, s.taken, s.biased, s.step, out0, out1) = s.sems(
            "copied turned turned_copied projected kept taken biased step out0 out1")
        s.out = (out0, out1)

        with nc.Block() as block:
            def run(eng, before, body):
                if before is not None:
                    before(0, 0)
                with eng.Fori(0, last) as i:
                    body(i, False)
                body(last, True)

            @block.scalar
            def _(act):
                act.sem_inc(out0, 16)
                act.sem_inc(out1, 16)

                def copy_step(i, k):
                    if not (isinstance(i, int) and i + k == 0):
                        act.wait_ge(turned, (i + k) * 2)
                    nc.scalar.activation(copy[:, :, :], c.hn[:, bass.ds(i * SET + k * SET, SET), :], ACT.Copy).then_inc(copied, 1)

                def evacuate(i, k):
                    if not (isinstance(i, int) and i + k == 0):
                        act.wait_ge(projected, (i + k) * SET)
                    for h, (a, b) in enumerate(HALVES):
                        act.wait_ge(turned, (i + k) * 2 + (h + 1))
                        nc.scalar.activation(turned_sb[:, a * P:b * P], ps_t[:, 0:(b - a) * P], ACT.Copy).then_inc(turned_copied, 1)

                def before(i, k):
                    copy_step(i, k)
                    evacuate(i, k)

                def body(i, is_last):
                    for p in range(SET):
                        if take_act is not None:
                            act.wait_ge(projected, i * SET + (p + 1))
                            take_act(s, act, i, p, ps_n[p])
                        if p == 1 and not is_last:
                            copy_step(i, 1)
                    if not is_last:
                        evacuate(i, 1)

                run(act, before, body)

            @block.tensor
            def _(pe):
                pe.sem_inc(s.taken, SET)
                pe.sem_inc(s.kept, SET)

                def turn_step(i, k):
                    pe.wait_ge(copied, i + (k + 1))
                    for h, (a, b) in enumerate(HALVES):
                        if not (isinstance(i, int) and i + k == 0 and h == 0):
                            pe.wait_ge(turned_copied, (i + k) * 2 + h)
                        for p in range(a, b):
                            ins = nc.tensor.transpose(ps_t[:, (p - a) * P:(p - a + 1) * P], copy[:, p, :], c.ident[:, :])
                        ins.then_inc(turned, 1)

                def body(i, is_last):
                    for p in range(SET):
                        pe.wait_ge(turned_copied, i * 2 + (1 if p < HALVES[0][1] else 2))
                        pe.wait_ge(s.taken, i * SET + (p + 1))
                        if take_act is not None:
                            pe.wait_ge(s.kept, i * SET + (p + 1))

                        def matmul(a, b, weights, p=p):
                            return nc.tensor.matmul(ps_n[p][:, a:b], turned_sb[:, p * P:(p + 1) * P], weights, start=True, stop=True)

                        products(matmul).then_inc(projected, 1)
                    if not is_last:
                        turn_step(i, 1)

                run(pe, turn_step, body)

            @block.vector
            def _(dve):
                def body(i, is_last):
                    for p in range(SET):
                        if take_act is not None:
                            dve.wait_ge(s.kept, i * SET + (p + 1 + SET))
                        else:
                            dve.wait_ge(projected, i * SET + (p + 1))
                        take_dve(s, dve, i, p, ps_n[p])
                    if end_dve is not None:
                        end_dve(s, dve, i)

                run(dve, None, body)

            @block.sync
            def _(sp):
                if store is not None:
                    def body(i, is_last):
                        for h, (a, b) in enumerate(HALVES):
                            sp.wait_ge(s.biased, i * SET + b)
                            store(s, sp, i, a, b).then_inc(s.out[h], 16)

                    run(sp, None, body)
                    for sem in s.out:
                        sp.wait_ge(sem, 16 * (last + 2))


def store_free(s, act, i, p):
    if p in (0, 4):
        act.wait_ge(s.out[p // 4], i * 16 + 16)


def split_step(s, dve, i, table, width):
    v = s.nc.vector
    blocks = bass.ds(i * SET, SET)
    rest = s.rest[:, :, 0:width]
    dve.wait_ge(s.taken, i * SET + 2 * SET)
    v.tensor_copy(table[:, blocks, 1, :], rest).then_inc(s.step, 1)
    dve.wait_ge(s.step, i * 2 + 1)
    v.tensor_tensor(table[:, blocks, 2, :], rest, table[:, blocks, 1, :], ALU.subtract).then_inc(s.step, 1)
    dve.wait_ge(s.step, i * 2 + 2)


def layer0_nodes(nc, c):
    nb, d = c.nb, c.d
    normalise(nc, c, "0", c.accd)
    with Scope(nc, "fold") as s:
        ps_w = s.bank("ps_w")
        s_w, s_turn, s_m = s.sems("s_w s_turn s_m")
        with nc.Block() as block:
            @block.tensor
            def _(pe):
                nc.tensor.transpose(ps_w[:, 0:P], c.wq[:, :], c.ident[:, :])
                nc.tensor.transpose(ps_w[:, P:2 * P], c.wk[:, :], c.ident[:, :]).then_inc(s_turn, 1)
                pe.wait_ge(s_w, 4)
                nc.tensor.matmul(ps_w[:, 2 * P:3 * P], c.wqkT[:, 0, :], c.wqkT[:, 1, :], start=True,
                                 stop=True).then_inc(s_m, 1)

            @block.vector
            def _(dve):
                v = nc.vector
                v.tensor_scalar(c.bias_f[:, :], c.bias_f[:, :], 1.0, None, ALU.add)
                v.tensor_tensor(c.wnode[:, 0:d], c.wf[:, 0, :], c.wf[:, 2, :], ALU.add).then_inc(s_w, 1)
                v.tensor_tensor(c.wnode[:, 2 * d:3 * d], c.wf[:, 1, :], c.wf[:, 2, :], ALU.subtract).then_inc(s_w, 1)
                dve.wait_ge(s_turn, 1)
                v.tensor_scalar(c.wqkT[:, 0, :], ps_w[:, 0:P], c.wa[:, 0:1], float(d) ** -0.5, ALU.mult,
                                ALU.mult).then_inc(s_w, 1)
                v.tensor_copy(c.wqkT[:, 1, :], ps_w[:, P:2 * P]).then_inc(s_w, 1)
                dve.wait_ge(s_m, 1)
                v.tensor_copy(c.wnode[:, d:2 * d], ps_w[:, 2 * P:3 * P]).then_inc(s_w, 1)
                dve.wait_ge(s_w, 5)

    table = c.lut[:, :].rearrange("p (b k n) -> p b k n", k=3, n=c.AGW)

    def products(matmul):
        return matmul(0, 3 * d, c.wnode[:, :])

    def take_act(s, act, i, p, ps):
        store_free(s, act, i, p)
        nc.scalar.activation(s.keep[:, p, :], ps[:, 2 * d:3 * d], ACT.Copy)
        nc.scalar.activation(table[:, bass.ds(i * SET + p, 1), 0, :], ps[:, 0:2 * d].unsqueeze(1), ACT.Copy).then_inc(s.kept, 1)

    def take_dve(s, dve, i, p, ps):
        nc.vector.tensor_tensor(s.rest[:, p:p + 1, :], ps[:, 0:2 * d].unsqueeze(1), table[:, bass.ds(i * SET + p, 1), 0, :],
                                ALU.subtract).then_inc(s.taken, 1)
        nc.vector.tensor_tensor(s.keep[:, p, :], s.keep[:, p, :], c.bias_f[:, :], ALU.add).then_inc(s.biased, 1)

    def end_dve(s, dve, i):
        split_step(s, dve, i, table, 2 * d)

    def store(s, sp, i, a, b):
        return sp.dma_start(c.tab_b.rearrange("(b p) n -> p b n", p=P)[:, bass.ds(i * SET + a, b - a), :], s.keep[:, a:b, :])

    project(nc, c, "0", products, take_act, take_dve, end_dve, store)


def load_blocks(eng, c, key, at, ahead, regs):
    n = len(regs)
    eng.load(regs, c.blk[0:1, key, bass.ds(at.g(ahead) * n, n)])
    return [eng.snap(r, min_val=0, max_val=c.nb - 1) for r in regs]


def source_hots(c, out, at, ahead):
    for j in range(G):
        last = c.nc.vector.tensor_scalar(out[:, j, :], c.iota1_b[:, :], c.meta[:, at.tile(j, ahead), 0],
                                         None, ALU.is_equal)
    return last


def turn(c, ps, hot):
    for j in range(G):
        last = c.nc.tensor.transpose(ps[:, j * P:(j + 1) * P], hot[:, j, :], c.ident_b[:, :])
    return last


def group_rows(rows, at):
    view = rows.rearrange("(g p r) n -> g p (r n)", p=P, r=G)
    return view[bass.ds(at.g(), 1), :, :].rearrange("a p n -> (a p) n")


def layer0_edges(nc, c):
    pl, nb, d, ef, attr = c.pl, c.nb, c.d, c.ef, c.attr
    ZW, AGW = c.ZW, c.AGW
    groups = pl.groups[0]
    PER = G // UNIT[0]
    with Scope(nc, "layer0") as s:
        row = s.sb("row", [P, 4, G, attr])
        row_i = row[:, :, :, :].bitcast(i32)
        source = s.sb("source", [P, 4, G])
        hot = s.sb("hot", [P, 4, G, P])
        hot_t = s.sb("hot_t", [P, 2, G * P], bf16)
        attr_t = s.sb("attr_t", [ef, 2, G * P])
        bt = s.sb("bt", [P, 4, G, d])
        pre = s.sb("pre", [P, 2, G, d])
        feat = s.sb("feat", [P, 2, G, d])
        z = s.sb("z", [P, 2, G, ZW])
        dot = s.sb("dot", [P, 2, G])
        e_att = s.sb("e_att", [P, 2, G])
        e_minus = s.sb("e_minus", [P, 2, G])
        ps_a = [s.bank(f"ps_a{u}")[:, :].rearrange("p (g n) -> p g n", g=G) for u in range(2)]
        ps_g = [s.bank(f"ps_g{u}")[:, :].rearrange("p (g n) -> p g n", g=G) for u in range(2)]
        ps_hot = s.bank("ps_hot")
        ps_attr = s.bank("ps_attr")
        ps_sum = [s.bank(f"ps_sum{u}") for u in range(2)]
        row_in = [s.sem(f"row_in{q}") for q in range(4)]
        b_in = [s.sem(f"b_in{q}") for q in range(4)]
        (zeroed, fields_ready, source_ready, hot_ready, turned, attr_turned, hot_t_ready, attr_t_ready, a_ready, g_ready,
         pre_ready, ex_ready, feat_ready, prod_ready, dot_ready, att_ready, e_ready, e_minus_ready, z_ready,
         sums_ready, added, gather_step) = s.sems(
            "zeroed fields_ready source_ready hot_ready turned attr_turned hot_t_ready attr_t_ready a_ready g_ready "
            "pre_ready ex_ready feat_ready prod_ready dot_ready att_ready e_ready e_minus_ready z_ready "
            "sums_ready added gather_step")

        with nc.Block() as block:
            @block.sync
            def _(sp):
                def body(at):
                    q = at.slot(4)
                    wait(sp, attr_turned, at.g(1 - 4))
                    wait(sp, fields_ready, at.g(1 - 4))
                    wait(sp, pre_ready, at.g(1 - 4))
                    sp.dma_start(row[:, q, :, :].rearrange("p g n -> p (g n)"), group_rows(c.rows_s[0:pl.rows[0], :], at)).then_inc(row_in[q], 16)

                run_groups(sp, groups, 0, body)

            @block.gpsimd
            def _(pool):
                limit = pool.to_reg(pl.n - 1)

                def body(at):
                    q = at.slot(4)
                    pool.wait_ge(row_in[q], at.uses(4) * 16)
                    wait(pool, pre_ready, at.g(1 - 4))
                    pool.sem_inc(gather_step, 1)
                    for j in range(G):
                        nc.gpsimd.indirect_dma_start(
                            bt[:, q, j, :], None, c.tab_b[0:pl.n, :],
                            bass.IndirectOffsetOnAxis(row_i[:, q, j, DST:DST + 1], 0),
                            bounds_check=limit, oob_is_err=False).then_inc(b_in[q], 16)

                run_groups(pool, groups, 0, body)

            @block.scalar
            def _(act):
                a = nc.scalar

                def exponential(at, ahead):
                    t = at.slot(2, ahead)
                    act.wait_ge(pre_ready, at.g(ahead + 1))
                    wait(act, prod_ready, at.g(ahead + 1 - 2))
                    wait(act, z_ready, at.g(ahead + 1 - 2))
                    a.activation(feat[:, t, :, :], pre[:, t, :, :], ACT.Exp, bias=c.minus_1[:, 0:1]).then_inc(ex_ready, 1)

                def evacuate_hot(at, ahead):
                    act.wait_ge(turned, at.g(ahead + 1))
                    wait(act, g_ready, at.g(ahead + 1 - 2))
                    a.activation(hot_t[:, at.slot(2, ahead), :], ps_hot[:, :], ACT.Copy).then_inc(hot_t_ready, 1)

                def evacuate_attr(at, ahead):
                    act.wait_ge(attr_turned, at.g(ahead + 1))
                    wait(act, a_ready, at.g(ahead + 1 - 2))
                    a.activation(attr_t[:, at.slot(2, ahead), :], ps_attr[0:ef, :], ACT.Copy).then_inc(attr_t_ready, 1)

                def attention(at, ahead):
                    t, n = at.slot(2, ahead), at.g(ahead + 1)
                    act.wait_ge(dot_ready, n)
                    wait(act, sums_ready, at.g(ahead + 1 - 2))
                    a.activation(z[:, t, :, d], dot[:, t, :], ACT.Tanh).then_inc(att_ready, 1)
                    act.wait_ge(att_ready, n)
                    a.activation(e_att[:, t, :], z[:, t, :, d], ACT.Exp).then_inc(e_ready, 1)
                    act.wait_ge(e_ready, n)
                    a.activation(e_minus[:, t, :], e_att[:, t, :], ACT.Copy, scale=-1.0).then_inc(e_minus_ready, 1)
                    act.wait_ge(e_minus_ready, n)
                    for j in range(G):
                        last = a.activation(z[:, t, j, 0:d], feat[:, t, j, :], ACT.Identity,
                                            bias=e_minus[:, t, j:j + 1], scale=e_att[:, t, j:j + 1])
                    last.then_inc(z_ready, 1)

                def body(at):
                    if at.has(1):
                        attention(at, 1)
                    if at.has(4):
                        evacuate_hot(at, 4)
                    if at.has(3):
                        exponential(at, 3)
                    if at.has(5):
                        evacuate_attr(at, 5)

                run_groups(act, groups, 5, body)

            @block.vector
            def _(dve):
                v = nc.vector
                regs = [dve.alloc_register(f"dve_blk{j}") for j in range(PER)]

                def add_sums(at, blocks, j):
                    dve.wait_ge(sums_ready, at.g(1))
                    dve.wait_ge(added, at.g() * PER + (j + 1))
                    dest = c.acc[:, bass.ds(blocks[j] * ZW, ZW)]
                    v.tensor_tensor(dest, dest, ps_sum[at.slot(2)][:, j * ZW:(j + 1) * ZW], ALU.add).then_inc(added, 1)

                def arguments(at, ahead):
                    t, q = at.slot(2, ahead), at.slot(4, ahead)
                    dve.wait_ge(b_in[q], at.uses(4, ahead) * (16 * G))
                    dve.wait_ge(a_ready, at.g(ahead + 1))
                    wait(dve, dot_ready, at.g(ahead + 1 - 2))
                    v.tensor_tensor(pre[:, t, :, :], ps_a[t], bt[:, q, :, :], ALU.add).then_inc(pre_ready, 1)

                def features(at, ahead, between):
                    t = at.slot(2, ahead)
                    dve.wait_ge(ex_ready, at.g(ahead + 1))
                    v.scalar_tensor_tensor(feat[:, t, :, :], feat[:, t, :, :], 1.0, pre[:, t, :, :], ALU.min,
                                           ALU.max).then_inc(feat_ready, 1)
                    between(0)
                    dve.wait_ge(feat_ready, at.g(ahead + 1))
                    dve.wait_ge(g_ready, at.g(ahead + 1))
                    v.scalar_tensor_tensor(pre[:, t, :, :], feat[:, t, :, :], 1.0, ps_g[t],
                                           ALU.subtract, ALU.mult).then_inc(prod_ready, 1)
                    between(1)
                    dve.wait_ge(prod_ready, at.g(ahead + 1))
                    wait(dve, att_ready, at.g(ahead + 1 - 2))
                    v.tensor_reduce(dot[:, t, :], pre[:, t, :, :], AX.X, ALU.add).then_inc(dot_ready, 1)

                def sources(at, ahead):
                    q = at.slot(4, ahead)
                    dve.wait_ge(row_in[q], at.uses(4, ahead) * 16)
                    v.scalar_tensor_tensor(source[:, q, :], row[:, q, :, 0], 8.0, row[:, q, :, SRC_1], ALU.is_lt,
                                           ALU.mult).then_inc(source_ready, 1)
                    v.tensor_copy(c.meta[:, at.tiles(ahead), :], row[:, q, :, SRC_1:DST_HI + 1])
                    v.tensor_copy(c.where[:, :, at.tiles(ahead)], row_i[:, q, :, DST:DROW + 1].rearrange("p g f -> p f g")
                                  ).then_inc(fields_ready, 1)

                def hots(at, ahead):
                    q = at.slot(4, ahead)
                    wait(dve, sums_ready, at.g(ahead + 1 - 4))
                    dve.wait_ge(source_ready, at.g(ahead + 1))
                    for j in range(G):
                        last = v.tensor_scalar(hot[:, q, j, :], c.iota1[:, :], source[:, q, j:j + 1], None, ALU.is_equal)
                    last.then_inc(hot_ready, 1)

                def body(at):
                    if at.has(0):
                        blocks = load_blocks(dve, c, 0, at, 0, regs)

                    def between(step):
                        if step == 0 and at.has(5):
                            sources(at, 5)
                        if step == 1 and at.has(0):
                            add_sums(at, blocks, 0)

                    if at.has(3):
                        arguments(at, 3)
                    if at.has(2):
                        features(at, 2, between)
                    else:
                        between(0)
                        between(1)
                    if at.has(0):
                        for j in range(1, PER):
                            add_sums(at, blocks, j)
                    if at.has(5):
                        hots(at, 5)

                v.memset(c.acc[:, :], 0.0).then_inc(added, 1)
                run_groups(dve, groups, 5, body)
                dve.wait_ge(added, groups * PER + 1)

            @block.tensor
            def _(pe):
                t_ = nc.tensor
                regs = [pe.alloc_register(f"pe_blk{j}") for j in range(PER)]

                def turn_attr(at, ahead):
                    q = at.slot(4, ahead)
                    pe.wait_ge(row_in[q], at.uses(4, ahead) * 16)
                    wait(pe, attr_t_ready, at.g(ahead))
                    for j in range(G):
                        last = t_.transpose(ps_attr[0:ef, j * P:(j + 1) * P], row[:, q, j, 0:ef], c.ident[:, :])
                    last.then_inc(attr_turned, 1)

                def turn_hot(at, ahead):
                    q = at.slot(4, ahead)
                    pe.wait_ge(hot_ready, at.g(ahead + 1))
                    wait(pe, hot_t_ready, at.g(ahead))
                    for j in range(G):
                        last = t_.transpose(ps_hot[:, j * P:(j + 1) * P], hot[:, q, j, :], c.ident[:, :])
                    last.then_inc(turned, 1)

                def look_up(at, ahead):
                    t = at.slot(2, ahead)
                    blocks = load_blocks(pe, c, 0, at, ahead, regs)
                    pe.wait_ge(hot_t_ready, at.g(ahead + 1))
                    pe.wait_ge(attr_t_ready, at.g(ahead + 1))
                    wait(pe, pre_ready, at.g(ahead + 1 - 2))

                    def matmul(out, j, k, start, stop, part):
                        return t_.matmul(out, hot_t[:, t, j * P:(j + 1) * P],
                                         c.lut[:, bass.ds(blocks[j // UNIT[0]] * (3 * AGW) + (k * AGW + part * d), d)],
                                         start=start, stop=stop)

                    for j in range(G):
                        for k in range(3):
                            matmul(ps_a[t][:, j, :], j, k, k == 0, False, 0)
                        last = t_.matmul(ps_a[t][:, j, :], attr_t[:, t, j * P:(j + 1) * P], c.w4[:, :],
                                         start=False, stop=True)
                    last.then_inc(a_ready, 1)
                    wait(pe, prod_ready, at.g(ahead + 1 - 2))
                    for j in range(G):
                        for k in range(3):
                            last = matmul(ps_g[t][:, j, :], j, k, k == 0, k == 2, 1)
                    last.then_inc(g_ready, 1)

                def sum_up(at, ahead):
                    t, q = at.slot(2, ahead), at.slot(4, ahead)
                    pe.wait_ge(z_ready, at.g(ahead + 1))
                    wait(pe, added, at.g(ahead + 1 - 2) * PER + 1 if at.groups is None or at.u + ahead >= 2 else 0)
                    for j in range(G):
                        b, k = j // UNIT[0], j % UNIT[0]
                        last = t_.matmul(ps_sum[t][:, b * ZW:(b + 1) * ZW], hot[:, q, j, :], z[:, t, j, :],
                                         start=(k == 0), stop=(k == UNIT[0] - 1))
                    last.then_inc(sums_ready, 1)

                def body(at):
                    if at.has(5):
                        turn_attr(at, 5)
                    if at.has(1):
                        sum_up(at, 1)
                    if at.has(4):
                        look_up(at, 4)
                    if at.has(5):
                        turn_hot(at, 5)

                run_groups(pe, groups, 5, body)


def layer0_update(nc, c):
    nb, d, hid = c.nb, c.d, c.hid
    x_loads = 16 * (-(-c.LAST // 12) + 1)
    with Scope(nc, "update") as s:
        s_step, s_exp, s_x = s.sems("s_step s_exp s_x")
        with nc.Block() as block:
            @block.scalar
            def _(act):
                nc.scalar.activation(c.stat[:, 3, :], c.acc3[:, :, d], ACT.Exp, scale=-1.0).then_inc(s_exp, 1)

            @block.sync
            def _(sp):
                sp.wait_ge(s_step, 1)
                assert load_x(c, sp, c.xn, s_x) == x_loads

            @block.vector
            def _(dve):
                v = nc.vector
                v.memset(c.xn[:, c.LAST, :], 0.0).then_inc(s_step, 1)
                dve.wait_ge(s_exp, 1)
                v.tensor_tensor(c.acc3[:, :, 0:d], c.acc3[:, :, 0:d],
                                c.stat[:, 3, :].unsqueeze(2).to_broadcast([P, nb, d]), ALU.mult).then_inc(s_step, 1)
                dve.wait_ge(s_step, 2)
                v.tensor_tensor(c.hn[:, :, :], c.hn[:, :, :], c.acc3[:, :, 0:d], ALU.add).then_inc(s_step, 1)
                dve.wait_ge(s_x, x_loads)
                v.tensor_tensor(c.xn[:, :, :], c.xn[:, :, :],
                                c.bias_u[:, :].unsqueeze(1).to_broadcast([P, nb, d]), ALU.add).then_inc(s_step, 1)
                dve.wait_ge(s_step, 4)

    def product(matmul):
        return matmul(0, d, c.wu[:, :])

    def add_x(s, dve, i, p, ps):
        b = bass.ds(i * SET + p, 1)
        nc.vector.tensor_tensor(c.xn[:, b, :], c.xn[:, b, :], ps[:, 0:d].unsqueeze(1), ALU.add).then_inc(s.taken, 1)

    project(nc, c, "u", product, None, add_x)
    normalise(nc, c, "1", c.xn[:, :, :])

    table = c.lut[:, 0:c.X_AT].rearrange("p (b k n) -> p b k n", k=3, n=hid)

    def products(matmul):
        return matmul(0, 2 * hid + d, c.wnode1[:, :])

    def take_act(s, act, i, p, ps):
        store_free(s, act, i, p)
        nc.scalar.activation(s.keep[:, p, 0:hid], ps[:, hid:2 * hid], ACT.Copy)
        nc.scalar.activation(table[:, bass.ds(i * SET + p, 1), 0, :], ps[:, 0:hid].unsqueeze(1), ACT.Copy).then_inc(s.kept, 1)

    def take_dve(s, dve, i, p, ps):
        nc.vector.tensor_tensor(s.rest[:, p:p + 1, 0:hid], ps[:, 0:hid].unsqueeze(1), table[:, bass.ds(i * SET + p, 1), 0, :],
                                ALU.subtract)
        nc.vector.tensor_copy(c.hn[:, bass.ds(i * SET + p, 1), :], ps[:, 2 * hid:2 * hid + d].unsqueeze(1)).then_inc(s.taken, 1)
        nc.vector.tensor_tensor(s.keep[:, p, 0:hid], s.keep[:, p, 0:hid], c.bias_1[:, :], ALU.add).then_inc(s.biased, 1)

    def end_dve(s, dve, i):
        split_step(s, dve, i, table, hid)

    def store(s, sp, i, a, b):
        return sp.dma_start(c.tab_q.rearrange("(b p) n -> p b n", p=P)[:, bass.ds(i * SET + a, b - a), :],
                            s.keep[:, a:b, 0:hid])

    project(nc, c, "1", products, take_act, take_dve, end_dve, store)


def weights_pass(nc, c):
    pl, nb, d, hid = c.pl, c.nb, c.d, c.hid
    groups = pl.groups[0]
    PER = G // UNIT[0]
    with Scope(nc, "weights") as s:
        want = s.sb("want", [P, 4, G], i32)
        hot = s.sb("hot", [P, 2, G, P], bf16)
        hot_t = s.sb("hot_t", [P, 2, G * P], bf16)
        qt = s.sb("qt", [P, 4, G, hid])
        pre = s.sb("pre", [P, 2, G, hid])
        act_h = s.sb("act_h", [P, 2, G, hid])
        c.fill_d = s.sb("fill_d", [P, G, c.ZW])
        half_tanh = s.sb("half_tanh", [P, 2, G])
        weight = s.sb("weight", [P, 2, G])
        b2_half = s.sb("b2_half", [P, 1])
        hot_lo = s.sb("hot_lo", [P, 2, G, P])
        hot_hi = s.sb("hot_hi", [P, 2, G, nb])
        ps_p = [s.bank(f"ps_p{u}")[:, 0:G * hid].rearrange("p (g n) -> p g n", g=G) for u in range(2)]
        ps_hot = s.bank("ps_hot", 1, bf16)
        ps_deg = s.bank("ps_deg")
        q_in = [s.sem(f"q_in{q}") for q in range(4)]
        (filled_d, fill_ready, half_ready, hot_ready, turned, hot_t_ready, want_ready, p_ready, pre_ready, gelu_ready, prod_ready,
         logit_ready, tanh_ready, weight_ready, hi_ready, summed, sigmoid_ready, gather_step) = s.sems(
            "filled_d fill_ready half_ready hot_ready turned hot_t_ready want_ready p_ready pre_ready gelu_ready prod_ready "
            "logit_ready tanh_ready weight_ready hi_ready summed sigmoid_ready gather_step")

        with nc.Block() as block:
            @block.sync
            def _(sp):
                sp.wait_ge(fill_ready, 2)
                fill_padding(sp, c, 1, 0, nb, "sp_last_run_d", filled_d)
                sp.wait_ge(filled_d, nb * 16)

            @block.gpsimd
            def _(pool):
                limit = pool.to_reg(pl.n - 1)

                def body(at):
                    q = at.slot(4)
                    pool.wait_ge(want_ready, at.g(1))
                    wait(pool, pre_ready, at.g(1 - 4))
                    pool.sem_inc(gather_step, 1)
                    for j in range(G):
                        nc.gpsimd.indirect_dma_start(
                            qt[:, q, j, :], None, c.tab_q[0:pl.n, :],
                            bass.IndirectOffsetOnAxis(want[:, q, j:j + 1], 0),
                            bounds_check=limit, oob_is_err=False).then_inc(q_in[q], 16)

                run_groups(pool, groups, 0, body)

            @block.scalar
            def _(act):
                a = nc.scalar

                def body(at):
                    if at.has(0):
                        act.wait_ge(logit_ready, at.g(1))
                        wait(act, weight_ready, at.g(1 - 2))
                        a.activation(half_tanh[:, at.slot(2), :], c.ew[:, at.tiles()], ACT.Tanh, bias=b2_half[:, 0:1],
                                     scale=0.5).then_inc(tanh_ready, 1)
                    if at.has(2):
                        act.wait_ge(pre_ready, at.g(3))
                        wait(act, logit_ready, at.g(3 - 2))
                        a.activation(act_h[:, at.slot(2, 2), :, :], pre[:, at.slot(2, 2), :, :], ACT.Gelu).then_inc(gelu_ready, 1)
                    if at.has(4):
                        act.wait_ge(turned, at.g(5))
                        wait(act, p_ready, at.g(5 - 2))
                        a.activation(hot_t[:, at.slot(2, 4), :], ps_hot[:, 0:G * P], ACT.Copy).then_inc(hot_t_ready, 1)
                    if at.has(5):
                        wait(act, pre_ready, at.g(6 - 4))
                        a.activation(want[:, at.slot(4, 5), :], c.where[:, 0, at.tiles(5)], ACT.Copy).then_inc(want_ready, 1)

                act.wait_ge(half_ready, 1)
                run_groups(act, groups, 5, body)
                act.wait_ge(weight_ready, groups)
                a.activation(c.ew[:, :], c.ew[:, :], ACT.Sigmoid, bias=c.b2_col[:, 0:1]).then_inc(sigmoid_ready, 1)
                act.wait_ge(sigmoid_ready, 1)

            @block.vector
            def _(dve):
                v = nc.vector
                w2 = c.w2_row[:, :].unsqueeze(1).to_broadcast([P, G, hid])
                hi_iota = c.iota[:, 0:nb].unsqueeze(1).to_broadcast([P, G, nb])

                def arguments(at, ahead):
                    t, q = at.slot(2, ahead), at.slot(4, ahead)
                    dve.wait_ge(q_in[q], at.uses(4, ahead) * (16 * G))
                    dve.wait_ge(p_ready, at.g(ahead + 1))
                    wait(dve, gelu_ready, at.g(ahead + 1 - 2))
                    v.tensor_tensor(pre[:, t, :, :], ps_p[t], qt[:, q, :, :], ALU.add).then_inc(pre_ready, 1)

                def logits(at, ahead):
                    t = at.slot(2, ahead)
                    dve.wait_ge(gelu_ready, at.g(ahead + 1))
                    v.tensor_tensor(act_h[:, t, :, :], act_h[:, t, :, :], w2, ALU.mult).then_inc(prod_ready, 1)
                    dve.wait_ge(prod_ready, at.g(ahead + 1))
                    v.tensor_reduce(c.ew[:, at.tiles(ahead)], act_h[:, t, :, :], AX.X, ALU.add).then_inc(logit_ready, 1)

                def hots(at, ahead):
                    wait(dve, turned, at.g(ahead + 1 - 2))
                    source_hots(c, hot[:, at.slot(2, ahead), :, :], at, ahead).then_inc(hot_ready, 1)

                def target_hots(at):
                    t = at.slot(2)
                    wait(dve, summed, at.g(1 - 2))
                    v.tensor_tensor(hot_hi[:, t, :, :], c.meta[:, at.tiles(), 2].unsqueeze(2).to_broadcast([P, G, nb]),
                                    hi_iota, ALU.is_equal).then_inc(hi_ready, 1)
                    dve.wait_ge(tanh_ready, at.g(1))
                    v.tensor_scalar(weight[:, t, :], half_tanh[:, t, :], 0.5, 0.5, ALU.mult, ALU.add).then_inc(weight_ready, 1)
                    for j in range(G):
                        v.tensor_scalar(hot_lo[:, t, j, :], c.iota[:, :], c.meta[:, at.tile(j), 1], None, ALU.is_equal)
                    dve.wait_ge(hi_ready, at.g(0) * 2 + 1)
                    dve.wait_ge(weight_ready, at.g(1))
                    v.tensor_tensor(hot_hi[:, t, :, :], hot_hi[:, t, :, :],
                                    weight[:, t, :].unsqueeze(2).to_broadcast([P, G, nb]), ALU.mult).then_inc(hi_ready, 1)

                def body(at):
                    if at.has(2):
                        arguments(at, 2)
                    if at.has(0):
                        target_hots(at)
                    if at.has(4):
                        hots(at, 4)
                    if at.has(1):
                        logits(at, 1)

                v.memset(c.fill_d[:, :, :], 0.0).then_inc(fill_ready, 1)
                dve.wait_ge(fill_ready, 1)
                v.memset(c.fill_d[:, :, d:d + 1], -1.0).then_inc(fill_ready, 1)
                v.tensor_scalar(b2_half[:, :], c.b2_col[:, :], 0.5, None, ALU.mult).then_inc(half_ready, 1)
                run_groups(dve, groups, 4, body)
                dve.wait_ge(summed, groups + 1)
                v.tensor_scalar(c.stat[:, 0, :], ps_deg[:, 0:nb], 1.0, None, ALU.add).then_inc(half_ready, 1)
                dve.wait_ge(half_ready, 2)

            @block.tensor
            def _(pe):
                t_ = nc.tensor
                regs = [pe.alloc_register(f"pe_w_blk{j}") for j in range(PER)]

                def turn_group(at, ahead):
                    pe.wait_ge(hot_ready, at.g(ahead + 1))
                    wait(pe, hot_t_ready, at.g(ahead))
                    turn(c, ps_hot, hot[:, at.slot(2, ahead), :, :]).then_inc(turned, 1)

                def look_up(at, ahead):
                    t = at.slot(2, ahead)
                    blocks = load_blocks(pe, c, 0, at, ahead, regs)
                    pe.wait_ge(hot_t_ready, at.g(ahead + 1))
                    wait(pe, pre_ready, at.g(ahead + 1 - 2))
                    for j in range(G):
                        for k in range(3):
                            last = t_.matmul(ps_p[t][:, j, :], hot_t[:, t, j * P:(j + 1) * P],
                                             c.lut[:, bass.ds(blocks[j // UNIT[0]] * (3 * hid) + k * hid, hid)],
                                             start=(k == 0), stop=(k == 2))
                    last.then_inc(p_ready, 1)

                def add_degrees(at):
                    t = at.slot(2)
                    pe.wait_ge(hi_ready, at.g(1) * 2)
                    for j in range(G):
                        last = t_.matmul(ps_deg[:, 0:nb], hot_lo[:, t, j, :], hot_hi[:, t, j, :], start=False, stop=False)
                    last.then_inc(summed, 1)

                def body(at):
                    if at.has(3):
                        look_up(at, 3)
                    if at.has(4):
                        turn_group(at, 4)
                    if at.has(0):
                        add_degrees(at)

                t_.matmul(ps_deg[:, 0:nb], c.zeros[:, :], c.zeros[:, 0:nb], start=True, stop=False)
                run_groups(pe, groups, 4, body)
                t_.matmul(ps_deg[:, 0:nb], c.zeros[:, :], c.zeros[:, 0:nb], start=False, stop=True).then_inc(summed, 1)


def scale_nodes(nc, c):
    nb, d = c.nb, c.d
    with Scope(nc, "scale") as s:
        s_step, s_root = s.sems("s_step s_root")
        with nc.Block() as block:
            @block.vector
            def _(dve):
                v = nc.vector
                n = 0

                def link(ins):
                    nonlocal n
                    n += 1
                    ins.then_inc(s_step, 1)
                    dve.wait_ge(s_step, n)

                dve.wait_ge(s_root, 1)
                link(v.reciprocal(c.dinv[:, :], c.stat[:, 1, :]))
                link(v.tensor_tensor(c.hn[:, :, :], c.hn[:, :, :], c.dinv[:, :].unsqueeze(2).to_broadcast([P, nb, d]), ALU.mult))
                x_lut = c.lut[:, c.X_AT:c.X_AT + nb * 3 * d].rearrange("p (b k n) -> p b k n", k=3, n=d)
                link(v.tensor_copy(x_lut[:, :, 0, :], c.hn[:, :, :]))
                link(v.tensor_tensor(c.accd, c.hn[:, :, :], x_lut[:, :, 0, :], ALU.subtract))
                link(v.tensor_copy(x_lut[:, :, 1, :], c.accd))
                link(v.tensor_tensor(x_lut[:, :, 2, :], c.accd, x_lut[:, :, 1, :], ALU.subtract))

            @block.scalar
            def _(act):
                nc.scalar.activation(c.stat[:, 1, :], c.stat[:, 0, :], ACT.Sqrt).then_inc(s_root, 1)
                act.wait_ge(s_root, 1)


def message_pass(nc, c):
    pl, nb, d = c.pl, c.nb, c.d
    ZW = c.ZW
    groups = pl.groups[0]
    PER = G // UNIT[0]
    with Scope(nc, "message") as s:
        want = s.sb("want", [P, 4, G], i32)
        hot = s.sb("hot", [P, 2, G, P], bf16)
        hot_t = s.sb("hot_t", [P, 2, G * P], bf16)
        msg = s.sb("msg", [P, 4, G, ZW])
        ps_x = [s.bank(f"ps_x{u}")[:, :].rearrange("p (g n) -> p g n", g=G) for u in range(2)]
        ps_hot = s.bank("ps_hot", 1, bf16)
        sent = [s.sem(f"sent{q}") for q in range(4)]
        (hot_ready, turned, hot_t_ready, want_ready, x_ready, msg_ready, own_ready, scatter_step) = s.sems(
            "hot_ready turned hot_t_ready want_ready x_ready msg_ready own_ready scatter_step")

        with nc.Block() as block:
            @block.gpsimd
            def _(pool):
                limit = pool.to_reg(pl.rows[1] - 1)

                def body(at):
                    q = at.slot(4)
                    pool.wait_ge(want_ready, at.g(1))
                    pool.wait_ge(msg_ready, at.g(1))
                    pool.sem_inc(scatter_step, 1)
                    for j in range(G):
                        nc.gpsimd.indirect_dma_start(
                            c.rows_d[0:pl.rows[1], :], bass.IndirectOffsetOnAxis(want[:, q, j:j + 1], 0), msg[:, q, j, :], None,
                            bounds_check=limit, oob_is_err=False).then_inc(sent[q], 16)

                run_groups(pool, groups, 0, body)
                for q in range(4):
                    pool.wait_ge(sent[q], -(-(groups - q) // 4) * 16 * G)

            @block.scalar
            def _(act):
                a = nc.scalar

                def body(at):
                    if at.has(2):
                        act.wait_ge(turned, at.g(3))
                        wait(act, x_ready, at.g(3 - 2))
                        a.activation(hot_t[:, at.slot(2, 2), :], ps_hot[:, 0:G * P], ACT.Copy).then_inc(hot_t_ready, 1)
                    if at.has(0):
                        q = at.slot(4)
                        wait(act, sent[q], at.uses(4, 0, -1) * (16 * G))
                        a.activation(msg[:, q, :, d], c.meta[:, at.tiles(), 1], ACT.Copy)
                        a.activation(want[:, q, :], c.where[:, 1, at.tiles()], ACT.Copy).then_inc(want_ready, 1)

                run_groups(act, groups, 2, body)

            @block.vector
            def _(dve):
                v = nc.vector

                def body(at):
                    if at.has(3):
                        wait(dve, turned, at.g(4 - 2))
                        source_hots(c, hot[:, at.slot(2, 3), :, :], at, 3).then_inc(hot_ready, 1)
                    if at.has(0):
                        q = at.slot(4)
                        dve.wait_ge(x_ready, at.g(1))
                        wait(dve, sent[q], at.uses(4, 0, -1) * (16 * G))
                        v.tensor_tensor(msg[:, q, :, 0:d], ps_x[at.slot(2)],
                                        c.ew[:, at.tiles()].unsqueeze(2).to_broadcast([P, G, d]), ALU.mult).then_inc(msg_ready, 1)

                run_groups(dve, groups, 3, body)
                v.tensor_tensor(c.hn[:, :, :], c.hn[:, :, :], c.dinv[:, :].unsqueeze(2).to_broadcast([P, nb, d]),
                                ALU.mult).then_inc(own_ready, 1)
                v.tensor_tensor(c.xn[:, :, :], c.xn[:, :, :],
                                c.bias_c[:, :].unsqueeze(1).to_broadcast([P, nb, d]), ALU.add).then_inc(own_ready, 1)
                dve.wait_ge(own_ready, 2)
                v.tensor_tensor(c.xn[:, :, :], c.xn[:, :, :], c.hn[:, :, :], ALU.add).then_inc(own_ready, 1)
                dve.wait_ge(own_ready, 3)

            @block.tensor
            def _(pe):
                t_ = nc.tensor
                regs = [pe.alloc_register(f"pe_m_blk{j}") for j in range(PER)]

                def body(at):
                    if at.has(1):
                        t = at.slot(2, 1)
                        blocks = load_blocks(pe, c, 0, at, 1, regs)
                        pe.wait_ge(hot_t_ready, at.g(2))
                        wait(pe, msg_ready, at.g(2 - 2))
                        for j in range(G):
                            for k in range(3):
                                last = t_.matmul(ps_x[t][:, j, :], hot_t[:, t, j * P:(j + 1) * P],
                                                 c.lut[:, bass.ds(blocks[j // UNIT[0]] * (3 * d) + (c.X_AT + k * d), d)],
                                                 start=(k == 0), stop=(k == 2))
                        last.then_inc(x_ready, 1)
                    if at.has(2):
                        pe.wait_ge(hot_ready, at.g(3))
                        wait(pe, hot_t_ready, at.g(2))
                        turn(c, ps_hot, hot[:, at.slot(2, 2), :, :]).then_inc(turned, 1)

                run_groups(pe, groups, 2, body)


def target_pass(nc, c):
    pl, nb, d, ZW = c.pl, c.nb, c.d, c.ZW
    groups = pl.groups[1]
    assert UNIT[1] == G
    with Scope(nc, "target") as s:
        msg = s.sb("msg", [P, 4, G, ZW])
        hot = s.sb("hot", [P, 4, G, P])
        ps = [s.bank(f"ps{u}") for u in range(4)]
        msg_in = [s.sem(f"msg_in{q}") for q in range(4)]
        hot_ready, sums_ready, added = s.sems("hot_ready sums_ready added")
        with nc.Block() as block:
            @block.sync
            def _(sp):
                def body(at):
                    q = at.slot(4)
                    wait(sp, sums_ready, at.g(1 - 4))
                    sp.dma_start(msg[:, q, :, :].rearrange("p g n -> p (g n)"), group_rows(c.rows_d[0:pl.rows[1], :], at)).then_inc(msg_in[q], 16)

                run_groups(sp, groups, 0, body)

            @block.gpsimd
            def _(pool):
                nc.gpsimd.memset(c.accd, 0.0).then_inc(added, 1)

            @block.vector
            def _(dve):
                v = nc.vector
                regs = [dve.alloc_register("dve_t_blk")]

                def body(at):
                    if at.has(2):
                        q = at.slot(4, 2)
                        dve.wait_ge(msg_in[q], at.uses(4, 2) * 16)
                        wait(dve, sums_ready, at.g(3 - 4))
                        for j in range(G):
                            last = v.tensor_scalar(hot[:, q, j, :], c.iota[:, :], msg[:, q, j, d:d + 1], None, ALU.is_equal)
                        last.then_inc(hot_ready, 1)
                    if at.has(0):
                        blocks = load_blocks(dve, c, 1, at, 0, regs)
                        dve.wait_ge(sums_ready, at.g(1))
                        dve.wait_ge(added, at.g(1))
                        dest = c.acc[:, bass.ds(blocks[0] * d, d)]
                        v.tensor_tensor(dest, dest, ps[at.slot(4)][:, 0:d], ALU.add).then_inc(added, 1)

                run_groups(dve, groups, 2, body)
                dve.wait_ge(added, groups + 1)

            @block.tensor
            def _(pe):
                t_ = nc.tensor

                def body(at):
                    q = at.slot(4)
                    pe.wait_ge(hot_ready, at.g(1))
                    if at.has(-4):
                        pe.wait_ge(added, at.g(2 - 4))
                    for j in range(G):
                        last = t_.matmul(ps[q][:, 0:d], hot[:, q, j, :], msg[:, q, j, 0:d], start=(j == 0), stop=(j == G - 1))
                    last.then_inc(sums_ready, 1)

                run_groups(pe, groups, 0, body)


def finish(nc, c):
    nb, d, pl = c.nb, c.d, c.pl
    whole = c.LAST * P
    PARTS = 3
    step = c.LAST // PARTS
    with Scope(nc, "finish") as s:
        scaled, ready, s_out = s.sems("scaled ready s_out")
        with nc.Block() as block:
            @block.vector
            def _(dve):
                v = nc.vector

                def blocks(k):
                    return slice(k * step, (k + 1) * step if k < PARTS - 1 else nb)

                for k in range(PARTS):
                    a = blocks(k)
                    v.tensor_tensor(c.accd[:, a, :], c.accd[:, a, :],
                                    c.dinv[:, a].unsqueeze(2).to_broadcast([P, a.stop - a.start, d]), ALU.mult).then_inc(scaled, 1)

                    dve.wait_ge(scaled, k + 1)
                    v.tensor_tensor(c.accd[:, a, :], c.accd[:, a, :], c.xn[:, a, :], ALU.add).then_inc(ready, 1)

            @block.sync
            def _(sp):
                out_v = c.out[0:whole, :].rearrange("(b p) n -> p b n", p=P)
                for k in range(PARTS):
                    sp.wait_ge(ready, k + 1)
                    a = slice(k * step, (k + 1) * step)
                    sp.dma_start(out_v[:, a, :], c.accd[:, a, :]).then_inc(s_out, 16)
                sp.dma_start(c.out[whole:, :], c.accd[0:pl.tail, c.LAST, :]).then_inc(s_out, 16)
                sp.wait_ge(s_out, 16 * (PARTS + 1))


_INS = ["x", "src", "dst", "edge_attr_70", "L0_gnn_Wf", "L0_gnn_bf", "L0_gnn_Wq", "L0_gnn_Wk", "L0_gnn_Wa",
        "L0_gnn_Wu", "L0_gnn_bu", "L1_gnn_mlp_w1", "L1_gnn_mlp_b1", "L1_gnn_mlp_w2", "L1_gnn_mlp_b2",
        "L1_gnn_conv_w", "L1_gnn_conv_b"]


def kernel(**inputs):
    import concourse.bacc as bacc
    from concourse.bass_utils import run_bass_kernel_spmd

    nc = bacc.Bacc("TRN2", target_bir_lowering=False, num_devices=1)
    arrays, args = {}, []
    for name in _INS:
        a = np.ascontiguousarray(inputs[name])
        arrays[name] = a
        args.append(nc.dram_tensor(name, a.shape, mybir.dt.from_np(a.dtype), kind="ExternalInput").ap())
    out = nc.dram_tensor("out", inputs["x"].shape, f32, kind="ExternalOutput").ap()
    gnn(nc, *args, out)
    r = run_bass_kernel_spmd(nc, [arrays], core_ids=[0])
    return r.results[0]["out"]
```
